# Optimizing a Trainium2 kernel written in Bass

```python
import numpy as np
import jax
import jax.numpy as jnp

def _softmax(x, axis=-1):
    return jax.nn.softmax(x, axis=axis)

def _gelu(x):
    return jax.nn.gelu(x, approximate=True)

def _silu(x):
    return jax.nn.silu(x)

def _sigmoid(x):
    return jax.nn.sigmoid(x)

def _layernorm(x, axis=-1, eps=1e-05):
    m = jnp.mean(x, axis=axis, keepdims=True)
    v = jnp.var(x, axis=axis, keepdims=True)
    return (x - m) / jnp.sqrt(v + eps)

def _scatter_add(tgt, idx, src, axis=0):
    return tgt.at[idx].add(src)

def _segment_sum(src, seg, n):
    return jax.ops.segment_sum(src, seg, n)
kernel_name = 'mk_xattn_ffn_d4_seqx_r8_8037a9'

def setup_inputs(seed: int=0):
    np.random.seed(seed)
    _w = jnp.asarray

    def _rec_inputs():
        import jax
        import jax.numpy as jnp
        _rk = jax.random.key(seed)
        x = 7.22e-05 + 1 * jax.random.normal(jax.random.fold_in(_rk, 1), (32, 56, 128), jnp.float32)
        _lenS = 56 - jax.random.randint(jax.random.fold_in(_rk, 7), (32,), 0, max(1, 56 // 4) + 1, jnp.int32)
        _lenS2 = 1500 - jax.random.randint(jax.random.fold_in(_rk, 8), (32,), 0, max(1, 1500 // 4) + 1, jnp.int32)
        _ctx_768P = jax.random.normal(jax.random.fold_in(_rk, 11), (32, 16, 96), jnp.float32)
        _ctx_768c = jax.random.dirichlet(jax.random.fold_in(_rk, 511), 0.3 * jnp.ones((16,), jnp.float32), (32, 1500))
        _ctx_768t = jnp.einsum('bsk,bkd->bsd', _ctx_768c, _ctx_768P)
        _ctx_768t = _ctx_768t * jax.lax.rsqrt(jnp.mean(jnp.square(_ctx_768t)) + 1e-12) * 0.953939
        ctx_768 = -0.000191848 + 0.999787 * (_ctx_768t + 0.3 * jax.random.normal(jax.random.fold_in(_rk, 611), (32, 1500, 96), jnp.float32))
        _validS = jnp.arange(56)[None, :] < _lenS[:, None]
        _validS2 = jnp.arange(1500)[None, :] < _lenS2[:, None]
        _causal = jnp.tril(jnp.ones((56, 56), dtype=bool))
        mask_BxS2_bf1 = jnp.ones((32, 1500), dtype=bool)
        return (x, ctx_768, mask_BxS2_bf1)
    x, ctx_768, mask_BxS2_bf1 = _rec_inputs()

    def _L0_xattn_setup():
        import jax, jax.numpy as jnp
        import numpy as np
        N_HEADS = 16
        key = jax.random.key(seed)
        ks = jax.random.split(key, 8)
        b, l, m = (8, 128, 128)
        d_embed, d_cross = (128, 96)
        s_q = 1.0 / np.sqrt(d_embed)
        s_kv = 1.0 / np.sqrt(d_cross)
        return {'x': jax.random.normal(ks[0], (b, l, d_embed), jnp.float32), 'y': jax.random.normal(ks[1], (b, m, d_cross), jnp.float32), 'Wq': jax.random.normal(ks[2], (d_embed, d_embed), jnp.float32) * s_q, 'bq': jax.random.normal(ks[3], (d_embed,), jnp.float32) * 0.01, 'Wkv': jax.random.normal(ks[4], (2 * d_embed, d_cross), jnp.float32) * s_kv, 'bkv': jax.random.normal(ks[5], (2 * d_embed,), jnp.float32) * 0.01, 'Wo': jax.random.normal(ks[6], (d_embed, d_embed), jnp.float32) * s_q, 'bo': jax.random.normal(ks[7], (d_embed,), jnp.float32) * 0.01}
    _L0_xattn_all = _L0_xattn_setup()
    _L0_xattn_in = {k: v for k, v in _L0_xattn_all.items() if k in ('Wq', 'bq', 'Wkv', 'bkv', 'Wo', 'bo')}
    del _L0_xattn_all

    def _L0_ffn_setup():
        import jax, jax.numpy as jnp
        import numpy as np
        B, S, H = (2, 256, 128)
        E_DYN, E_FIX = (8, 1)
        I_DYN, I_FIX = (64, 256)
        TOP_K = 4
        TOP_P = 0.75
        JITTER_EPS = 0.1
        CAPACITY_FACTOR = 1.25
        MIN_CAPACITY = 4

        def _sparse_mixer(scores):
            T = scores.shape[0]
            rows = jnp.arange(T)
            masked_scores = scores
            mults, sels = ([], [])
            for _ in range(TOP_K):
                thr = jnp.max(masked_scores, axis=-1, keepdims=True)
                sel = jnp.argmax(masked_scores, axis=-1)
                factor = jnp.maximum(jnp.abs(scores), jnp.abs(thr))
                jmask = (thr - scores) / factor > 2.0 * JITTER_EPS
                gates = jax.nn.softmax(jnp.where(jmask, -jnp.inf, masked_scores), axis=-1)
                mult = jnp.take_along_axis(gates, sel[:, None], axis=-1)[:, 0]
                masked_scores = masked_scores.at[rows, sel].set(-jnp.inf)
                mults.append(mult)
                sels.append(sel)
            return (jnp.stack(mults, axis=-1), jnp.stack(sels, axis=-1))
        key = jax.random.key(seed)
        k = jax.random.split(key, 8)
        sc = 0.02
        return {'hidden_states': jax.random.normal(k[0], (B, S, H), jnp.float32), 'gate_w': jax.random.normal(k[1], (E_DYN + E_FIX, H), jnp.float32) * sc, 'dyn_gate_w': jax.random.normal(k[2], (E_DYN, I_DYN, H), jnp.float32) * sc, 'dyn_up_w': jax.random.normal(k[3], (E_DYN, I_DYN, H), jnp.float32) * sc, 'dyn_down_w': jax.random.normal(k[4], (E_DYN, H, I_DYN), jnp.float32) * sc, 'sh_gate_w': jax.random.normal(k[5], (E_FIX, I_FIX, H), jnp.float32) * sc, 'sh_up_w': jax.random.normal(k[6], (E_FIX, I_FIX, H), jnp.float32) * sc, 'sh_down_w': jax.random.normal(k[7], (E_FIX, H, I_FIX), jnp.float32) * sc}
    _L0_ffn_all = _L0_ffn_setup()
    _L0_ffn_in = {k: v for k, v in _L0_ffn_all.items() if k in ('gate_w', 'dyn_gate_w', 'dyn_up_w', 'dyn_down_w', 'sh_gate_w', 'sh_up_w', 'sh_down_w')}
    del _L0_ffn_all

    def _L1_xattn_setup():
        import jax, jax.numpy as jnp
        import numpy as np
        HEADS = 16
        DIM_HEAD = 64
        SCALE = DIM_HEAD ** (-0.5)
        key = jax.random.key(seed)
        ks = jax.random.split(key, 6)
        B, N, C = (4, 512, 128)
        M, Cc = (64, 96)
        inner = HEADS * DIM_HEAD
        s = lambda d: d ** (-0.5)
        return {'x': jax.random.normal(ks[0], (B, N, C), jnp.float32), 'context': jax.random.normal(ks[1], (B, M, Cc), jnp.float32), 'Wq': jax.random.normal(ks[2], (C, inner), jnp.float32) * s(C), 'Wk': jax.random.normal(ks[3], (Cc, inner), jnp.float32) * s(Cc), 'Wv': jax.random.normal(ks[4], (Cc, inner), jnp.float32) * s(Cc), 'Wo': jax.random.normal(ks[5], (inner, C), jnp.float32) * s(inner), 'bo': jnp.zeros((C,), jnp.float32)}
    _L1_xattn_all = _L1_xattn_setup()
    _L1_xattn_in = {k: v for k, v in _L1_xattn_all.items() if k in ('Wq', 'Wk', 'Wv', 'Wo', 'bo')}
    del _L1_xattn_all

    def _L1_ffn_setup():
        import jax, jax.numpy as jnp
        import numpy as np
        L, E, H, F, K = (4, 4, 128, 512, 2)
        B, S = (4, 256)
        EPS = 1e-05

        def _moe_layer(x, rw, rb, g, b, w1, b1, w2, b2):
            logits = jnp.einsum('bsh,he->bse', x, rw) + rb
            probs = jax.nn.softmax(logits, axis=-1)
            vals, idx = jax.lax.top_k(probs, K)
            vals = vals / vals.sum(axis=-1, keepdims=True)
            mu = x.mean(axis=-1, keepdims=True)
            xc = x - mu
            xhat = xc * jax.lax.rsqrt((xc * xc).mean(axis=-1, keepdims=True) + EPS)
            xe = xhat[None] * g[:, None, None, :] + b[:, None, None, :]
            h = jax.nn.gelu(jnp.einsum('ebsh,ehf->ebsf', xe, w1) + b1[:, None, None, :], approximate=False)
            y = jnp.einsum('ebsf,efh->ebsh', h, w2) + b2[:, None, None, :]
            expert_out = x[None] + y
            comb = jnp.einsum('bsk,bske->bse', vals, jax.nn.one_hot(idx, E, dtype=x.dtype))
            return jnp.einsum('bse,ebsh->bsh', comb, expert_out)
        key = jax.random.key(seed)
        ks = jax.random.split(key, 4)
        return {'hidden_states': jax.random.normal(ks[0], (B, S, H), jnp.float32), 'router_w': 0.02 * jax.random.normal(ks[1], (L, H, E), jnp.float32), 'router_b': jnp.zeros((L, E), jnp.float32), 'ln_g': jnp.ones((L, E, H), jnp.float32), 'ln_b': jnp.zeros((L, E, H), jnp.float32), 'w1': 0.02 * jax.random.normal(ks[2], (L, E, H, F), jnp.float32), 'b1': jnp.zeros((L, E, F), jnp.float32), 'w2': 0.02 * jax.random.normal(ks[3], (L, E, F, H), jnp.float32), 'b2': jnp.zeros((L, E, H), jnp.float32)}
    _L1_ffn_all = _L1_ffn_setup()
    _L1_ffn_in = {k: v for k, v in _L1_ffn_all.items() if k in ('router_w', 'router_b', 'ln_g', 'ln_b', 'w1', 'b1', 'w2', 'b2')}
    del _L1_ffn_all

    def _L2_xattn_setup():
        import jax, jax.numpy as jnp
        import numpy as np
        DIM = 128
        CTX_DIM = 96
        HEADS = 16
        key = jax.random.key(seed)
        ks = jax.random.split(key, 7)
        B, N, M = (4, 512, 32)
        x = jax.random.normal(ks[0], (B, N, DIM), dtype=jnp.float32)
        context = jax.random.normal(ks[1], (B, M, CTX_DIM), dtype=jnp.float32)
        context_mask = jnp.ones((B, M), dtype=bool)
        s_d = 1.0 / np.sqrt(DIM)
        s_c = 1.0 / np.sqrt(CTX_DIM)
        Wq = jax.random.normal(ks[2], (DIM, DIM), dtype=jnp.float32) * s_d
        Wk = jax.random.normal(ks[3], (CTX_DIM, DIM), dtype=jnp.float32) * s_c
        Wv = jax.random.normal(ks[4], (CTX_DIM, DIM), dtype=jnp.float32) * s_c
        Wo = jax.random.normal(ks[5], (DIM, DIM), dtype=jnp.float32) * s_d
        return {'x': x, 'context': context, 'context_mask': context_mask, 'Wq': Wq, 'Wk': Wk, 'Wv': Wv, 'Wo': Wo}
    _L2_xattn_all = _L2_xattn_setup()
    _L2_xattn_in = {k: v for k, v in _L2_xattn_all.items() if k in ('Wq', 'Wk', 'Wv', 'Wo')}
    del _L2_xattn_all

    def _L2_ffn_setup():
        import jax, jax.numpy as jnp
        import numpy as np
        B, S, D = (4, 128, 128)
        E, K = (8, 2)
        H = 2 * D
        key = jax.random.key(seed)
        ks = jax.random.split(key, 5)
        x = jax.random.normal(ks[0], (B, S, D), dtype=jnp.float32)
        Wg = jax.random.normal(ks[1], (E, D), dtype=jnp.float32) * 0.02
        W1 = jax.random.normal(ks[2], (E, H, D), dtype=jnp.float32) * 0.02
        W2 = jax.random.normal(ks[3], (E, H, D), dtype=jnp.float32) * 0.02
        W3 = jax.random.normal(ks[4], (E, D, H), dtype=jnp.float32) * 0.02
        return {'x': x, 'Wg': Wg, 'W1': W1, 'W2': W2, 'W3': W3}
    _L2_ffn_all = _L2_ffn_setup()
    _L2_ffn_in = {k: v for k, v in _L2_ffn_all.items() if k in ('Wg', 'W1', 'W2', 'W3')}
    del _L2_ffn_all

    def _L3_xattn_setup():
        import jax, jax.numpy as jnp
        import numpy as np
        B, LQ, LK = (4, 256, 256)
        D1, D2, H = (128, 96, 128)
        key = jax.random.key(seed)
        ks = jax.random.split(key, 9)
        s1, s2, sh = (1.0 / np.sqrt(D1), 1.0 / np.sqrt(D2), 1.0 / np.sqrt(H))
        return {'query': jax.random.normal(ks[0], (B, LQ, D1), jnp.float32), 'key': jax.random.normal(ks[1], (B, LK, D2), jnp.float32), 'value': jax.random.normal(ks[2], (B, LK, D2), jnp.float32), 'Wq': jax.random.normal(ks[3], (D1, H), jnp.float32) * s1, 'bq': jax.random.normal(ks[4], (H,), jnp.float32) * s1, 'Wk': jax.random.normal(ks[5], (D2, H), jnp.float32) * s2, 'bk': jax.random.normal(ks[6], (H,), jnp.float32) * s2, 'Wv': jax.random.normal(ks[7], (D2, H), jnp.float32) * s2, 'bv': jax.random.normal(ks[8], (H,), jnp.float32) * s2}
    _L3_xattn_all = _L3_xattn_setup()
    _L3_xattn_in = {k: v for k, v in _L3_xattn_all.items() if k in ('Wq', 'bq', 'Wk', 'bk', 'Wv', 'bv')}
    del _L3_xattn_all

    def _L3_ffn_setup():
        import jax, jax.numpy as jnp
        import numpy as np
        BLOCK_SIZE = 32
        FP6_E2M3_MAX = 7.5

        def _build_fp6_e2m3_grid():
            vals = set()
            for bits in range(64):
                s = bits >> 5 & 1
                e = bits >> 3 & 3
                m = bits & 7
                v = m / 8.0 if e == 0 else (1.0 + m / 8.0) * 2.0 ** (e - 1)
                vals.add(-v if s else v)
            return np.array(sorted(vals), dtype=np.float32)
        _GRID = jnp.asarray(_build_fp6_e2m3_grid())

        def _nearest_on_grid(x, grid):
            idx = jnp.clip(jnp.searchsorted(grid, x), 0, grid.shape[0] - 1)
            idx_lo = jnp.maximum(idx - 1, 0)
            v_hi = grid[idx]
            v_lo = grid[idx_lo]
            return jnp.where(jnp.abs(x - v_lo) <= jnp.abs(x - v_hi), v_lo, v_hi)

        def _mx_quantize(t, eps=1e-30):
            rows, K = t.shape
            blocks = t.reshape(rows, K // BLOCK_SIZE, BLOCK_SIZE)
            scales = jnp.maximum(jnp.max(jnp.abs(blocks), axis=-1) / FP6_E2M3_MAX, eps)
            q = _nearest_on_grid(blocks / scales[..., None], _GRID)
            return (q, scales)
        key = jax.random.key(seed)
        k1, k2, k3 = jax.random.split(key, 3)
        x = jax.random.normal(k1, (8, 1024, 128), dtype=jnp.float32)
        weight = jax.random.normal(k2, (128, 128), dtype=jnp.float32) * 0.02
        bias = jax.random.normal(k3, (128,), dtype=jnp.float32) * 0.02
        return {'x': x, 'weight': weight, 'bias': bias}
    _L3_ffn_all = _L3_ffn_setup()
    _L3_ffn_in = {k: v for k, v in _L3_ffn_all.items() if k in ('weight', 'bias')}
    del _L3_ffn_all
    return {'x': x, 'ctx_768': ctx_768, 'mask_BxS2_bf1': mask_BxS2_bf1, 'L0_xattn_Wq': _L0_xattn_in['Wq'], 'L0_xattn_bq': _L0_xattn_in['bq'], 'L0_xattn_Wkv': _L0_xattn_in['Wkv'], 'L0_xattn_bkv': _L0_xattn_in['bkv'], 'L0_xattn_Wo': _L0_xattn_in['Wo'], 'L0_xattn_bo': _L0_xattn_in['bo'], 'L0_ffn_gate_w': _L0_ffn_in['gate_w'], 'L0_ffn_dyn_gate_w': _L0_ffn_in['dyn_gate_w'], 'L0_ffn_dyn_up_w': _L0_ffn_in['dyn_up_w'], 'L0_ffn_dyn_down_w': _L0_ffn_in['dyn_down_w'], 'L0_ffn_sh_gate_w': _L0_ffn_in['sh_gate_w'], 'L0_ffn_sh_up_w': _L0_ffn_in['sh_up_w'], 'L0_ffn_sh_down_w': _L0_ffn_in['sh_down_w'], 'L1_xattn_Wq': _L1_xattn_in['Wq'], 'L1_xattn_Wk': _L1_xattn_in['Wk'], 'L1_xattn_Wv': _L1_xattn_in['Wv'], 'L1_xattn_Wo': _L1_xattn_in['Wo'], 'L1_xattn_bo': _L1_xattn_in['bo'], 'L1_ffn_router_w': _L1_ffn_in['router_w'], 'L1_ffn_router_b': _L1_ffn_in['router_b'], 'L1_ffn_ln_g': _L1_ffn_in['ln_g'], 'L1_ffn_ln_b': _L1_ffn_in['ln_b'], 'L1_ffn_w1': _L1_ffn_in['w1'], 'L1_ffn_b1': _L1_ffn_in['b1'], 'L1_ffn_w2': _L1_ffn_in['w2'], 'L1_ffn_b2': _L1_ffn_in['b2'], 'L2_xattn_Wq': _L2_xattn_in['Wq'], 'L2_xattn_Wk': _L2_xattn_in['Wk'], 'L2_xattn_Wv': _L2_xattn_in['Wv'], 'L2_xattn_Wo': _L2_xattn_in['Wo'], 'L2_ffn_Wg': _L2_ffn_in['Wg'], 'L2_ffn_W1': _L2_ffn_in['W1'], 'L2_ffn_W2': _L2_ffn_in['W2'], 'L2_ffn_W3': _L2_ffn_in['W3'], 'L3_xattn_Wq': _L3_xattn_in['Wq'], 'L3_xattn_bq': _L3_xattn_in['bq'], 'L3_xattn_Wk': _L3_xattn_in['Wk'], 'L3_xattn_bk': _L3_xattn_in['bk'], 'L3_xattn_Wv': _L3_xattn_in['Wv'], 'L3_xattn_bv': _L3_xattn_in['bv'], 'L3_ffn_weight': _L3_ffn_in['weight'], 'L3_ffn_bias': _L3_ffn_in['bias']}

def reference(x, ctx_768, mask_BxS2_bf1, L0_xattn_Wq, L0_xattn_bq, L0_xattn_Wkv, L0_xattn_bkv, L0_xattn_Wo, L0_xattn_bo, L0_ffn_gate_w, L0_ffn_dyn_gate_w, L0_ffn_dyn_up_w, L0_ffn_dyn_down_w, L0_ffn_sh_gate_w, L0_ffn_sh_up_w, L0_ffn_sh_down_w, L1_xattn_Wq, L1_xattn_Wk, L1_xattn_Wv, L1_xattn_Wo, L1_xattn_bo, L1_ffn_router_w, L1_ffn_router_b, L1_ffn_ln_g, L1_ffn_ln_b, L1_ffn_w1, L1_ffn_b1, L1_ffn_w2, L1_ffn_b2, L2_xattn_Wq, L2_xattn_Wk, L2_xattn_Wv, L2_xattn_Wo, L2_ffn_Wg, L2_ffn_W1, L2_ffn_W2, L2_ffn_W3, L3_xattn_Wq, L3_xattn_bq, L3_xattn_Wk, L3_xattn_bk, L3_xattn_Wv, L3_xattn_bv, L3_ffn_weight, L3_ffn_bias):
    import jax
    import jax.numpy as jnp

    def _L0_xattn_ref(x, y, Wq, bq, Wkv, bkv, Wo, bo):
        import jax, jax.numpy as jnp
        import numpy as np
        N_HEADS = 16
        b, l, d = x.shape
        m = y.shape[1]
        h = N_HEADS
        dh = d // h
        q = (jnp.einsum('bld,ed->ble', x, Wq) + bq).reshape(b, l, h, dh)
        kv = (jnp.einsum('bmc,ec->bme', y, Wkv) + bkv).reshape(b, m, h, 2 * dh)
        k, v = (kv[..., :dh], kv[..., dh:])
        scale = 1.0 / jnp.sqrt(jnp.asarray(dh, x.dtype))
        att = jax.nn.softmax(jnp.einsum('blhd,bmhd->blmh', q, k) * scale, axis=2)
        out = jnp.einsum('blmh,bmhd->blhd', att, v).reshape(b, l, d)
        return jnp.einsum('bld,ed->ble', out, Wo) + bo

    def _L0_ffn_ref(hidden_states, gate_w, dyn_gate_w, dyn_up_w, dyn_down_w, sh_gate_w, sh_up_w, sh_down_w):
        import jax, jax.numpy as jnp
        import numpy as np
        B, S, H = (2, 256, 128)
        E_DYN, E_FIX = (8, 1)
        I_DYN, I_FIX = (64, 256)
        TOP_K = 4
        TOP_P = 0.75
        JITTER_EPS = 0.1
        CAPACITY_FACTOR = 1.25
        MIN_CAPACITY = 4

        def _sparse_mixer(scores):
            T = scores.shape[0]
            rows = jnp.arange(T)
            masked_scores = scores
            mults, sels = ([], [])
            for _ in range(TOP_K):
                thr = jnp.max(masked_scores, axis=-1, keepdims=True)
                sel = jnp.argmax(masked_scores, axis=-1)
                factor = jnp.maximum(jnp.abs(scores), jnp.abs(thr))
                jmask = (thr - scores) / factor > 2.0 * JITTER_EPS
                gates = jax.nn.softmax(jnp.where(jmask, -jnp.inf, masked_scores), axis=-1)
                mult = jnp.take_along_axis(gates, sel[:, None], axis=-1)[:, 0]
                masked_scores = masked_scores.at[rows, sel].set(-jnp.inf)
                mults.append(mult)
                sels.append(sel)
            return (jnp.stack(mults, axis=-1), jnp.stack(sels, axis=-1))
        Bv, Sv, Hv = hidden_states.shape
        T = Bv * Sv
        x = hidden_states.reshape(T, Hv)
        full_logits = x @ gate_w.T
        dyn_logits = full_logits[:, :E_DYN]
        probs = jax.nn.softmax(dyn_logits, axis=-1)
        sorted_p = jnp.sort(probs, axis=-1)[:, ::-1]
        csum = jnp.cumsum(sorted_p, axis=-1)
        dyn_k = jnp.minimum(jnp.sum(csum < TOP_P, axis=-1) + 1, TOP_K)
        mult, sel = _sparse_mixer(dyn_logits)
        slot_valid = jnp.arange(TOP_K)[None, :] < dyn_k[:, None]
        mult = jnp.where(slot_valid, mult, 0.0)
        rows = jnp.arange(T)
        rw = jnp.zeros((T, E_DYN), x.dtype).at[rows[:, None], sel].add(mult)
        rw = rw / jnp.sum(rw, axis=-1, keepdims=True)
        mask_dyn = (rw > 0).astype(jnp.int32)
        cap = max(int(np.ceil(T / E_DYN * CAPACITY_FACTOR)), MIN_CAPACITY)
        mask_dyn = mask_dyn * (jnp.cumsum(mask_dyn, axis=0) <= cap)
        expert_mask = jnp.concatenate([mask_dyn, jnp.ones((T, E_FIX), jnp.int32)], axis=-1)
        maskf = expert_mask.astype(x.dtype)
        gw = jax.nn.softmax(jnp.where(expert_mask == 0, -jnp.inf, full_logits), axis=-1)
        gd = rw * jnp.sum(gw[:, :E_DYN], axis=-1, keepdims=True)
        global_w = jnp.concatenate([gd, gw[:, E_DYN:]], axis=-1) * maskf
        g = jnp.einsum('th,eih->tei', x, dyn_gate_w)
        u = jnp.einsum('th,eih->tei', x, dyn_up_w)
        y_dyn = jnp.einsum('tei,ehi->teh', jax.nn.silu(g) * u, dyn_down_w)
        out = jnp.einsum('te,teh->th', global_w[:, :E_DYN], y_dyn)
        gs = jnp.einsum('th,fih->tfi', x, sh_gate_w)
        us = jnp.einsum('th,fih->tfi', x, sh_up_w)
        y_sh = jnp.einsum('tfi,fhi->tfh', jax.nn.silu(gs) * us, sh_down_w)
        out = out + jnp.einsum('tf,tfh->th', global_w[:, E_DYN:], y_sh)
        return out.reshape(Bv, Sv, Hv)

    def _L1_xattn_ref(x, context, Wq, Wk, Wv, Wo, bo):
        import jax, jax.numpy as jnp
        import numpy as np
        HEADS = 16
        DIM_HEAD = 64
        SCALE = DIM_HEAD ** (-0.5)
        B, N, _ = x.shape
        M = context.shape[1]
        q = (x @ Wq).reshape(B, N, HEADS, DIM_HEAD).transpose(0, 2, 1, 3)
        k = (context @ Wk).reshape(B, M, HEADS, DIM_HEAD).transpose(0, 2, 1, 3)
        v = (context @ Wv).reshape(B, M, HEADS, DIM_HEAD).transpose(0, 2, 1, 3)
        dots = jnp.einsum('bhnd,bhmd->bhnm', q, k) * SCALE
        attn = jax.nn.softmax(dots, axis=-1)
        out = jnp.einsum('bhnm,bhmd->bhnd', attn, v)
        out = out.transpose(0, 2, 1, 3).reshape(B, N, HEADS * DIM_HEAD)
        return out @ Wo + bo

    def _L1_ffn_ref(hidden_states, router_w, router_b, ln_g, ln_b, w1, b1, w2, b2):
        import jax, jax.numpy as jnp
        import numpy as np
        L, E, H, F, K = (4, 4, 128, 512, 2)
        B, S = (4, 256)
        EPS = 1e-05

        def _moe_layer(x, rw, rb, g, b, w1, b1, w2, b2):
            logits = jnp.einsum('bsh,he->bse', x, rw) + rb
            probs = jax.nn.softmax(logits, axis=-1)
            vals, idx = jax.lax.top_k(probs, K)
            vals = vals / vals.sum(axis=-1, keepdims=True)
            mu = x.mean(axis=-1, keepdims=True)
            xc = x - mu
            xhat = xc * jax.lax.rsqrt((xc * xc).mean(axis=-1, keepdims=True) + EPS)
            xe = xhat[None] * g[:, None, None, :] + b[:, None, None, :]
            h = jax.nn.gelu(jnp.einsum('ebsh,ehf->ebsf', xe, w1) + b1[:, None, None, :], approximate=False)
            y = jnp.einsum('ebsf,efh->ebsh', h, w2) + b2[:, None, None, :]
            expert_out = x[None] + y
            comb = jnp.einsum('bsk,bske->bse', vals, jax.nn.one_hot(idx, E, dtype=x.dtype))
            return jnp.einsum('bse,ebsh->bsh', comb, expert_out)
        x = hidden_states
        for l in range(L):
            x = _moe_layer(x, router_w[l], router_b[l], ln_g[l], ln_b[l], w1[l], b1[l], w2[l], b2[l])
        return x

    def _L2_xattn_ref(x, context, context_mask, Wq, Wk, Wv, Wo):
        import jax, jax.numpy as jnp
        import numpy as np
        DIM = 128
        CTX_DIM = 96
        HEADS = 16
        B, N, _ = x.shape
        M = context.shape[1]
        hd = DIM // HEADS
        scale = hd ** (-0.5)
        q = (x @ Wq).reshape(B, N, HEADS, hd).transpose(0, 2, 1, 3)
        k = (context @ Wk).reshape(B, M, HEADS, hd).transpose(0, 2, 1, 3)
        v = (context @ Wv).reshape(B, M, HEADS, hd).transpose(0, 2, 1, 3)
        scores = jnp.einsum('bhid,bhjd->bhij', q, k) * scale
        max_neg = -jnp.finfo(scores.dtype).max
        scores = jnp.where(context_mask[:, None, None, :], scores, max_neg)
        attn = jax.nn.softmax(scores, axis=-1)
        out = jnp.einsum('bhij,bhjd->bhid', attn, v)
        out = out.transpose(0, 2, 1, 3).reshape(B, N, DIM)
        return out @ Wo

    def _L2_ffn_ref(x, Wg, W1, W2, W3):
        import jax, jax.numpy as jnp
        import numpy as np
        B, S, D = (4, 128, 128)
        E, K = (8, 2)
        H = 2 * D
        gate_out = jnp.einsum('bsd,ed->bse', x, Wg)
        top_v, top_i = jax.lax.top_k(gate_out, K)
        probs = jax.nn.softmax(top_v, axis=-1)
        out = jnp.zeros_like(x)
        for e in range(E):
            w_e = jnp.sum(probs * (top_i == e), axis=-1)
            h1 = jnp.einsum('bsd,hd->bsh', x, W1[e])
            h2 = jnp.einsum('bsd,hd->bsh', x, W2[e])
            g = h1 * jax.nn.sigmoid(h1) * h2
            y = jnp.einsum('bsh,dh->bsd', g, W3[e])
            out = out + y * w_e[..., None]
        return out

    def _L3_xattn_ref(query, key, value, Wq, bq, Wk, bk, Wv, bv):
        import jax, jax.numpy as jnp
        import numpy as np
        B, LQ, LK = (4, 256, 256)
        D1, D2, H = (128, 96, 128)
        q = jnp.einsum('bqd,dh->bqh', query, Wq) + bq
        k = jnp.einsum('bkd,dh->bkh', key, Wk) + bk
        v = jnp.einsum('bkd,dh->bkh', value, Wv) + bv
        scores = jnp.einsum('bqh,bkh->bqk', q, k)
        weights = jax.nn.softmax(scores, axis=-1)
        return jnp.einsum('bqk,bkh->bqh', weights, v)

    def _L3_ffn_ref(x, weight, bias):
        import jax, jax.numpy as jnp
        import numpy as np
        BLOCK_SIZE = 32
        FP6_E2M3_MAX = 7.5

        def _build_fp6_e2m3_grid():
            vals = set()
            for bits in range(64):
                s = bits >> 5 & 1
                e = bits >> 3 & 3
                m = bits & 7
                v = m / 8.0 if e == 0 else (1.0 + m / 8.0) * 2.0 ** (e - 1)
                vals.add(-v if s else v)
            return np.array(sorted(vals), dtype=np.float32)
        _GRID = jnp.asarray(_build_fp6_e2m3_grid())

        def _nearest_on_grid(x, grid):
            idx = jnp.clip(jnp.searchsorted(grid, x), 0, grid.shape[0] - 1)
            idx_lo = jnp.maximum(idx - 1, 0)
            v_hi = grid[idx]
            v_lo = grid[idx_lo]
            return jnp.where(jnp.abs(x - v_lo) <= jnp.abs(x - v_hi), v_lo, v_hi)

        def _mx_quantize(t, eps=1e-30):
            rows, K = t.shape
            blocks = t.reshape(rows, K // BLOCK_SIZE, BLOCK_SIZE)
            scales = jnp.maximum(jnp.max(jnp.abs(blocks), axis=-1) / FP6_E2M3_MAX, eps)
            q = _nearest_on_grid(blocks / scales[..., None], _GRID)
            return (q, scales)
        batch_shape = x.shape[:-1]
        in_features = x.shape[-1]
        x2 = x.astype(jnp.float32).reshape(-1, in_features)
        w2 = weight.astype(jnp.float32)
        xq, xs = _mx_quantize(x2)
        wq, ws = _mx_quantize(w2)
        xd = (xq * xs[..., None]).reshape(x2.shape)
        wd = (wq * ws[..., None]).reshape(w2.shape)
        out = xd @ wd.T + bias
        return out.reshape(*batch_shape, -1)
    x = x + _L0_xattn_ref(_layernorm(x, axis=-1), ctx_768, L0_xattn_Wq, L0_xattn_bq, L0_xattn_Wkv, L0_xattn_bkv, L0_xattn_Wo, L0_xattn_bo)
    x = x + _L0_ffn_ref(_layernorm(x, axis=-1), L0_ffn_gate_w, L0_ffn_dyn_gate_w, L0_ffn_dyn_up_w, L0_ffn_dyn_down_w, L0_ffn_sh_gate_w, L0_ffn_sh_up_w, L0_ffn_sh_down_w)
    x = x + _L1_xattn_ref(_layernorm(x, axis=-1), ctx_768, L1_xattn_Wq, L1_xattn_Wk, L1_xattn_Wv, L1_xattn_Wo, L1_xattn_bo)
    x = x + _L1_ffn_ref(_layernorm(x, axis=-1), L1_ffn_router_w, L1_ffn_router_b, L1_ffn_ln_g, L1_ffn_ln_b, L1_ffn_w1, L1_ffn_b1, L1_ffn_w2, L1_ffn_b2)
    x = x + _L2_xattn_ref(_layernorm(x, axis=-1), ctx_768, mask_BxS2_bf1, L2_xattn_Wq, L2_xattn_Wk, L2_xattn_Wv, L2_xattn_Wo)
    x = x + _L2_ffn_ref(_layernorm(x, axis=-1), L2_ffn_Wg, L2_ffn_W1, L2_ffn_W2, L2_ffn_W3)
    x = x + _L3_xattn_ref(_layernorm(x, axis=-1), ctx_768, ctx_768, L3_xattn_Wq, L3_xattn_bq, L3_xattn_Wk, L3_xattn_bk, L3_xattn_Wv, L3_xattn_bv)
    x = x + _L3_ffn_ref(_layernorm(x, axis=-1), L3_ffn_weight, L3_ffn_bias)
    return x

_drawn_inputs = setup_inputs


def setup_inputs(seed=0):
    import zlib

    import numpy as np

    out = dict(_drawn_inputs(seed))
    spreads = {'L1_xattn_bo': (0.0, 0.1),
     'L1_ffn_router_b': (0.0, 0.1),
     'L1_ffn_ln_g': (1.0, 0.6),
     'L1_ffn_ln_b': (0.0, 0.8),
     'L1_ffn_b1': (0.0, 0.316),
     'L1_ffn_b2': (0.0, 0.1)}
    factors = {'L0_xattn_bq': 8.0,
     'L0_xattn_bkv': 3.554,
     'L0_xattn_bo': 3.892,
     'L0_ffn_gate_w': 8.0,
     'L0_ffn_dyn_gate_w': 8.0,
     'L0_ffn_dyn_up_w': 8.0,
     'L0_ffn_dyn_down_w': 8.0,
     'L0_ffn_sh_gate_w': 6.169,
     'L0_ffn_sh_up_w': 6.736,
     'L0_ffn_sh_down_w': 6.177,
     'L2_ffn_Wg': 8.0,
     'L2_ffn_W1': 8.0,
     'L2_ffn_W2': 8.0,
     'L2_ffn_W3': 8.0,
     'L3_xattn_bk': 64.0,
     'L3_ffn_bias': 7.68,
     'L3_xattn_bv': 3.026}
    for name, (base, spread) in spreads.items():
        noise = np.random.default_rng([zlib.crc32(name.encode()), seed]).standard_normal(out[name].shape)
        drawn = base * np.exp(spread * noise) if base else spread * noise
        out[name] = jnp.asarray(drawn.astype(out[name].dtype))
    for name, factor in factors.items():
        out[name] = (out[name] * factor).astype(out[name].dtype)
    return out
```

```python
from contextlib import ExitStack

import concourse.bass as bass
from concourse import mybir

F32 = mybir.dt.float32
F32R = mybir.dt.float32r
U8 = mybir.dt.uint8
U32 = mybir.dt.uint32
ALU = mybir.AluOpType
ACT = mybir.ActivationFunctionType
AX = mybir.AxisListType

P = 128
D = 128
B, L = 32, 56
S, C = 1500, 96
T = B * L
NT = T // P
KT, NK = 12, 125
BANKS, BK = 3, 500
GT = KT // BANKS
CR = C + 2
CO = C + 1
PAIR = 2 * L
NP = B // 2
TC = 448
NC = T // TC
BIG = 1.5 * 2.0 ** 127
EPS = 1e-5
HEADS = 16
CAP = 280
ONLY = None
ROUND = 12582912.0


class Stage:

    def __init__(self, nc, ctx, name):
        self.nc, self.ctx, self.name, self.sems = nc, ctx, name, []
        ctx.callback(self.release)

    def release(self):
        if self.sems:
            self.nc.clear_and_free_semaphores(self.sems)
            self.nc.all_engine_barrier()

    def sb(self, name, shape, dt=F32):
        return self.ctx.enter_context(self.nc.sbuf_tensor(f"{self.name}_{name}", shape, dt))

    def ps(self, name, shape):
        return self.ctx.enter_context(self.nc.psum_tensor(f"{self.name}_{name}", shape, F32))

    def sem(self, name):
        self.sems.append(self.nc.alloc_semaphore(f"{self.name}_{name}"))
        return self.sems[-1]


def chain(eng, sem):
    count = [0]

    def link(ins):
        count[0] += 1
        ins.then_inc(sem, 1)
        eng.wait_ge(sem, count[0])

    return link


def constants(nc, g):
    with ExitStack() as ctx:
        st = Stage(nc, ctx, "const")
        cleared, dved = st.sem("cleared"), st.sem("dve")
        block = ctx.enter_context(nc.Block())

        @block.vector
        def _(dve):
            link = chain(dve, dved)
            link(dve.memset(g.ones[:], 1.0))
            link(dve.memset(g.zeros[:], 0.0))
            link(dve.memset(g.xnt[:, T:T + 2 * PAIR], 0.0))
            link(dve.memset(g.half[:], -0.5))

        @block.gpsimd
        def _(pool):
            pool.memset(g.ident[:], 0.0).then_inc(cleared, 1)
            pool.memset(g.tri[:], 1.0).then_inc(cleared, 1)
            pool.memset(g.hm8[:], 1.0).then_inc(cleared, 1)
            pool.memset(g.hm64[:], 1.0).then_inc(cleared, 1)
            picks = ((g.pick_f0, 12, 64), (g.pick_f1, ME, 128), (g.pick_f2, 8, 256))
            for tile, _, _ in picks:
                pool.memset(tile[:], 1.0).then_inc(cleared, 1)
            pool.iota(g.iota8[:], [[1, 8]], base=0, channel_multiplier=0,
                      allow_small_or_imprecise_dtypes=True).then_inc(cleared, 1)
            pool.wait_ge(cleared, 8)
            pool.affine_select(out=g.ident[:], in_=g.ident[:], compare_op=ALU.not_equal, fill=1.0, base=0,
                               pattern=[[-1, P]], channel_multiplier=1).then_inc(cleared, 1)
            pool.affine_select(out=g.tri[:], in_=g.tri[:], compare_op=ALU.is_ge, fill=0.0, base=0,
                               pattern=[[1, P]], channel_multiplier=-1).then_inc(cleared, 1)

            def band(tile, cols, width, n):
                pool.affine_select(out=tile, in_=tile, compare_op=ALU.is_ge, fill=0.0, base=0,
                                   pattern=[[-width, cols]], channel_multiplier=1).then_inc(cleared, 1)
                pool.wait_ge(cleared, n + 1)
                pool.affine_select(out=tile, in_=tile, compare_op=ALU.is_ge, fill=0.0, base=width - 1,
                                   pattern=[[width, cols]], channel_multiplier=-1).then_inc(cleared, 1)

            band(g.hm8[:], 16, 8, 10)
            band(g.hm64[:], 2, 64, 12)
            for tile, cols, width in picks:
                v = tile[:].rearrange("e (c w) -> e c w", w=width)
                pool.affine_select(out=v, in_=v, compare_op=ALU.is_equal, fill=0.0, base=0,
                                   pattern=[[-1, cols], [0, width]], channel_multiplier=1).then_inc(cleared, 1)
            pool.wait_ge(cleared, 17)
            pool.tensor_copy(g.pick_f0[:, 9 * 64:12 * 64].rearrange("e (c w) -> e c w", w=64),
                             g.pick_f0[:, 8 * 64:9 * 64].rearrange("e (c w) -> e c w", c=1).broadcast_to([9, 3, 64])
                             ).then_inc(cleared, 1)
            pool.wait_ge(cleared, 18)


def context_prep(nc, g, ctx_d, mask_d, ctx_t):
    with ExitStack() as ctx:
        st = Stage(nc, ctx, "cprep")
        nat = st.sb("nat", [NK, 2, KT, C])
        tr = st.sb("tr", [CO, 2, S])
        mask8, maskf = st.sb("mask8", [B, S], U8), st.sb("maskf", [B, S])
        ps = [st.ps(f"ps{n}", [P, 512]) for n in range(6)]
        loaded = [st.sem(f"loaded{n}") for n in range(2)]
        stored = [st.sem(f"stored{n}") for n in range(2)]
        mask_in, mask_done, mask_out = st.sem("mask_in"), st.sem("mask_done"), st.sem("mask_out")
        turned, kept, ones = st.sem("turned"), st.sem("kept"), st.sem("ones")
        block = ctx.enter_context(nc.Block())
        ctx_v = ctx_d.rearrange("b (p t) c -> p b (t c)", t=KT)

        @block.sync
        def _(sp):
            sp.dma_start(mask8[:], mask_d).then_inc(mask_in, 16)
            for h in range(2):
                sp.dma_start(nat[:, h, :, :].rearrange("p t c -> p (t c)"), ctx_v[:, h, :]).then_inc(loaded[h], 16)
            sp.wait_ge(mask_done, 2)
            sp.dma_start(ctx_t[:, C + 1, :], maskf[:]).then_inc(mask_out, 16)

            with sp.Fori(1, NP) as i:
                for h in range(2):
                    sp.wait_ge(turned, 6 * i - 3 + 3 * h - 0)
                    sp.dma_start(nat[:, h, :, :].rearrange("p t c -> p (t c)"),
                                 ctx_v[:, bass.ds(2 * i + h, 1), :].rearrange("p o c -> p (o c)")
                                 ).then_inc(loaded[h], 16)
            sp.wait_ge(mask_out, 16)

        @block.tensor
        def _(pe):
            def pair(i, first):
                for h in range(2):
                    pe.wait_ge(loaded[h], 16 * (i + 1))
                    for k in range(BANKS):
                        if not first:
                            pe.wait_ge(kept, 6 * i + 3 * h + k - 5)
                        for q in range(GT):
                            m = pe.transpose(ps[3 * h + k][0:C, q * NK:(q + 1) * NK], nat[:, h, k * GT + q, :],
                                             g.ident[0:NK, 0:NK])
                        m.then_inc(turned, 1)
            pair(0, True)
            with pe.Fori(1, NP) as i:
                pair(i, False)

        @block.vector
        def _(dve):
            dve.memset(tr[C:C + 1, :, :], 1.0).then_inc(ones, 1)
            dve.wait_ge(mask_in, 16)
            dve.tensor_scalar(maskf[:].rearrange("b (t p) -> b t p", t=KT),
                              mask8[:].rearrange("b (p t) -> b t p", t=KT), -1.0, None, ALU.add
                              ).then_inc(mask_done, 1)
            dve.wait_ge(mask_done, 1)
            dve.tensor_scalar(maskf[:], maskf[:], BIG, None, ALU.mult).then_inc(mask_done, 1)

            def pair(i, first):
                for h in range(2):
                    for k in range(BANKS):
                        dve.wait_ge(turned, 6 * i + 3 * h + k + 1)
                        if not first and k == 0:
                            dve.wait_ge(stored[h], 16 * i)
                        dve.tensor_copy(tr[0:C, h, k * BK:(k + 1) * BK], ps[3 * h + k][0:C, 0:BK]).then_inc(kept, 1)
            pair(0, True)
            with dve.Fori(1, NP) as i:
                pair(i, False)

        @block.scalar
        def _(act):
            act.wait_ge(ones, 1)
            with act.Fori(0, NP) as i:
                for h in range(2):
                    act.wait_ge(kept, 6 * i + 3 * h + 3)
                    act.dma_start(ctx_t[bass.ds(2 * i + h, 1), 0:CO, :].rearrange("o r s -> (o r) s"), tr[:, h, :]
                                  ).then_inc(stored[h], 16)
            for h in range(2):
                act.wait_ge(stored[h], 16 * NP)


def renorm(nc, g, name, base, addt=None, scale=None, raw_t=None, norm=True):
    with ExitStack() as ctx:
        st = Stage(nc, ctx, name)
        xc, sq = g.xn, st.sb("sq", [P, NT, D])
        mu, var, rstd = st.sb("mu", [P, NT]), st.sb("var", [P, NT]), st.sb("rstd", [P, NT])
        psa = [st.ps(f"psa{n}", [P, 4, P]) for n in range(4)]
        psb = [st.ps(f"psb{n}", [P, 4, P]) for n in range(4)]
        turned, based, raw_turned, dved = st.sem("turned"), st.sem("based"), st.sem("raw_turned"), st.sem("dved")
        raw_kept, powed, back, varred, normed = (st.sem(x) for x in ("raw_kept", "powed", "back", "varred", "normed"))
        kept = st.sem("kept")
        groups = [(n, 4 * n, min(4 * n + 4, NT)) for n in range(4)]
        block = ctx.enter_context(nc.Block())

        def bc(x, a, b):
            return x[:, a:b].rearrange("p (t o) -> p t o", o=1).broadcast_to([P, b - a, D])

        @block.tensor
        def _(pe):
            for n, a, b in groups if addt is not None else ():
                for t in range(a, b):
                    m = pe.transpose(psa[n][:, t - a, :], addt[:, t * P:(t + 1) * P], g.ident[:])
                m.then_inc(turned, 1)
            for n, a, b in groups if raw_t is not None else ():
                if addt is not None:
                    pe.wait_ge(based, n + 1)
                for t in range(a, b):
                    m = pe.transpose(psb[n][:, t - a, :], base[:, t, :], g.ident[:])
                m.then_inc(raw_turned, 1)
            for n, a, b in groups if norm else ():
                pe.wait_ge(normed, n + 1)
                if raw_t is not None:
                    pe.wait_ge(raw_kept, n + 1)
                for t in range(a, b):
                    m = pe.transpose(psb[n][:, t - a, :], g.xn[:, t, :], g.ident[:])
                m.then_inc(back, 1)

        @block.vector
        def _(dve):
            link = chain(dve, dved)
            for n, a, b in groups:
                v = base[:, a:b, :]
                if scale is not None:
                    link(dve.tensor_tensor(v, v, bc(scale, a, b), ALU.mult))
                if addt is not None:
                    dve.wait_ge(turned, n + 1)
                    dve.tensor_tensor(v, v, psa[n][:, 0:b - a, :], ALU.add).then_inc(based, 1)
                    dve.wait_ge(based, n + 1)
                if norm:
                    link(dve.tensor_reduce(mu[:, a:b], v, AX.X, ALU.add))
                    link(dve.tensor_scalar(mu[:, a:b], mu[:, a:b], 1.0 / D, None, ALU.mult))
                    link(dve.tensor_tensor(xc[:, a:b, :], v, bc(mu, a, b), ALU.subtract))
                    link(dve.tensor_tensor(sq[:, a:b, :], xc[:, a:b, :], xc[:, a:b, :], ALU.mult))
                    link(dve.tensor_reduce(var[:, a:b], sq[:, a:b, :], AX.X, ALU.add))
                    dve.tensor_scalar(var[:, a:b], var[:, a:b], 1.0 / D, EPS, ALU.mult, ALU.add).then_inc(varred, 1)
            for n, a, b in groups if norm else ():
                dve.wait_ge(powed, n + 1)
                dve.tensor_tensor(g.xn[:, a:b, :], xc[:, a:b, :], bc(rstd, a, b), ALU.mult).then_inc(normed, 1)

        @block.gpsimd
        def _(pool):
            for n, a, b in groups if norm else ():
                pool.wait_ge(varred, n + 1)
                pool.tensor_tensor(rstd[:, a:b], var[:, a:b], g.half[:, a:b], ALU.pow).then_inc(powed, 1)

        @block.scalar
        def _(act):
            for n, a, b in groups if raw_t is not None else ():
                act.wait_ge(raw_turned, n + 1)
                act.activation(raw_t[:, a * P:b * P].rearrange("p (t c) -> p t c", c=P), psb[n][:, 0:b - a, :],
                               ACT.Copy).then_inc(raw_kept, 1)
            for n, a, b in groups if norm else ():
                act.wait_ge(back, n + 1)
                act.activation(g.xnt[:, a * P:b * P].rearrange("p (t c) -> p t c", c=P), psb[n][:, 0:b - a, :],
                               ACT.Copy).then_inc(kept, 1)


def attention(nc, g, name, ctx_d, ctx_t, heads, kc, scale, loads, turns, masked, q_bias, o_bias, mask_row, vo_direct):
    hc = heads // kc
    with ExitStack() as outer:
        so = Stage(nc, outer, name)
        a_w = so.sb("a", [P, heads, CR])
        vo = so.sb("vo", [CO, heads, D])
        cb = so.sb("cb", [CR, heads])
        ob = so.sb("ob", [P, 1])

        with ExitStack() as ctx:
            st = Stage(nc, ctx, name + "w")
            buf = {n: st.sb(n, shape) for n, shape, _ in loads}
            wkm, wvm = st.sb("wkm", [P, heads, CR]), st.sb("wvm", [P, heads, CO])
            ps = [st.ps(f"ps{n}", [P, 512]) for n in range(8)]
            cleared, loaded, made, kept, mixed = (st.sem(x) for x in ("cleared", "loaded", "made", "kept", "masked"))
            tile = dict(buf, wkm=wkm, wvm=wvm, a=a_w, vo=vo, cb=cb, ob=ob)
            clears = [(tile[n][:], v) for n, v in masked["clear"]]
            if mask_row:
                clears += [(cb[C:CR, :], 1.0), (cb[C:CO, :], 0.0)]
            moves = [(tile[n], f, src) for n, _, ls in loads for f, src in ls]
            moves += [(tile[n], f, src) for n, f, src in masked["direct"]]
            jobs = [(lambda s=s: s(tile), None, w, n, lambda d=d: d(tile), 1.0) for s, w, n, d in turns]
            nturn = len(jobs)
            hg = min(hc, 5 if hc < 5 else 4)
            for k in range(kc):
                for h0 in range(0, hc, hg):
                    a, b = k * hc + h0, k * hc + h0 + hg
                    jobs.append((lambda k=k: tile["wq"][:, k, :], lambda a=a, b=b: wkm[:, a:b, :], D, hg * CR,
                                 lambda a=a, b=b: a_w[:, a:b, :], scale))
            if q_bias:
                for h in range(heads):
                    jobs.append((lambda h=h: wkm[:, h, :], lambda: tile["bq"][:, 0:1], CR, 1,
                                 lambda h=h: cb[:, h:h + 1], scale))
            if not vo_direct:
                for h in range(heads):
                    jobs.append((lambda h=h: wvm[:, h, :], lambda h=h: tile["wo"][:, h // hc, :], CO, D,
                                 lambda h=h: vo[:, h, :], 1.0))
            block = ctx.enter_context(nc.Block())

            @block.sync
            def _(sp):
                sp.wait_ge(cleared, len(clears))
                for t, f, src in moves:
                    with nc.allow_non_contiguous_dma(reason="biases as columns"):
                        sp.dma_start(f(t), src).then_inc(loaded, 16)
                sp.wait_ge(loaded, 16 * len(moves))

            @block.tensor
            def _(pe):
                pe.wait_ge(loaded, 16 * len(moves))
                for n, (lhs, rhs, rows, cols, _, _) in enumerate(jobs):
                    if n >= 8:
                        pe.wait_ge(kept, n - 7)
                    if n == nturn:
                        pe.wait_ge(mixed, 1 if vo_direct else 2)
                    if rhs is None:
                        src = lhs()
                        k = src.shape[0]
                        m = pe.transpose(ps[n % 8][0:rows, 0:cols], src, g.ident[0:k, 0:k])
                    else:
                        m = pe.matmul(ps[n % 8][0:rows, 0:cols], lhs(), rhs(), start=True, stop=True)
                    m.then_inc(made, 1)

            @block.vector
            def _(dve):
                for n, (t, v) in enumerate(clears):
                    dve.memset(t, v).then_inc(cleared, 1)
                    dve.wait_ge(cleared, n + 1)
                if heads == HEADS:
                    hm = g.hm8 if kc == 1 else g.hm64
                for n, (_, _, rows, cols, dst, sc) in enumerate(jobs):
                    if n == nturn:
                        dve.wait_ge(kept, nturn) if nturn else None
                        dve.wait_ge(loaded, 16 * len(moves))
                        for q, (dst_w, src_w, w) in enumerate(((wkm, "wkT", CR), (wvm, "wvT", CO))):
                            if q == 1 and vo_direct:
                                continue
                            s4 = tile[src_w][:, :, :].rearrange("p k (o c) -> p k o c", o=1)
                            d4 = dst_w[:, :, :].rearrange("p (k h) c -> p k h c", k=kc)
                            if heads == 1:
                                ins = dve.tensor_copy(d4, s4)
                            else:
                                m4 = hm[:, 0:hc].rearrange("p (k h c) -> p k h c", k=1, c=1)
                                ins = dve.tensor_tensor(d4, s4.broadcast_to([P, kc, hc, w]),
                                                        m4.broadcast_to([P, kc, hc, w]), ALU.mult)
                            ins.then_inc(mixed, 1)
                    dve.wait_ge(made, n + 1)
                    out, src = dst(), ps[n % 8][0:rows, 0:cols]
                    if len(out.shape) == 3:
                        src = src.rearrange("p (a b) -> p a b", a=out.shape[1])
                    dve.tensor_scalar(out, src, sc, None, ALU.mult).then_inc(kept, 1)

        full = heads == HEADS
        gp = 1 if full else 2
        ng = NP // gp
        slots = 2 * gp
        nu = 2 * HEADS * L // P if full else gp
        total = nu * ng
        tg = gp * PAIR
        hq = min(heads, TC // PAIR)
        nq = heads // hq
        width = heads * L if full else P // 2
        with ExitStack() as ctx:
            st = Stage(nc, ctx, name + "m")
            raw = st.sb("raw", [CR, slots, S])
            cxt = st.sb("cxt", [CR, slots, 2, S], F32R)
            cn = st.sb("cn", [NK, slots, KT, CO])
            q32 = st.sb("q32", [CR, TC])
            qhi, qlo = (st.sb(n, [CR, slots, width if full else P], F32R) for n in ("qhi", "qlo"))
            prob = st.sb("prob", [P, 2, S])
            prob_t = st.sb("prob_t", [NK, 2, KT, P])
            bank_max, neg_max = st.sb("bank_max", [P, 2, BANKS]), st.sb("neg_max", [P, 2])
            den, on = st.sb("den", [P, 2]), st.sb("on", [P, 2, CO])
            on_t = st.sb("on_t", [CO, slots, width])
            ps_s = st.ps("ps_s", [P, BANKS, 512])
            ps_t = [st.ps(f"ps_t{n}", [P, 512]) for n in range(2)]
            ps_o, ps_r, ps_q = st.ps("ps_o", [P, 512]), st.ps("ps_r", [P, 512]), st.ps("ps_q", [P, 512])
            ctx_in = [st.sem(f"ctx_in{h}") for h in range(slots)]
            ctxt_in = [st.sem(f"ctxt_in{h}") for h in range(slots)]
            high_made = [st.sem(f"high_made{h}") for h in range(slots)]
            low_made = [st.sem(f"low_made{h}") for h in range(slots)]
            (ones_set, scored, bank_maxed, maxed, exped, turned, kept_dve, kept_act, summed, denned, normed,
             o_turned, o_kept, q_made, q_added, q_kept, projected, out_kept) = (st.sem(x) for x in (
                 "ones_set", "scored", "bank_maxed", "maxed", "exped", "turned", "kept_dve", "kept_act", "summed",
                 "denned", "normed", "o_turned", "o_kept", "q_made", "q_added", "q_kept", "projected", "out_kept"))
            ctx_v = ctx_d.rearrange("b (p t) c -> p b t c", t=KT)
            block = ctx.enter_context(nc.Block())

            def sequences(u):
                u %= nu
                return [u * slots // nu] if full else [2 * u, 2 * u + 1]

            def first_of(u):
                return not full or u % nu % (nu // 2) == 0

            def used(h):
                return (h + 1) * nu // 2 if full else h // 2 + 1

            peel = -(-4 // nu)
            behind = 1 + 3 // nu

            def steps(eng, step):
                for i in range(peel):
                    for u in range(nu):
                        step(i, u)
                with eng.Fori(peel, ng if full else ng - 1) as i:
                    for u in range(nu):
                        step(i, u)
                if not full:
                    for u in range(nu):
                        step(ng - 1, u)
                for u in range(4):
                    step(ng, u)

            def live(i, u, lag):
                return not isinstance(i, int) or 0 <= nu * i + u - lag < total

            def later(i, u, lag):
                return not isinstance(i, int) or nu * i + u - lag > 0

            def low_part(eng, i, h):
                eng.wait_ge(high_made[h], i + 1)
                eng.tensor_tensor(cxt[:, h, 1, :], raw[:, h, :], cxt[:, h, 0, :].bitcast(F32), ALU.subtract
                                  ).then_inc(low_made[h], 1)

            @block.sync
            def _(sp):
                sp.wait_ge(ones_set, 3)

                def load_turned(i, first):
                    for h in range(slots):
                        if not first:
                            sp.wait_ge(low_made[h], i)
                        sp.dma_start(raw[:, h, :], ctx_t[bass.ds(slots * i + h, 1), :, :].rearrange("o r s -> (o r) s")
                                     ).then_inc(ctxt_in[h], 16)

                def load(i, first):
                    for h in range(slots):
                        if not first:
                            sp.wait_ge(summed, nu * i - nu + used(h))
                        sp.dma_start(cn[:, h, :, 0:C],
                                     ctx_v[:, bass.ds(slots * i + h, 1), :, :].rearrange("p o t c -> p (o t) c")
                                     ).then_inc(ctx_in[h], 16)

                load_turned(0, True)
                load_turned(1, False)
                load(0, True)
                with sp.Fori(1, ng - 1) as i:
                    load_turned(i + 1, False)
                    load(i, False)
                load(ng - 1, False)
                for h in range(slots):
                    sp.wait_ge(ctx_in[h], 16 * ng)
                    sp.wait_ge(ctxt_in[h], 16 * ng)

            @block.gpsimd
            def _(pool):
                def split(i, first):
                    for h in range(slots):
                        if full:
                            pool.wait_ge(ctxt_in[h], 16 * (i + 1))
                            if not first:
                                pool.wait_ge(scored, BANKS * (nu * i - nu + used(h)))
                            pool.tensor_tensor(cxt[:, h, 0, :], raw[:, h, :],
                                               g.zeros[0:CR, 0:1].broadcast_to([CR, S]), ALU.add).then_inc(high_made[h], 1)
                        if full or h % 2:
                            low_part(pool, i, h)
                split(0, True)
                with pool.Fori(1, ng) as i:
                    split(i, False)

            @block.tensor
            def _(pe):
                def queries(i, q):
                    n = nq * i + q
                    if not isinstance(n, int) or n > 0:
                        pe.wait_ge(q_kept, n)
                    if q == 0 and (not isinstance(i, int) or i > behind):
                        pe.wait_ge(out_kept, i - behind)
                    for h in range(hq):
                        m = pe.matmul(ps_q[0:CR, h * tg:(h + 1) * tg], a_w[:, q * hq + h, :],
                                      g.xnt[:, bass.ds(i * tg, tg)], start=True, stop=True)
                    m.then_inc(q_made, 1)

                def scores(i, u):
                    v = nu * i + u
                    for h in sequences(u) if first_of(u) else ():
                        pe.wait_ge(low_made[h], i + 1)
                    if u == 0:
                        pe.wait_ge(q_kept, nq * (i + 1))
                    for k in range(BANKS):
                        if later(i, u, 0):
                            pe.wait_ge(exped, BANKS * (v - 1) + k + 1)
                        keys = slice(k * BK, (k + 1) * BK)
                        for h in sequences(u):
                            at = (slice(u * P - h * width, (u + 1) * P - h * width)) if full else slice(0, P)
                            for part, w in ((qhi, 0), (qhi, 1), (qlo, 0)):
                                m = pe.matmul(ps_s[:, k, 0:BK], part[:, h, at], cxt[:, h, w, keys],
                                              start=(part is qhi and w == 0 and h == sequences(u)[0]),
                                              stop=(part is qlo and h == sequences(u)[-1]))
                        m.then_inc(scored, 1)

                def turn(i, u, k):
                    v = nu * i + u
                    pe.wait_ge(exped, BANKS * v + k + 1)
                    if k < 2:
                        if later(i, u, 0):
                            pe.wait_ge(*((kept_dve, 2 * v) if k == 0 else (kept_act, v)))
                    else:
                        pe.wait_ge(kept_dve, 2 * v + 1)
                    for q in range(GT):
                        t = k * GT + q
                        m = pe.transpose(ps_t[(BANKS * u + k) % 2][0:NK, q * P:(q + 1) * P],
                                         prob[:, u % 2, t * NK:(t + 1) * NK], g.ident[:])
                    m.then_inc(turned, 1)

                def sums(i, u):
                    v = nu * i + u
                    pe.wait_ge(kept_dve, 2 * v + 2)
                    pe.wait_ge(kept_act, v + 1)
                    for h in sequences(u) if first_of(u) else ():
                        pe.wait_ge(ctx_in[h], 16 * (i + 1 + (u // nu)))
                    if later(i, u, 0):
                        pe.wait_ge(normed, v)
                    hs = sequences(u)
                    part = P // len(hs)
                    for n, h in enumerate(hs):
                        at = slice(n * part, (n + 1) * part)
                        for t in range(KT):
                            m = pe.matmul(ps_o[at, 0:CO], prob_t[:, u % 2, t, at], cn[:, h, t, :],
                                          start=(t == 0), stop=(t == KT - 1))
                    m.then_inc(summed, 1)

                def o_turn(i, u):
                    v = nu * i + u
                    pe.wait_ge(normed, v + 1)
                    if later(i, u, 0):
                        pe.wait_ge(o_kept, v)
                    pe.transpose(ps_r[0:CO, 0:P], on[:, u % 2, :], g.ident[:]).then_inc(o_turned, 1)

                def project(i):
                    pe.wait_ge(o_kept, nu * (i + 1))
                    n = nq * (i + behind + 1)
                    pe.wait_ge(q_kept, min(n, nq * (ng + 1)) if isinstance(i, int) else n)
                    for h in range(heads):
                        m = pe.matmul(ps_q[:, 0:tg], vo[:, h, :], on_t[:, :, h * L:(h + 1) * L],
                                      start=(h == 0), stop=(h == heads - 1))
                    m.then_inc(projected, 1)

                def step(i, u):
                    if live(i, u, 0):
                        scores(i, u)
                    if live(i, u, 1):
                        turn(i, u - 1, 0)
                        turn(i, u - 1, 1)
                    if (u - 4) % nu == nu - 1 and live(i, u, 4):
                        project(i + (u - 4) // nu)
                    if live(i, u, 3):
                        o_turn(i, u - 3)
                    if live(i, u, 0) and u == nu - 1:
                        for q in range(nq):
                            queries(i + 1, q)
                    if live(i, u, 2):
                        sums(i, u - 2)
                    if live(i, u, 1):
                        turn(i, u - 1, 2)

                for q in range(nq):
                    queries(0, q)
                steps(pe, step)

            @block.vector
            def _(dve):
                def queries(i):
                    for q in range(nq):
                        n = nq * i + q
                        src = ps_q[0:CR, 0:hq * tg].rearrange("p (h b l) -> p b h l", h=hq, b=slots)
                        mid = q32[:, 0:hq * tg].rearrange("p (b h l) -> p b h l", b=slots, h=hq)
                        bias = cb[:, q * hq:(q + 1) * hq].rearrange("p (b h l) -> p b h l", b=1, l=1)
                        dve.wait_ge(q_made, n + 1)
                        dve.tensor_tensor(mid, src, bias.broadcast_to([CR, slots, hq, L]), ALU.add
                                          ).then_inc(q_added, 1)
                        if full:
                            cols = slice(q * hq * L, (q + 1) * hq * L)
                            views = [(qhi[:, :, cols], qlo[:, :, cols], q32[:, 0:hq * tg].rearrange(
                                "p (b c) -> p b c", b=slots))]
                        else:
                            views = [tuple(x[:, h::2, P // 2 * h:P // 2 * h + L] for x in (qhi, qlo)) +
                                     (q32[:, 0:tg].rearrange("p (b c) -> p b c", b=slots)[:, h::2, :],)
                                     for h in range(2)]
                        dve.wait_ge(q_added, (1 + len(views)) * n + 1)
                        for hi, _, x in views:
                            dve.tensor_copy(hi, x).then_inc(q_added, 1)
                        dve.wait_ge(q_added, (1 + len(views)) * (n + 1))
                        for m, (hi, lo, x) in enumerate(views):
                            ins = dve.tensor_tensor(lo, x, hi.bitcast(F32), ALU.subtract)
                        ins.then_inc(q_kept, 1)

                def maxima(i, u):
                    s = u % 2
                    v = nu * i + u
                    for k in range(BANKS):
                        dve.wait_ge(scored, BANKS * v + k + 1)
                        dve.tensor_reduce(bank_max[:, s, k:k + 1], ps_s[:, k, 0:BK], AX.X, ALU.max
                                          ).then_inc(bank_maxed, 1)
                    dve.wait_ge(bank_maxed, BANKS * (v + 1))
                    dve.tensor_reduce(neg_max[:, s:s + 1], bank_max[:, s, :], AX.X, ALU.max, negate=True
                                      ).then_inc(maxed, 1)

                def keep(i, u, k):
                    v = nu * i + u
                    dve.wait_ge(turned, BANKS * v + k + 1)
                    if later(i, u, 1):
                        dve.wait_ge(summed, v - 1)
                    dve.tensor_copy(prob_t[:, u % 2, k * GT:(k + 1) * GT, :],
                                    ps_t[(BANKS * u + k) % 2][0:NK, :].rearrange("p (t r) -> p t r", t=GT)
                                    ).then_inc(kept_dve, 1)

                def normalise(i, u):
                    s = u % 2
                    v = nu * i + u
                    dve.wait_ge(summed, v + 1)
                    dve.reciprocal(den[:, s:s + 1], ps_o[:, C:CO]).then_inc(denned, 1)
                    dve.wait_ge(denned, v + 1)
                    if later(i, u, 1):
                        dve.wait_ge(o_turned, v - 1)
                    dve.tensor_scalar(on[:, s, :], ps_o[:, 0:CO], den[:, s:s + 1], None, ALU.mult
                                      ).then_inc(normed, 1)

                def step(i, u):
                    if live(i, u, 0):
                        maxima(i, u)
                    if live(i, u, 1):
                        keep(i, u - 1, 0)
                        keep(i, u - 1, 1)
                    if live(i, u, 0) and u == nu - 1:
                        queries(i + 1)
                    if not full and live(i, u, -nu):
                        low_part(dve, i + 1, 2 * u)
                    if live(i, u, 2):
                        normalise(i, u - 2)

                dve.memset(qhi[:].bitcast(F32), 0.0).then_inc(ones_set, 1)
                dve.memset(qlo[:].bitcast(F32), 0.0).then_inc(ones_set, 1)
                dve.memset(cn[:, :, :, C:CO], 1.0).then_inc(ones_set, 1)
                dve.wait_ge(ones_set, 2)
                queries(0)
                if not full:
                    for u in range(nu):
                        low_part(dve, 0, 2 * u)
                steps(dve, step)

            @block.scalar
            def _(act):
                def high_part(i, u):
                    for h in sequences(u):
                        act.wait_ge(ctxt_in[h], 16 * (i + 1))
                        act.activation(cxt[:, h, 0, :], raw[:, h, :], ACT.Copy).then_inc(high_made[h], 1)

                def exps(i, u):
                    s = u % 2
                    v = nu * i + u
                    act.wait_ge(maxed, v + 1)
                    if later(i, u, 1):
                        act.wait_ge(turned, BANKS * (v - 1))
                    for k in range(BANKS):
                        act.activation(prob[:, s, k * BK:(k + 1) * BK], ps_s[:, k, 0:BK], ACT.Exp,
                                       bias=neg_max[:, s:s + 1]).then_inc(exped, 1)

                def keep(i, u):
                    v = nu * i + u
                    act.wait_ge(turned, BANKS * (v + 1))
                    if later(i, u, 1):
                        act.wait_ge(summed, v - 1)
                    act.activation(prob_t[:, u % 2, 2 * GT:KT, :],
                                   ps_t[(BANKS * u + 2) % 2][0:NK, :].rearrange("p (t r) -> p t r", t=GT),
                                   ACT.Copy).then_inc(kept_act, 1)

                def o_keep(i, u):
                    v = nu * i + u
                    act.wait_ge(o_turned, v + 1)
                    if u % nu == 0 and (not isinstance(i, int) or v > 0):
                        act.wait_ge(projected, i + u // nu)
                    flat = on_t[:].rearrange("p b c -> p (b c)")
                    act.activation(flat[:, u % nu * P:(u % nu + 1) * P], ps_r[0:CO, 0:P], ACT.Copy
                                   ).then_inc(o_kept, 1)

                def out(i):
                    act.wait_ge(projected, i + 1)
                    act.activation(g.addt[:, bass.ds(i * tg, tg)], ps_q[:, 0:tg], ACT.Identity,
                                   bias=ob[:, 0:1]).then_inc(out_kept, 1)

                def step(i, u):
                    if live(i, u, 0):
                        exps(i, u)
                    if (u - 4) % nu == nu - 1 and live(i, u, 4):
                        out(i + (u - 4) // nu)
                    if live(i, u, 3):
                        o_keep(i, u - 3)
                    if live(i, u, 1):
                        keep(i, u - 1)
                    if not full and live(i, u, -nu):
                        high_part(i + 1, u)

                if not full:
                    for u in range(nu):
                        high_part(0, u)
                steps(act, step)


def head_rows(x, part):
    if len(x.shape) == 2:
        return x.rearrange("(h k d) c -> k h d c", h=HEADS, k=2)[part]
    return x.rearrange("(h k d) -> k h d", h=HEADS, k=2)[part]


def col(x):
    return x.rearrange("(p o) -> p o", o=1)


def spread(x, n):
    return x.rearrange("p (t o) -> p t o", o=1).broadcast_to([P, NT, n])


def logits(nc, g, name, xt, experts, w_dram, b_dram, w_turned, out):
    with ExitStack() as ctx:
        st = Stage(nc, ctx, name)
        raw, w, bias = st.sb("raw", [16, D]), st.sb("w", [D, experts]), st.sb("bias", [1, experts])
        psw, psl = st.ps("psw", [P, 512]), st.ps("psl", [P, NT, experts])
        loaded, turned, kept, made, done = (st.sem(x) for x in ("loaded", "turned", "kept", "made", "done"))
        n_in = 1 + (b_dram is not None)
        block = ctx.enter_context(nc.Block())

        @block.sync
        def _(sp):
            if b_dram is not None:
                sp.dma_start(bias[:], b_dram.rearrange("(o e) -> o e", o=1)).then_inc(loaded, 16)
            sp.dma_start(w[:] if w_turned else raw[0:experts, :], w_dram).then_inc(loaded, 16)
            sp.wait_ge(loaded, 16 * n_in)

        @block.tensor
        def _(pe):
            pe.wait_ge(loaded, 16 * n_in)
            if not w_turned:
                pe.transpose(psw[:, 0:experts], raw[0:experts, :], g.ident[0:experts, 0:experts]).then_inc(turned, 1)
                pe.wait_ge(kept, 1)
            for t in range(NT):
                if b_dram is not None:
                    pe.matmul(psl[:, t, :], g.ones[0:1, :], bias[:], start=True, stop=False)
                m = pe.matmul(psl[:, t, :], xt[:, t * P:(t + 1) * P], w[:], start=b_dram is None, stop=True)
            m.then_inc(made, 1)

        @block.vector
        def _(dve):
            if not w_turned:
                dve.wait_ge(turned, 1)
                dve.tensor_copy(w[:], psw[:, 0:experts]).then_inc(kept, 1)
            dve.wait_ge(made, 1)
            dve.tensor_copy(out, psl[:, :, :]).then_inc(done, 1)


def turn_weights(nc, g, name, experts, src, dst):
    with ExitStack() as ctx:
        st = Stage(nc, ctx, name)
        ps = [st.ps(f"ps{n}", [P, 512]) for n in range(4)]
        made, kept = st.sem("made"), st.sem("kept")
        block = ctx.enter_context(nc.Block())

        @block.tensor
        def _(pe):
            for n in range(4):
                for t in range(4 * n, min(4 * n + 4, NT)):
                    m = pe.transpose(ps[n][0:experts, (t % 4) * P:(t % 4 + 1) * P], src[:, t, :], g.ident[:])
                m.then_inc(made, 1)

        @block.vector
        def _(dve):
            for n in range(4):
                a, b = 512 * n, min(512 * n + 512, T)
                dve.wait_ge(made, n + 1)
                dve.tensor_copy(dst[0:experts, a:b], ps[n][0:experts, 0:b - a]).then_inc(kept, 1)


def route_mixer(nc, g, full, gw):
    with ExitStack() as ctx:
        st = Stage(nc, ctx, "mixer")
        t8 = lambda n: st.sb(n, [P, NT, 8])
        t1 = lambda n: st.sb(n, [P, NT])
        dyn, top, ptop, idx = t8("dyn"), t8("top"), t8("ptop"), st.sb("idx", [P, NT, 8], U32)
        idxf, mag, hot, alive, e1, e2, e3, rw, mask = (t8(n) for n in (
            "idxf", "mag", "hot", "alive", "e1", "e2", "e3", "rw", "mask"))
        s1, s2, csum, valid = t1("s1"), t1("s2"), t1("csum"), t1("valid")
        w9, carry = st.sb("w9", [P, NT, 9]), st.sb("carry", [P, NT, 8])
        ps = st.ps("ps", [P, 512])
        pst = st.ps("pst", [P, 512])
        dved, asked, exped, masked, counted = (st.sem(x) for x in ("dved", "asked", "exped", "masked", "counted"))
        block = ctx.enter_context(nc.Block())
        exps = []

        @block.vector
        def _(dve):
            link = chain(dve, dved)

            def exp(tile):
                exps.append(tile)
                dve.wait_ge(exped, len(exps))

            def tt(out, a, b, op):
                link(dve.tensor_tensor(out, a, b, op))

            def ask(ins):
                ins.then_inc(asked, 1)

            link(dve.tensor_copy(dyn[:], full[:, :, 0:8]))
            for t in range(NT):
                dve.max(top[:, t, :], dyn[:, t, :]).then_inc(dved, 1)
            dve.wait_ge(dved, 1 + NT)
            for t in range(NT):
                dve.max_index(idx[:, t, :], top[:, t, :], dyn[:, t, :]).then_inc(dved, 1)
            dve.wait_ge(dved, 1 + 2 * NT)
            done = [1 + 2 * NT]

            def link(ins):
                done[0] += 1
                ins.then_inc(dved, 1)
                dve.wait_ge(dved, done[0])

            link(dve.tensor_copy(idxf[:], idx[:]))
            link(dve.scalar_tensor_tensor(mag[:], dyn[:], -1.0, dyn[:], ALU.mult, ALU.max))
            ask(dve.tensor_tensor(ptop[:], top[:], top[:, :, 0:1].broadcast_to([P, NT, 8]), ALU.subtract))
            exp(ptop[:])
            link(dve.tensor_reduce(s1[:], ptop[:], AX.X, ALU.add))
            link(dve.reciprocal(s1[:], s1[:]))
            link(dve.tensor_tensor(ptop[:], ptop[:], spread(s1[:], 8), ALU.mult))
            link(dve.memset(csum[:], 0.0))
            link(dve.memset(alive[:], 1.0))
            link(dve.memset(rw[:], 0.0))
            for k in range(4):
                thr = top[:, :, k:k + 1].broadcast_to([P, NT, 8])
                link(dve.tensor_scalar(valid[:], csum[:], 0.75, None, ALU.is_lt))
                link(dve.tensor_tensor(csum[:], csum[:], ptop[:, :, k], ALU.add))
                link(dve.tensor_tensor(hot[:], idxf[:, :, k:k + 1].broadcast_to([P, NT, 8]),
                                       g.iota8[:].rearrange("p (o e) -> p o e", o=1).broadcast_to([P, NT, 8]),
                                       ALU.is_equal))
                link(dve.tensor_tensor(e1[:], thr, dyn[:], ALU.subtract))
                link(dve.tensor_scalar(s2[:], top[:, :, k], -1.0, None, ALU.mult))
                link(dve.tensor_tensor(s2[:], s2[:], top[:, :, k], ALU.max))
                link(dve.tensor_tensor(e2[:], mag[:], spread(s2[:], 8), ALU.max))
                link(dve.tensor_scalar(e2[:], e2[:], 1e-37, None, ALU.max))
                link(dve.reciprocal(e2[:], e2[:]))
                link(dve.tensor_tensor(e2[:], e1[:], e2[:], ALU.mult))
                link(dve.tensor_scalar(e2[:], e2[:], 0.2, None, ALU.is_le))
                link(dve.tensor_tensor(e2[:], e2[:], alive[:], ALU.mult))
                ask(dve.tensor_scalar(e3[:], e1[:], 0.0, -1.0, ALU.max, ALU.mult))
                exp(e3[:])
                link(dve.tensor_tensor(e3[:], e3[:], e2[:], ALU.mult))
                link(dve.tensor_reduce(s1[:], e3[:], AX.X, ALU.add))
                link(dve.reciprocal(s1[:], s1[:]))
                link(dve.tensor_tensor(s1[:], s1[:], valid[:], ALU.mult))
                link(dve.tensor_tensor(e1[:], hot[:], spread(s1[:], 8), ALU.mult))
                link(dve.tensor_tensor(rw[:], rw[:], e1[:], ALU.add))
                link(dve.tensor_tensor(alive[:], alive[:], hot[:], ALU.subtract))
            link(dve.tensor_reduce(s1[:], rw[:], AX.X, ALU.add))
            link(dve.reciprocal(s1[:], s1[:]))
            link(dve.tensor_tensor(rw[:], rw[:], spread(s1[:], 8), ALU.mult))
            dve.tensor_scalar(mask[:], rw[:], 0.0, None, ALU.is_gt).then_inc(masked, 1)
            dve.wait_ge(counted, 1)
            link(dve.memset(carry[:, 0, :], 0.0))
            for t in range(1, NT):
                link(dve.tensor_tensor(carry[:, t, :], carry[:, t - 1, :], pst[:, (t - 1) * 8:t * 8], ALU.add))
            link(dve.tensor_tensor(carry[:], carry[:], ps[:, 0:NT * 8].rearrange("p (t e) -> p t e", e=8), ALU.add))
            link(dve.tensor_scalar(carry[:], carry[:], float(CAP), None, ALU.is_le))
            dve.wait_ge(masked, 1)
            link(dve.tensor_tensor(mask[:], mask[:], carry[:], ALU.mult))
            link(dve.tensor_scalar(e1[:], mask[:], -1.0, BIG, ALU.add, ALU.mult))
            link(dve.tensor_tensor(w9[:, :, 0:8], dyn[:], e1[:], ALU.add))
            link(dve.tensor_copy(w9[:, :, 8:9], full[:, :, 8:9]))
            link(dve.tensor_reduce(s1[:], w9[:], AX.X, ALU.max))
            ask(dve.tensor_tensor(w9[:], w9[:], spread(s1[:], 9), ALU.subtract))
            exp(w9[:])
            link(dve.tensor_reduce(s1[:], w9[:], AX.X, ALU.add))
            link(dve.reciprocal(s1[:], s1[:]))
            link(dve.tensor_tensor(w9[:], w9[:], spread(s1[:], 9), ALU.mult))
            link(dve.tensor_reduce(s1[:], w9[:, :, 0:8], AX.X, ALU.add))
            link(dve.tensor_tensor(rw[:], rw[:], spread(s1[:], 8), ALU.mult))
            link(dve.tensor_tensor(gw[:, :, 0:8], rw[:], mask[:], ALU.mult))
            link(dve.tensor_copy(gw[:, :, 8:9], w9[:, :, 8:9]))

        @block.scalar
        def _(act):
            for n, tile in enumerate(exps):
                act.wait_ge(asked, n + 1)
                act.activation(tile, tile, ACT.Exp).then_inc(exped, 1)

        @block.tensor
        def _(pe):
            pe.wait_ge(masked, 1)
            m = mask[:].rearrange("p t e -> p (t e)")
            pe.matmul(ps[:, 0:NT * 8], g.tri[:], m, start=True, stop=True)
            pe.matmul(pst[:, 0:NT * 8], g.ones[:], m, start=True, stop=True).then_inc(counted, 1)


def route_top2(nc, g, name, lg, experts, of_probs, w, wsum):
    with ExitStack() as ctx:
        st = Stage(nc, ctx, name)
        t8 = lambda n: st.sb(n, [P, NT, 8])
        v, top, idxf, h0, h1 = t8("v"), t8("top"), t8("idxf"), t8("h0"), t8("h1")
        idx = st.sb("idx", [P, NT, 8], U32)
        s1, s2 = st.sb("s1", [P, NT]), st.sb("s2", [P, NT])
        dved, asked, exped = st.sem("dved"), st.sem("asked"), st.sem("exped")
        block = ctx.enter_context(nc.Block())

        @block.vector
        def _(dve):
            link = chain(dve, dved)
            if of_probs:
                link(dve.memset(v[:], -1.0))
                link(dve.tensor_reduce(s1[:], lg, AX.X, ALU.max))
                dve.tensor_tensor(v[:, :, 0:experts], lg, spread(s1[:], experts), ALU.subtract).then_inc(asked, 1)
                dve.wait_ge(exped, 1)
                link(dve.tensor_reduce(s1[:], v[:, :, 0:experts], AX.X, ALU.add))
                link(dve.reciprocal(s1[:], s1[:]))
                link(dve.tensor_tensor(v[:, :, 0:experts], v[:, :, 0:experts], spread(s1[:], experts), ALU.mult))
            else:
                link(dve.tensor_copy(v[:], lg))
            for t in range(NT):
                link(dve.max(top[:, t, :], v[:, t, :]))
            for t in range(NT):
                link(dve.max_index(idx[:, t, :], top[:, t, :], v[:, t, :]))
            link(dve.tensor_copy(idxf[:], idx[:]))
            iota = g.iota8[:].rearrange("p (o e) -> p o e", o=1).broadcast_to([P, NT, 8])
            link(dve.tensor_tensor(h0[:], idxf[:, :, 0:1].broadcast_to([P, NT, 8]), iota, ALU.is_equal))
            link(dve.tensor_tensor(h1[:], idxf[:, :, 1:2].broadcast_to([P, NT, 8]), iota, ALU.is_equal))
            if not of_probs:
                dve.tensor_tensor(v[:, :, 0:2], top[:, :, 0:2], top[:, :, 0:1].broadcast_to([P, NT, 2]),
                                  ALU.subtract).then_inc(asked, 1)
                dve.wait_ge(exped, 1)
                link(dve.tensor_copy(top[:, :, 0:2], v[:, :, 0:2]))
            link(dve.tensor_tensor(s1[:], top[:, :, 0], top[:, :, 1], ALU.add))
            link(dve.reciprocal(s1[:], s1[:]))
            link(dve.tensor_tensor(s2[:], top[:, :, 1], s1[:], ALU.mult))
            link(dve.tensor_tensor(s1[:], top[:, :, 0], s1[:], ALU.mult))
            link(dve.tensor_tensor(h0[:], h0[:], spread(s1[:], 8), ALU.mult))
            link(dve.tensor_tensor(h1[:], h1[:], spread(s2[:], 8), ALU.mult))
            link(dve.tensor_tensor(w, h0[:, :, 0:experts], h1[:, :, 0:experts], ALU.add))
            if wsum is not None:
                link(dve.tensor_reduce(wsum, w, AX.X, ALU.add))

        @block.scalar
        def _(act):
            act.wait_ge(asked, 1)
            t = v[:, :, 0:experts if of_probs else 2]
            act.activation(t, t, ACT.Exp).then_inc(exped, 1)


def gated_mlp(nc, g, name, packs, up_srcs, down_srcs, pick, experts, gwt):
    with ExitStack() as outer:
        so = Stage(nc, outer, name)
        wg, wu, wd = (so.sb(n, [P, packs, D]) for n in ("wg", "wu", "wd"))
        with ExitStack() as ctx:
            st = Stage(nc, ctx, name + "w")
            raw = [st.sb(f"raw{n}", [P, packs, D]) for n in range(2)] + [st.sb("raw2", [P, packs * P])]
            ps = [st.ps(f"ps{n}", [P, 512]) for n in range(8)]
            loaded, made, kept = st.sem("loaded"), st.sem("made"), st.sem("kept")
            jobs = [(raw[w][:, k, :], (wg, wu)[w][:, k, :]) for w in range(2) for k in range(packs)]
            jobs += [(raw[2][:, k * P:(k + 1) * P], wd[:, k, :]) for k in range(packs)]
            n_in = len(up_srcs) + len(down_srcs)
            block = ctx.enter_context(nc.Block())

            @block.sync
            def _(sp):
                for w, k, n, src in up_srcs:
                    sp.dma_start(raw[w][:, k:k + n, :], src.rearrange("(k p) d -> p k d", p=P)).then_inc(loaded, 16)
                for k, n, src in down_srcs:
                    sp.dma_start(raw[2][:, k * P:(k + n) * P].rearrange("d (e i) -> d e i", e=src.shape[0]),
                                 src.rearrange("e d i -> d e i")).then_inc(loaded, 16)
                sp.wait_ge(loaded, 16 * n_in)

            @block.tensor
            def _(pe):
                pe.wait_ge(loaded, 16 * n_in)
                for n, (src, _) in enumerate(jobs):
                    if n >= 8:
                        pe.wait_ge(kept, n - 7)
                    pe.transpose(ps[n % 8][:, 0:P], src, g.ident[:]).then_inc(made, 1)

            @block.vector
            def _(dve):
                for n, (_, dst) in enumerate(jobs):
                    dve.wait_ge(made, n + 1)
                    dve.tensor_copy(dst, ps[n % 8][:, 0:P]).then_inc(kept, 1)

        with ExitStack() as ctx:
            st = Stage(nc, ctx, name + "m")
            sg, up, hid = (st.sb(n, [P, 2, TC]) for n in ("sg", "up", "hid"))
            ps_g, ps_u, ps_w = ([st.ps(f"ps_{n}{k}", [P, 512]) for k in range(2)] for n in "guw")
            ps_y = st.ps("ps_y", [P, 512])
            gated, made, silued, upped, weighted, added, kept = (st.sem(x) for x in (
                "gated", "made", "silued", "upped", "weighted", "added", "kept"))
            block = ctx.enter_context(nc.Block())

            @block.tensor
            def _(pe):
                def down(c, k):
                    n = packs * c + k
                    pe.wait_ge(weighted, n + 1)
                    pe.matmul(ps_y[:, 0:TC], wd[:, k, :], hid[:, k % 2, :], start=(k == 0), stop=(k == packs - 1)
                              ).then_inc(added, 1)

                def chunk(c, first):
                    x = g.xnt[:, bass.ds(c * TC, TC)]
                    for k in range(packs):
                        n = packs * c + k
                        if not first or k >= 2:
                            pe.wait_ge(silued, n - 1)
                        pe.matmul(ps_g[k % 2][:, 0:TC], wg[:, k, :], x, start=True, stop=True).then_inc(gated, 1)
                        if not first or k >= 2:
                            pe.wait_ge(weighted, n - 1)
                        pe.matmul(ps_u[k % 2][:, 0:TC], wu[:, k, :], x, start=True, stop=True)
                        pe.matmul(ps_w[k % 2][:, 0:TC], pick[0:experts, k * P:(k + 1) * P],
                                  gwt[0:experts, bass.ds(c * TC, TC)], start=True, stop=True).then_inc(made, 1)
                        if k == 1 and not first:
                            pe.wait_ge(kept, c)
                        if k > 0:
                            down(c, k - 1)
                    down(c, packs - 1)
                chunk(0, True)
                with pe.Fori(1, NC) as c:
                    chunk(c, False)

            @block.scalar
            def _(act):
                def chunk(c, first):
                    for k in range(packs):
                        n = packs * c + k
                        act.wait_ge(gated, n + 1)
                        if not first or k >= 2:
                            act.wait_ge(upped, n - 1)
                        act.activation(sg[:, k % 2, :], ps_g[k % 2][:, 0:TC], ACT.Silu).then_inc(silued, 1)
                    act.wait_ge(added, packs * (c + 1))
                    act.activation(g.addt[:, bass.ds(c * TC, TC)], ps_y[:, 0:TC], ACT.Copy).then_inc(kept, 1)
                chunk(0, True)
                with act.Fori(1, NC) as c:
                    chunk(c, False)

            @block.vector
            def _(dve):
                def chunk(c, first):
                    for k in range(packs):
                        n = packs * c + k
                        dve.wait_ge(silued, n + 1)
                        dve.wait_ge(made, n + 1)
                        dve.tensor_tensor(up[:, k % 2, :], sg[:, k % 2, :], ps_u[k % 2][:, 0:TC], ALU.mult
                                          ).then_inc(upped, 1)
                        dve.wait_ge(upped, n + 1)
                        if not first or k >= 2:
                            dve.wait_ge(added, n - 1)
                        dve.tensor_tensor(hid[:, k % 2, :], up[:, k % 2, :], ps_w[k % 2][:, 0:TC], ALU.mult
                                          ).then_inc(weighted, 1)
                chunk(0, True)
                with dve.Fori(1, NC) as c:
                    chunk(c, False)


ME, MF = 4, 4


def moe_layer(nc, g, name, w1_d, w2_d, b1_d, b2_d, lg_d, lb_d, gwt):
    with ExitStack() as ctx:
        st = Stage(nc, ctx, name)
        w1, w2 = st.sb("w1", [D, ME, MF, P]), st.sb("w2", [P, ME, MF, D])
        b1, b2, lng, lnb = st.sb("b1", [P, ME, MF]), st.sb("b2", [D, ME]), st.sb("lng", [D, ME]), st.sb("lnb", [D, ME])
        xe, hid, y, wb = st.sb("xe", [D, 2, TC]), st.sb("hid", [P, 2, TC]), st.sb("y", [D, TC]), st.sb("wb", [D, 2, TC])
        ps_h, ps_y, ps_w = ([st.ps(f"ps_{n}{k}", [P, 512]) for k in range(2)] for n in "hyw")
        loaded, scaled, upped, gelued, summed, spread_, wkept, yed, added = (st.sem(x) for x in (
            "loaded", "scaled", "upped", "gelued", "summed", "spread", "wkept", "yed", "added"))
        half = st.sem("half")
        block = ctx.enter_context(nc.Block())

        @block.sync
        def _(sp):
            sp.dma_start(w1[:].rearrange("h e k f -> h e (k f)"), w1_d.rearrange("e h f -> h e f")).then_inc(loaded, 16)
            with nc.allow_non_contiguous_dma(reason="vectors as columns"):
                sp.dma_start(b1[:], b1_d.rearrange("e (k p) -> p e k", p=P)).then_inc(loaded, 16)
                for t, src in ((b2, b2_d), (lng, lg_d), (lnb, lb_d)):
                    sp.dma_start(t[:], src.rearrange("e h -> h e")).then_inc(loaded, 16)
            sp.dma_start(w2[:].rearrange("p e k h -> p (e k) h"), w2_d.rearrange("e (k p) h -> p (e k) h", p=P)
                         ).then_inc(loaded, 16)
            sp.wait_ge(loaded, 96)

        @block.tensor
        def _(pe):
            pe.wait_ge(loaded, 96)

            def chunk(c, first):
                def down(e, k):
                    n = 16 * c + 4 * e + k
                    pe.wait_ge(gelued, n + 1)
                    if k == 0 and not (first and e < 2):
                        pe.wait_ge(yed, 4 * c + e - 1)
                    pe.matmul(ps_y[e % 2][:, 0:TC], w2[:, e, k, :], hid[:, k % 2, :], start=(k == 0), stop=(k == MF - 1)
                              ).then_inc(summed, 1)
                for e in range(ME):
                    m = 4 * c + e
                    if not (first and e < 2):
                        pe.wait_ge(wkept, m - 1)
                    pe.wait_ge(scaled, m + 1)
                    for k in range(MF):
                        n = 16 * c + 4 * e + k
                        if not (first and e == 0 and k < 2):
                            pe.wait_ge(gelued, n - 1)
                        pe.matmul(ps_h[k % 2][:, 0:TC], w1[:, e, k, :], xe[:, e % 2, :], start=True, stop=True
                                  ).then_inc(upped, 1)
                        if k == 0:
                            pe.matmul(ps_w[e % 2][:, 0:TC], g.pick_f1[0:ME, e * P:(e + 1) * P],
                                      gwt[0:ME, bass.ds(c * TC, TC)], start=True, stop=True).then_inc(spread_, 1)
                        if e or k:
                            down(e if k else e - 1, k - 1 if k else MF - 1)
                down(ME - 1, MF - 1)
            chunk(0, True)
            with pe.Fori(1, NC) as c:
                chunk(c, False)

        @block.scalar
        def _(act):
            act.wait_ge(loaded, 96)

            def chunk(c, first):
                for e in range(ME):
                    for k in range(MF):
                        n = 16 * c + 4 * e + k
                        act.wait_ge(upped, n + 1)
                        if not (first and e == 0 and k < 2):
                            act.wait_ge(summed, n - 1)
                        act.activation(hid[:, k % 2, :], ps_h[k % 2][:, 0:TC], ACT.Gelu, bias=b1[:, e, k:k + 1]
                                       ).then_inc(gelued, 1)
            chunk(0, True)
            with act.Fori(1, NC) as c:
                chunk(c, False)

        @block.vector
        def _(dve):
            dve.wait_ge(loaded, 96)

            def scale(c, e, first):
                m = 4 * c + e
                if not (first and e < 2):
                    dve.wait_ge(upped, 4 * (m - 1))
                dve.tensor_scalar(xe[:, e % 2, :], g.xnt[:, bass.ds(c * TC, TC)], lng[:, e:e + 1], lnb[:, e:e + 1],
                                  ALU.mult, ALU.add).then_inc(scaled, 1)

            def chunk(c, first):
                scale(c, 0, first)
                for e in range(ME):
                    m = 4 * c + e
                    if e + 1 < ME:
                        scale(c, e + 1, first)
                    dve.wait_ge(spread_, m + 1)
                    dve.tensor_copy(wb[:, e % 2, :], ps_w[e % 2][:, 0:TC]).then_inc(wkept, 1)
                    dve.wait_ge(wkept, m + 1)
                    dve.wait_ge(summed, 4 * (m + 1))
                    out = g.addt[:, bass.ds(c * TC, TC)]
                    if e == 0:
                        dve.scalar_tensor_tensor(out, ps_y[0][:, 0:TC], b2[:, 0:1], wb[:, 0, :], ALU.add, ALU.mult
                                                 ).then_inc(yed, 1)
                    else:
                        dve.scalar_tensor_tensor(y[:], ps_y[e % 2][:, 0:TC], b2[:, e:e + 1], wb[:, e % 2, :],
                                                 ALU.add, ALU.mult).then_inc(yed, 1)
                        dve.wait_ge(yed, m + 1)
                        dve.tensor_tensor(out, out, y[:], ALU.add).then_inc(added, 1)
            chunk(0, True)
            with dve.Fori(1, NC) as c:
                chunk(c, False)


def mx_linear(nc, g, w_d, b_d):
    with ExitStack() as ctx:
        st = Stage(nc, ctx, "mx")
        w, b = st.sb("w", [P, 1, D]), st.sb("b", [D, 1])
        wt, xt = st.sb("wt", [D, P]), st.sb("xt", [D, T])
        loaded, dved, quantised = st.sem("loaded"), st.sem("dved"), st.sem("quantised")
        turned, kept, made, done = st.sem("turned"), st.sem("kept"), st.sem("made"), st.sem("done")
        ps = [st.ps(f"ps{n}", [P, 512]) for n in range(8)]
        t = [st.sb(f"t{n}", [P, NT, D]) for n in range(4)]
        sc, rs = st.sb("sc", [P, NT * 4]), st.sb("rs", [P, NT * 4])
        block = ctx.enter_context(nc.Block())

        @block.sync
        def _(sp):
            sp.dma_start(w[:, 0, :], w_d).then_inc(loaded, 16)
            with nc.allow_non_contiguous_dma(reason="bias as a column"):
                sp.dma_start(b[:], col(b_d)).then_inc(loaded, 16)
            sp.wait_ge(loaded, 32)

        @block.vector
        def _(dve):
            link = chain(dve, dved)

            def quantise(x, n):
                v = x.rearrange("p t (k c) -> p (t k) c", c=32)
                y, a, r, s = (i[:, 0:n, :].rearrange("p t (k c) -> p (t k) c", c=32) for i in t)
                m = 4 * n
                bc = lambda q: q[:, 0:m].rearrange("p (k o) -> p k o", o=1).broadcast_to([P, m, 32])
                link(dve.tensor_reduce(sc[:, 0:m], v, AX.X, ALU.max, apply_absolute_value=True))
                link(dve.tensor_scalar(sc[:, 0:m], sc[:, 0:m], 1.0 / 7.5, 1e-30, ALU.mult, ALU.max))
                link(dve.reciprocal(rs[:, 0:m], sc[:, 0:m]))
                link(dve.tensor_tensor(y, v, bc(rs), ALU.mult))
                link(dve.scalar_tensor_tensor(a, y, -1.0, y, ALU.mult, ALU.max))
                link(dve.tensor_scalar(r, a, 2.0, -4.0, ALU.is_ge, ALU.mult))
                link(dve.tensor_scalar(a, a, 4.0, -2.0, ALU.is_ge, ALU.mult))
                link(dve.scalar_tensor_tensor(r, r, 8.0, a, ALU.add, ALU.add))
                link(dve.reciprocal(a, r))
                link(dve.tensor_tensor(y, y, r, ALU.mult))
                link(dve.tensor_scalar(s, y, ROUND, None, ALU.add))
                link(dve.tensor_scalar(s, s, -ROUND, None, ALU.add))
                link(dve.tensor_tensor(r, s, y, ALU.subtract))
                link(dve.tensor_scalar(r, r, 0.5, None, ALU.is_ge))
                link(dve.tensor_tensor(s, s, r, ALU.subtract))
                link(dve.tensor_tensor(s, s, a, ALU.mult))
                return s, bc(sc), v

            s, scale, v = quantise(g.xn[:], NT)
            dve.tensor_tensor(v, s, scale, ALU.mult).then_inc(quantised, 1)
            dve.wait_ge(quantised, 1)
            dve.wait_ge(loaded, 32)
            s, scale, v = quantise(w[:], 1)
            dve.tensor_tensor(v, s, scale, ALU.mult).then_inc(quantised, 1)
            for n in range(4):
                a, e = 512 * n, min(512 * n + 512, T)
                dve.wait_ge(turned, n + 1)
                dve.tensor_copy(xt[:, a:e], ps[n][:, 0:e - a]).then_inc(kept, 1)
            dve.wait_ge(turned, 5)
            dve.tensor_copy(wt[:], ps[4][:, 0:P]).then_inc(kept, 1)

        @block.tensor
        def _(pe):
            pe.wait_ge(quantised, 1)
            for n in range(4):
                for q in range(4 * n, min(4 * n + 4, NT)):
                    m = pe.transpose(ps[n][:, (q % 4) * P:(q % 4 + 1) * P], g.xn[:, q, :], g.ident[:])
                m.then_inc(turned, 1)
            pe.wait_ge(quantised, 2)
            pe.transpose(ps[4][:, 0:P], w[:, 0, :], g.ident[:]).then_inc(turned, 1)
            pe.wait_ge(kept, 5)
            for c in range(NC):
                pe.matmul(ps[c][:, 0:TC], wt[:], xt[:, c * TC:(c + 1) * TC], start=True, stop=True).then_inc(made, 1)

        @block.scalar
        def _(act):
            act.wait_ge(loaded, 32)
            for c in range(NC):
                act.wait_ge(made, c + 1)
                act.activation(g.addt[:, c * TC:(c + 1) * TC], ps[c][:, 0:TC], ACT.Identity, bias=b[:, 0:1]
                               ).then_inc(done, 1)


class Globals:
    pass


def build(nc, a, out):
    with ExitStack() as ctx:
        st = Stage(nc, ctx, "g")
        g = Globals()
        g.x, g.xn = st.sb("x", [P, NT, D]), st.sb("xn", [P, NT, D])
        g.xnt, g.addt = st.sb("xnt", [D, T + 2 * PAIR]), st.sb("addt", [D, T])
        g.ident, g.ones, g.tri = st.sb("ident", [P, P]), st.sb("ones", [P, P]), st.sb("tri", [P, P])
        g.hm8, g.hm64, g.iota8 = st.sb("hm8", [P, 16]), st.sb("hm64", [P, 2]), st.sb("iota8", [P, 8])
        g.pick_f0, g.pick_f1, g.pick_f2 = st.sb("pick_f0", [9, 768]), st.sb("pick_f1", [4, 512]), st.sb("pick_f2", [8, 2048])
        g.half = st.sb("half", [P, NT])
        g.zeros = st.sb("zeros", [P, 16])
        ctx_t = nc.dram_tensor("ctx_t", [B, CR, S], F32, kind="Internal").ap()

        constants(nc, g)
        with ExitStack() as c2:
            s2 = Stage(nc, c2, "load")
            loaded = s2.sem("loaded")
            with nc.Block() as block:
                @block.sync
                def _(sp):
                    sp.dma_start(g.x[:], a["x"].rearrange("b l d -> (b l) d").rearrange("(t p) d -> p t d", p=P)
                                 ).then_inc(loaded, 16)
                    sp.wait_ge(loaded, 16)
        context_prep(nc, g, a["ctx_768"], a["mask_BxS2_bf1"], ctx_t)
        renorm(nc, g, "n0", g.x)
        ctx_d = a["ctx_768"]

        def attend(name, **kw):
            attention(nc, g, name, ctx_d, ctx_t, **kw)

        def sub0():
            w = {k: a["L0_xattn_" + k] for k in ("Wq", "bq", "Wkv", "bkv", "Wo", "bo")}
            moves_k, moves_v = [], []
            for h in range(HEADS):
                for part, ls in ((0, moves_k), (1, moves_v)):
                    r0 = 16 * h + 8 * part
                    ls.append((lambda t, h=h: t[8 * h:8 * h + 8, 0, 0:C], w["Wkv"][r0:r0 + 8, :]))
                    ls.append((lambda t, h=h: t[8 * h:8 * h + 8, 0, C:C + 1], col(w["bkv"][r0:r0 + 8])))
            attend("a0", heads=HEADS, kc=1, scale=8.0 ** -0.5,
                   loads=[("wkT", [P, 1, CR], moves_k), ("wvT", [P, 1, CO], moves_v),
                          ("wq", [P, 1, D], [(lambda t: t[:, 0, :], w["Wq"])]),
                          ("wo_raw", [D, P], [(lambda t: t[:], w["Wo"])]), ("wo", [P, 1, D], []),
                          ("bq", [P, 1], [(lambda t: t[:], col(w["bq"]))])],
                   turns=[(lambda t: t["wo_raw"][:], P, D, lambda t: t["wo"][:, 0, :])],
                   masked={"clear": [("wkT", 0.0)], "direct": [("ob", lambda t: t[:], col(w["bo"]))]},
                   q_bias=True, o_bias=True, mask_row=False, vo_direct=False)
            renorm(nc, g, "n1", g.x, g.addt)

        def sub1():
            with ExitStack() as c2:
                s2 = Stage(nc, c2, "f0")
                lg, gw, gwt = s2.sb("lg", [P, NT, 9]), s2.sb("gw", [P, NT, 9]), s2.sb("gwt", [9, T])
                f = {k: a["L0_ffn_" + k] for k in ("gate_w", "dyn_gate_w", "dyn_up_w", "dyn_down_w", "sh_gate_w",
                                                   "sh_up_w", "sh_down_w")}
                logits(nc, g, "f0l", g.xnt, 9, f["gate_w"], None, False, lg[:])
                route_mixer(nc, g, lg, gw)
                turn_weights(nc, g, "f0t", 9, gw, gwt)
                fl = lambda x: x.rearrange("e i d -> (e i) d")
                gated_mlp(nc, g, "f0m", 6,
                          [(0, 0, 4, fl(f["dyn_gate_w"])), (1, 0, 4, fl(f["dyn_up_w"])),
                           (0, 4, 2, fl(f["sh_gate_w"])), (1, 4, 2, fl(f["sh_up_w"]))],
                          [(0, 4, f["dyn_down_w"]), (4, 2, f["sh_down_w"])], g.pick_f0, 9, gwt)
            renorm(nc, g, "n2", g.x, g.addt)

        def sub2():

            w = {k: a["L1_xattn_" + k] for k in ("Wq", "Wk", "Wv", "Wo", "bo")}
            turns = []
            for k in range(8):
                s = slice(k * P, (k + 1) * P)
                turns += [(lambda t, s=s: t["wk_raw"][:, s], P, C, lambda t, k=k: t["wkT"][:, k, 0:C]),
                          (lambda t, s=s: t["wv_raw"][:, s], P, C, lambda t, k=k: t["wvT"][:, k, 0:C]),
                          (lambda t, s=s: t["wq_raw"][:, s], P, D, lambda t, k=k: t["wq"][:, k, :])]
            attend("a1", heads=HEADS, kc=8, scale=64.0 ** -0.5,
                   loads=[("wkT", [P, 8, CR], []), ("wvT", [P, 8, CO], []), ("wq", [P, 8, D], []),
                          ("wk_raw", [C, 1024], [(lambda t: t[:], w["Wk"])]),
                          ("wv_raw", [C, 1024], [(lambda t: t[:], w["Wv"])]),
                          ("wq_raw", [D, 1024], [(lambda t: t[:], w["Wq"])]),
                          ("wo", [P, 8, D], [(lambda t: t[:], w["Wo"].rearrange("(k p) e -> p k e", p=P))])],
                   turns=turns,
                   masked={"clear": [("wkT", 0.0), ("wvT", 0.0), ("cb", 0.0)],
                           "direct": [("ob", lambda t: t[:], col(w["bo"]))]},
                   q_bias=False, o_bias=True, mask_row=False, vo_direct=False)
            renorm(nc, g, "n3", g.x, g.addt)

        def sub3():
            with ExitStack() as c2:
                s2 = Stage(nc, c2, "f1")
                hid, hid_t = s2.sb("hid", [P, NT, D]), s2.sb("hid_t", [D, T])
                lg, gw, gwt, gs = s2.sb("lg", [P, NT, 4]), s2.sb("gw", [P, NT, 4]), s2.sb("gwt", [4, T]), s2.sb("gs", [P, NT])
                copied = s2.sem("copied")
                with nc.Block() as block:
                    @block.vector
                    def _(dve):
                        dve.tensor_copy(hid[:], g.xn[:]).then_inc(copied, 1)
                f = {k: a["L1_ffn_" + k] for k in ("router_w", "router_b", "ln_g", "ln_b", "w1", "b1", "w2", "b2")}
                for m in range(4):
                    if m == 0:
                        renorm(nc, g, f"m{m}n", hid, raw_t=hid_t)
                    else:
                        renorm(nc, g, f"m{m}n", hid, g.addt, scale=gs, raw_t=hid_t)
                    logits(nc, g, f"m{m}l", hid_t, 4, f["router_w"][m], f["router_b"][m], True, lg[:])
                    route_top2(nc, g, f"m{m}r", lg[:], 4, True, gw[:], gs[:])
                    turn_weights(nc, g, f"m{m}t", 4, gw, gwt)
                    moe_layer(nc, g, f"m{m}f", f["w1"][m], f["w2"][m], f["b1"][m], f["b2"][m], f["ln_g"][m], f["ln_b"][m],
                              gwt)
                renorm(nc, g, "m4n", hid, g.addt, scale=gs, raw_t=g.addt, norm=False)
            renorm(nc, g, "n4", g.x, g.addt)

        def sub4():

            w = {k: a["L2_xattn_" + k] for k in ("Wq", "Wk", "Wv", "Wo")}
            attend("a2", heads=HEADS, kc=1, scale=8.0 ** -0.5,
                   loads=[("wkT", [P, 1, CR], []), ("wvT", [P, 1, CO], []), ("wq", [P, 1, D], []),
                          ("wk_raw", [C, P], [(lambda t: t[:], w["Wk"])]),
                          ("wv_raw", [C, P], [(lambda t: t[:], w["Wv"])]),
                          ("wq_raw", [D, P], [(lambda t: t[:], w["Wq"])]),
                          ("wo", [P, 1, D], [(lambda t: t[:, 0, :], w["Wo"])])],
                   turns=[(lambda t: t["wk_raw"][:], P, C, lambda t: t["wkT"][:, 0, 0:C]),
                          (lambda t: t["wv_raw"][:], P, C, lambda t: t["wvT"][:, 0, 0:C]),
                          (lambda t: t["wq_raw"][:], P, D, lambda t: t["wq"][:, 0, :])],
                   masked={"clear": [("wkT", 0.0), ("wvT", 0.0), ("cb", 0.0), ("ob", 0.0)], "direct": []},
                   q_bias=False, o_bias=False, mask_row=True, vo_direct=False)
            renorm(nc, g, "n5", g.x, g.addt)

        def sub5():
            with ExitStack() as c2:
                s2 = Stage(nc, c2, "f2")
                lg, gw, gwt = s2.sb("lg", [P, NT, 8]), s2.sb("gw", [P, NT, 8]), s2.sb("gwt", [8, T])
                f = {k: a["L2_ffn_" + k] for k in ("Wg", "W1", "W2", "W3")}
                logits(nc, g, "f2l", g.xnt, 8, f["Wg"], None, False, lg[:])
                route_top2(nc, g, "f2r", lg[:], 8, False, gw[:], None)
                turn_weights(nc, g, "f2t", 8, gw, gwt)
                fl = lambda x: x.rearrange("e i d -> (e i) d")
                gated_mlp(nc, g, "f2m", 16, [(0, 0, 16, fl(f["W1"])), (1, 0, 16, fl(f["W2"]))], [(0, 16, f["W3"])],
                          g.pick_f2, 8, gwt)
            renorm(nc, g, "n6", g.x, g.addt)

        def sub6():

            w = {k: a["L3_xattn_" + k] for k in ("Wq", "bq", "Wk", "bk", "Wv", "bv")}
            attend("a3", heads=1, kc=1, scale=1.0,
                   loads=[("wkT", [P, 1, CR], [(lambda t: t[:, 0, C:C + 1], col(w["bk"]))]), ("wq", [P, 1, D], []),
                          ("wk_raw", [C, P], [(lambda t: t[:], w["Wk"])]),
                          ("wq_raw", [D, P], [(lambda t: t[:], w["Wq"])]),
                          ("bq", [P, 1], [(lambda t: t[:], col(w["bq"]))])],
                   turns=[(lambda t: t["wk_raw"][:], P, C, lambda t: t["wkT"][:, 0, 0:C]),
                          (lambda t: t["wq_raw"][:], P, D, lambda t: t["wq"][:, 0, :])],
                   masked={"clear": [("wkT", 0.0), ("ob", 0.0)],
                           "direct": [("vo", lambda t: t[0:C, 0, :], w["Wv"]),
                                      ("vo", lambda t: t[C:CO, 0, :], w["bv"].rearrange("(o e) -> o e", o=1))]},
                   q_bias=True, o_bias=False, mask_row=False, vo_direct=True)
            renorm(nc, g, "n7", g.x, g.addt)

        def sub7():
            mx_linear(nc, g, a["L3_ffn_weight"], a["L3_ffn_bias"])
            renorm(nc, g, "n8", g.x, g.addt, norm=False)

        for k, sub in enumerate((sub0, sub1, sub2, sub3, sub4, sub5, sub6, sub7)):
            if ONLY is None or k in ONLY:
                sub()
        with ExitStack() as c2:
            s2 = Stage(nc, c2, "store")
            stored = s2.sem("stored")
            with nc.Block() as block:
                @block.sync
                def _(sp):
                    sp.dma_start(out.rearrange("b l d -> (b l) d").rearrange("(t p) d -> p t d", p=P), g.x[:]
                                 ).then_inc(stored, 16)
                    sp.wait_ge(stored, 16)


_INS = ["x", "ctx_768", "mask_BxS2_bf1", "L0_xattn_Wq", "L0_xattn_bq", "L0_xattn_Wkv", "L0_xattn_bkv", "L0_xattn_Wo",
        "L0_xattn_bo", "L0_ffn_gate_w", "L0_ffn_dyn_gate_w", "L0_ffn_dyn_up_w", "L0_ffn_dyn_down_w",
        "L0_ffn_sh_gate_w", "L0_ffn_sh_up_w", "L0_ffn_sh_down_w", "L1_xattn_Wq", "L1_xattn_Wk", "L1_xattn_Wv",
        "L1_xattn_Wo", "L1_xattn_bo", "L1_ffn_router_w", "L1_ffn_router_b", "L1_ffn_ln_g", "L1_ffn_ln_b", "L1_ffn_w1",
        "L1_ffn_b1", "L1_ffn_w2", "L1_ffn_b2", "L2_xattn_Wq", "L2_xattn_Wk", "L2_xattn_Wv", "L2_xattn_Wo",
        "L2_ffn_Wg", "L2_ffn_W1", "L2_ffn_W2", "L2_ffn_W3", "L3_xattn_Wq", "L3_xattn_bq", "L3_xattn_Wk",
        "L3_xattn_bk", "L3_xattn_Wv", "L3_xattn_bv", "L3_ffn_weight", "L3_ffn_bias"]


def kernel(**inputs):
    import numpy as _np
    import concourse.bacc as _bacc
    from concourse import mybir as _mybir
    from concourse.bass_utils import run_bass_kernel_spmd as _run

    nc = _bacc.Bacc("TRN2", target_bir_lowering=False, num_devices=1)
    arrays, args = {}, {}
    for name in _INS:
        a = _np.ascontiguousarray(inputs[name])
        if a.dtype.kind == "b":
            a = a.view(_np.uint8)
        arrays[f"in_{name}"] = a
        args[name] = nc.dram_tensor(f"in_{name}", a.shape, _mybir.dt.from_np(a.dtype), kind="ExternalInput").ap()
    out = nc.dram_tensor("out_0", (B, L, D), F32, kind="ExternalOutput").ap()
    build(nc, args, out)
    r = _run(nc, [arrays], core_ids=[0])
    return r.results[0]["out_0"]
```

```python
from contextlib import ExitStack

import concourse.bass as bass
from concourse import mybir

F32 = mybir.dt.float32
F32R = mybir.dt.float32r
U8 = mybir.dt.uint8
U32 = mybir.dt.uint32
ALU = mybir.AluOpType
ACT = mybir.ActivationFunctionType
AX = mybir.AxisListType

P = 128
D = 128
B, L = 32, 56
S, C = 1500, 96
T = B * L
NT = T // P
KT, NK = 12, 125
BANKS, BK = 3, 500
GT = KT // BANKS
CR = C + 2
CO = C + 1
PAIR = 2 * L
NP = B // 2
TC = 448
NC = T // TC
BIG = 1.5 * 2.0 ** 127
EPS = 1e-5
HEADS = 16
CAP = 280
ONLY = None
ROUND = 12582912.0


class Stage:

    def __init__(self, nc, ctx, name):
        self.nc, self.ctx, self.name, self.sems = nc, ctx, name, []
        ctx.callback(self.release)

    def release(self):
        if self.sems:
            self.nc.clear_and_free_semaphores(self.sems)
            self.nc.all_engine_barrier()

    def sb(self, name, shape, dt=F32):
        return self.ctx.enter_context(self.nc.sbuf_tensor(f"{self.name}_{name}", shape, dt))

    def ps(self, name, shape):
        return self.ctx.enter_context(self.nc.psum_tensor(f"{self.name}_{name}", shape, F32))

    def sem(self, name):
        self.sems.append(self.nc.alloc_semaphore(f"{self.name}_{name}"))
        return self.sems[-1]


def chain(eng, sem):
    count = [0]

    def link(ins):
        count[0] += 1
        ins.then_inc(sem, 1)
        eng.wait_ge(sem, count[0])

    return link


def constants(nc, g):
    with ExitStack() as ctx:
        st = Stage(nc, ctx, "const")
        cleared, dved = st.sem("cleared"), st.sem("dve")
        block = ctx.enter_context(nc.Block())

        @block.vector
        def _(dve):
            link = chain(dve, dved)
            link(dve.memset(g.ones[:], 1.0))
            link(dve.memset(g.zeros[:], 0.0))
            link(dve.memset(g.xnt[:, T:T + 2 * PAIR], 0.0))
            link(dve.memset(g.half[:], -0.5))

        @block.gpsimd
        def _(pool):
            pool.memset(g.ident[:], 0.0).then_inc(cleared, 1)
            pool.memset(g.tri[:], 1.0).then_inc(cleared, 1)
            pool.memset(g.hm8[:], 1.0).then_inc(cleared, 1)
            pool.memset(g.hm64[:], 1.0).then_inc(cleared, 1)
            picks = ((g.pick_f0, 12, 64), (g.pick_f1, ME, 128), (g.pick_f2, 8, 256))
            for tile, _, _ in picks:
                pool.memset(tile[:], 1.0).then_inc(cleared, 1)
            pool.iota(g.iota8[:], [[1, 8]], base=0, channel_multiplier=0,
                      allow_small_or_imprecise_dtypes=True).then_inc(cleared, 1)
            pool.wait_ge(cleared, 8)
            pool.affine_select(out=g.ident[:], in_=g.ident[:], compare_op=ALU.not_equal, fill=1.0, base=0,
                               pattern=[[-1, P]], channel_multiplier=1).then_inc(cleared, 1)
            pool.affine_select(out=g.tri[:], in_=g.tri[:], compare_op=ALU.is_ge, fill=0.0, base=0,
                               pattern=[[1, P]], channel_multiplier=-1).then_inc(cleared, 1)

            def band(tile, cols, width, n):
                pool.affine_select(out=tile, in_=tile, compare_op=ALU.is_ge, fill=0.0, base=0,
                                   pattern=[[-width, cols]], channel_multiplier=1).then_inc(cleared, 1)
                pool.wait_ge(cleared, n + 1)
                pool.affine_select(out=tile, in_=tile, compare_op=ALU.is_ge, fill=0.0, base=width - 1,
                                   pattern=[[width, cols]], channel_multiplier=-1).then_inc(cleared, 1)

            band(g.hm8[:], 16, 8, 10)
            band(g.hm64[:], 2, 64, 12)
            for tile, cols, width in picks:
                v = tile[:].rearrange("e (c w) -> e c w", w=width)
                pool.affine_select(out=v, in_=v, compare_op=ALU.is_equal, fill=0.0, base=0,
                                   pattern=[[-1, cols], [0, width]], channel_multiplier=1).then_inc(cleared, 1)
            pool.wait_ge(cleared, 17)
            pool.tensor_copy(g.pick_f0[:, 9 * 64:12 * 64].rearrange("e (c w) -> e c w", w=64),
                             g.pick_f0[:, 8 * 64:9 * 64].rearrange("e (c w) -> e c w", c=1).broadcast_to([9, 3, 64])
                             ).then_inc(cleared, 1)
            pool.wait_ge(cleared, 18)


def context_prep(nc, g, ctx_d, mask_d, ctx_t):
    with ExitStack() as ctx:
        st = Stage(nc, ctx, "cprep")
        nat = st.sb("nat", [NK, 2, KT, C])
        tr = st.sb("tr", [CO, 2, S])
        mask8, maskf = st.sb("mask8", [B, S], U8), st.sb("maskf", [B, S])
        ps = [st.ps(f"ps{n}", [P, 512]) for n in range(6)]
        loaded = [st.sem(f"loaded{n}") for n in range(2)]
        stored = [st.sem(f"stored{n}") for n in range(2)]
        mask_in, mask_done, mask_out = st.sem("mask_in"), st.sem("mask_done"), st.sem("mask_out")
        turned, kept, ones = st.sem("turned"), st.sem("kept"), st.sem("ones")
        block = ctx.enter_context(nc.Block())
        ctx_v = ctx_d.rearrange("b (p t) c -> p b (t c)", t=KT)

        @block.sync
        def _(sp):
            sp.dma_start(mask8[:], mask_d).then_inc(mask_in, 16)
            for h in range(2):
                sp.dma_start(nat[:, h, :, :].rearrange("p t c -> p (t c)"), ctx_v[:, h, :]).then_inc(loaded[h], 16)
            sp.wait_ge(mask_done, 2)
            sp.dma_start(ctx_t[:, C + 1, :], maskf[:]).then_inc(mask_out, 16)

            with sp.Fori(1, NP) as i:
                for h in range(2):
                    sp.wait_ge(turned, 6 * i - 3 + 3 * h - 0)
                    sp.dma_start(nat[:, h, :, :].rearrange("p t c -> p (t c)"),
                                 ctx_v[:, bass.ds(2 * i + h, 1), :].rearrange("p o c -> p (o c)")
                                 ).then_inc(loaded[h], 16)
            sp.wait_ge(mask_out, 16)

        @block.tensor
        def _(pe):
            def pair(i, first):
                for h in range(2):
                    pe.wait_ge(loaded[h], 16 * (i + 1))
                    for k in range(BANKS):
                        if not first:
                            pe.wait_ge(kept, 6 * i + 3 * h + k - 5)
                        for q in range(GT):
                            m = pe.transpose(ps[3 * h + k][0:C, q * NK:(q + 1) * NK], nat[:, h, k * GT + q, :],
                                             g.ident[0:NK, 0:NK])
                        m.then_inc(turned, 1)
            pair(0, True)
            with pe.Fori(1, NP) as i:
                pair(i, False)

        @block.vector
        def _(dve):
            dve.memset(tr[C:C + 1, :, :], 1.0).then_inc(ones, 1)
            dve.wait_ge(mask_in, 16)
            dve.tensor_scalar(maskf[:].rearrange("b (t p) -> b t p", t=KT),
                              mask8[:].rearrange("b (p t) -> b t p", t=KT), -1.0, None, ALU.add
                              ).then_inc(mask_done, 1)
            dve.wait_ge(mask_done, 1)
            dve.tensor_scalar(maskf[:], maskf[:], BIG, None, ALU.mult).then_inc(mask_done, 1)

            def pair(i, first):
                for h in range(2):
                    for k in range(BANKS):
                        dve.wait_ge(turned, 6 * i + 3 * h + k + 1)
                        if not first and k == 0:
                            dve.wait_ge(stored[h], 16 * i)
                        dve.tensor_copy(tr[0:C, h, k * BK:(k + 1) * BK], ps[3 * h + k][0:C, 0:BK]).then_inc(kept, 1)
            pair(0, True)
            with dve.Fori(1, NP) as i:
                pair(i, False)

        @block.scalar
        def _(act):
            act.wait_ge(ones, 1)
            with act.Fori(0, NP) as i:
                for h in range(2):
                    act.wait_ge(kept, 6 * i + 3 * h + 3)
                    act.dma_start(ctx_t[bass.ds(2 * i + h, 1), 0:CO, :].rearrange("o r s -> (o r) s"), tr[:, h, :]
                                  ).then_inc(stored[h], 16)
            for h in range(2):
                act.wait_ge(stored[h], 16 * NP)


def renorm(nc, g, name, base, addt=None, scale=None, raw_t=None, norm=True):
    with ExitStack() as ctx:
        st = Stage(nc, ctx, name)
        xc, sq = g.xn, st.sb("sq", [P, NT, D])
        mu, var, rstd = st.sb("mu", [P, NT]), st.sb("var", [P, NT]), st.sb("rstd", [P, NT])
        psa = [st.ps(f"psa{n}", [P, 4, P]) for n in range(4)]
        psb = [st.ps(f"psb{n}", [P, 4, P]) for n in range(4)]
        turned, based, raw_turned, dved = st.sem("turned"), st.sem("based"), st.sem("raw_turned"), st.sem("dved")
        raw_kept, powed, back, varred, normed = (st.sem(x) for x in ("raw_kept", "powed", "back", "varred", "normed"))
        kept = st.sem("kept")
        groups = [(n, 4 * n, min(4 * n + 4, NT)) for n in range(4)]
        block = ctx.enter_context(nc.Block())

        def bc(x, a, b):
            return x[:, a:b].rearrange("p (t o) -> p t o", o=1).broadcast_to([P, b - a, D])

        @block.tensor
        def _(pe):
            for n, a, b in groups if addt is not None else ():
                for t in range(a, b):
                    m = pe.transpose(psa[n][:, t - a, :], addt[:, t * P:(t + 1) * P], g.ident[:])
                m.then_inc(turned, 1)
            for n, a, b in groups if raw_t is not None else ():
                if addt is not None:
                    pe.wait_ge(based, n + 1)
                for t in range(a, b):
                    m = pe.transpose(psb[n][:, t - a, :], base[:, t, :], g.ident[:])
                m.then_inc(raw_turned, 1)
            for n, a, b in groups if norm else ():
                pe.wait_ge(normed, n + 1)
                if raw_t is not None:
                    pe.wait_ge(raw_kept, n + 1)
                for t in range(a, b):
                    m = pe.transpose(psb[n][:, t - a, :], g.xn[:, t, :], g.ident[:])
                m.then_inc(back, 1)

        @block.vector
        def _(dve):
            link = chain(dve, dved)
            for n, a, b in groups:
                v = base[:, a:b, :]
                if scale is not None:
                    link(dve.tensor_tensor(v, v, bc(scale, a, b), ALU.mult))
                if addt is not None:
                    dve.wait_ge(turned, n + 1)
                    dve.tensor_tensor(v, v, psa[n][:, 0:b - a, :], ALU.add).then_inc(based, 1)
                    dve.wait_ge(based, n + 1)
                if norm:
                    link(dve.tensor_reduce(mu[:, a:b], v, AX.X, ALU.add))
                    link(dve.tensor_scalar(mu[:, a:b], mu[:, a:b], 1.0 / D, None, ALU.mult))
                    link(dve.tensor_tensor(xc[:, a:b, :], v, bc(mu, a, b), ALU.subtract))
                    link(dve.tensor_tensor(sq[:, a:b, :], xc[:, a:b, :], xc[:, a:b, :], ALU.mult))
                    link(dve.tensor_reduce(var[:, a:b], sq[:, a:b, :], AX.X, ALU.add))
                    dve.tensor_scalar(var[:, a:b], var[:, a:b], 1.0 / D, EPS, ALU.mult, ALU.add).then_inc(varred, 1)
            for n, a, b in groups if norm else ():
                dve.wait_ge(powed, n + 1)
                dve.tensor_tensor(g.xn[:, a:b, :], xc[:, a:b, :], bc(rstd, a, b), ALU.mult).then_inc(normed, 1)

        @block.gpsimd
        def _(pool):
            for n, a, b in groups if norm else ():
                pool.wait_ge(varred, n + 1)
                pool.tensor_tensor(rstd[:, a:b], var[:, a:b], g.half[:, a:b], ALU.pow).then_inc(powed, 1)

        @block.scalar
        def _(act):
            for n, a, b in groups if raw_t is not None else ():
                act.wait_ge(raw_turned, n + 1)
                act.activation(raw_t[:, a * P:b * P].rearrange("p (t c) -> p t c", c=P), psb[n][:, 0:b - a, :],
                               ACT.Copy).then_inc(raw_kept, 1)
            for n, a, b in groups if norm else ():
                act.wait_ge(back, n + 1)
                act.activation(g.xnt[:, a * P:b * P].rearrange("p (t c) -> p t c", c=P), psb[n][:, 0:b - a, :],
                               ACT.Copy).then_inc(kept, 1)


def attend_by_values(nc, g, name, ctx_t, a_w, cb, ob, wv, wo4):
    nu, seq = 2 * HEADS * L // P, HEADS * L // P
    quads, dims = 4, P // HEADS
    qr, qd = HEADS * L // quads, P // quads
    total = nu * NP
    hq = TC // PAIR
    nq = HEADS // hq
    ends = [-(-qr * (x + 1) // P) - 1 for x in range(quads)]
    with ExitStack() as ctx:
        st = Stage(nc, ctx, name + "m")
        raw = st.sb("raw", [CR, 2, S])
        cxt = st.sb("cxt", [CR, 2, 2, S], F32R)
        vals = st.sb("vals", [NK, 2, KT, P])
        q32 = st.sb("q32", [CR, TC])
        qhi, qlo = (st.sb(n, [CR, 2, HEADS * L], F32R) for n in ("qhi", "qlo"))
        prob, prob_n = st.sb("prob", [P, 2, S]), st.sb("prob_n", [P, 2, S])
        prob_t = st.sb("prob_t", [NK, KT, HEADS * L])
        bank_max, neg_max = st.sb("bank_max", [P, 2, BANKS]), st.sb("neg_max", [P, 2])
        bank_den, den, rec = st.sb("bank_den", [P, 2, BANKS]), st.sb("den", [P, 2]), st.sb("rec", [P, 2])
        own = st.sb("own", [P, quads])
        picked = st.sb("picked", [P, 2, qr])
        av = st.sb("av", [P, quads, 2, L])
        ps_s = st.ps("ps_s", [P, BANKS, 512])
        ps_t = [st.ps(f"ps_t{n}", [P, 512]) for n in range(2)]
        ps_o, ps_v, ps_q = st.ps("ps_o", [P, 512]), st.ps("ps_v", [P, 512]), st.ps("ps_q", [P, 512])
        ctxt_in = [st.sem(f"ctxt_in{h}") for h in range(2)]
        high_made = [st.sem(f"high_made{h}") for h in range(2)]
        low_made = [st.sem(f"low_made{h}") for h in range(2)]
        (own_made, scored, bank_maxed, maxed, exped, summed_up, inverted, scaled_pool, scaled_act, turned, kept_dve,
         kept_act, summed, picked_out, av_made, v_made, v_kept, q_made, q_added, q_kept, projected, out_kept) = (
            st.sem(x) for x in (
                "own_made", "scored", "bank_maxed", "maxed", "exped", "summed_up", "inverted", "scaled_pool",
                "scaled_act", "turned", "kept_dve", "kept_act", "summed", "picked_out", "av_made", "v_made", "v_kept",
                "q_made", "q_added", "q_kept", "projected", "out_kept"))
        block = ctx.enter_context(nc.Block())

        def steps(eng, step):
            for u in range(nu):
                step(0, u)
            with eng.Fori(1, NP) as i:
                for u in range(nu):
                    step(i, u)
            for u in range(4):
                step(NP, u)

        def live(i, u, lag):
            return not isinstance(i, int) or 0 <= nu * i + u - lag < total

        def later(i, u, lag):
            return not isinstance(i, int) or nu * i + u - lag > 0

        def quad_after(u):
            return ends.index(u % seq) if u % seq in ends else None

        def quads_before(i, u, n):
            return quads * (2 * i + u // seq) + n

        def free_rows(eng, i, u):
            if not isinstance(i, int) or nu * i + u >= seq:
                last = (u % seq * P + P - 1) // qr
                eng.wait_ge(summed, quads * (2 * i + u // seq - 1) + last + 1)

        def values_due(u):
            return (u // 4, u % 4) if u < 8 and u % 4 < BANKS else None

        @block.sync
        def _(sp):
            sp.wait_ge(own_made, 1)

            def load(i, first):
                for h in range(2):
                    if not first:
                        sp.wait_ge(low_made[h], i)
                        sp.wait_ge(v_made, 2 * BANKS * i - BANKS * (1 - h))
                    sp.dma_start(raw[:, h, :], ctx_t[bass.ds(2 * i + h, 1), :, :].rearrange("o r s -> (o r) s")
                                 ).then_inc(ctxt_in[h], 16)
            load(0, True)
            with sp.Fori(1, NP) as i:
                load(i, False)
            for h in range(2):
                sp.wait_ge(ctxt_in[h], 16 * NP)

        @block.gpsimd
        def _(pool):
            def split(i, h, first):
                pool.wait_ge(ctxt_in[h], 16 * (i + 1))
                if not first:
                    pool.wait_ge(scored, BANKS * (nu * i - seq * (1 - h)))
                pool.tensor_tensor(cxt[:, h, 0, :], raw[:, h, :], g.zeros[0:CR, 0:1].broadcast_to([CR, S]), ALU.add
                                   ).then_inc(high_made[h], 1)
                pool.wait_ge(high_made[h], i + 1)
                pool.tensor_tensor(cxt[:, h, 1, :], raw[:, h, :], cxt[:, h, 0, :].bitcast(F32), ALU.subtract
                                   ).then_inc(low_made[h], 1)

            def pair(i, first, last):
                for u in range(nu):
                    v = nu * i + u
                    s = u % 2
                    pool.wait_ge(inverted, v + 1)
                    if later(i, u, 1):
                        pool.wait_ge(turned, BANKS * (v - 1))
                    w = (BANKS - 1) * BK
                    pool.tensor_tensor(prob_n[:, s, 0:w], prob[:, s, 0:w], rec[:, s:s + 1].broadcast_to([P, w]),
                                       ALU.mult).then_inc(scaled_pool, 1)
                    if u == 1:
                        split(i, 1, first)
                    if u == seq and not last:
                        split(i + 1, 0, False)
            split(0, 0, True)
            pair(0, True, False)
            with pool.Fori(1, NP - 1) as i:
                pair(i, False, False)
            pair(NP - 1, False, True)

        @block.tensor
        def _(pe):
            def queries(i, q):
                n = nq * i + q
                if not isinstance(n, int) or n > 0:
                    pe.wait_ge(q_kept, n)
                if q == 0 and (not isinstance(i, int) or i > 1):
                    pe.wait_ge(out_kept, i - 1)
                for h in range(hq):
                    m = pe.matmul(ps_q[0:CR, h * PAIR:(h + 1) * PAIR], a_w[:, q * hq + h, :],
                                  g.xnt[:, bass.ds(i * PAIR, PAIR)], start=True, stop=True)
                m.then_inc(q_made, 1)

            def scores(i, u):
                v, h = nu * i + u, u // seq
                if u % seq == 0:
                    pe.wait_ge(low_made[h], i + 1)
                if u == 0:
                    pe.wait_ge(q_kept, nq * (i + 1))
                rows = slice((u % seq) * P, (u % seq + 1) * P)
                for k in range(BANKS):
                    if later(i, u, 0):
                        pe.wait_ge(exped, BANKS * (v - 1) + k + 1)
                    keys = slice(k * BK, (k + 1) * BK)
                    for part, w in ((qhi, 0), (qhi, 1), (qlo, 0)):
                        m = pe.matmul(ps_s[:, k, 0:BK], part[:, h, rows], cxt[:, h, w, keys],
                                      start=(part is qhi and w == 0), stop=(part is qlo))
                    m.then_inc(scored, 1)

            def values(i, h, k):
                n = 2 * BANKS * i + BANKS * h + k
                pe.wait_ge(ctxt_in[h], 16 * (i + 1))
                if not isinstance(n, int) or n > 0:
                    pe.wait_ge(v_kept, n)
                for q in range(GT):
                    t = k * GT + q
                    m = pe.matmul(ps_v[0:NK, q * P:(q + 1) * P], raw[0:CO, h, t * NK:(t + 1) * NK], wv[:],
                                  start=True, stop=True)
                m.then_inc(v_made, 1)

            def turn(i, u, k):
                v = nu * i + u
                if k == 0:
                    pe.wait_ge(scaled_pool, v + 1)
                if k == BANKS - 1:
                    pe.wait_ge(scaled_act, v + 1)
                if k < 2:
                    if later(i, u, 0):
                        pe.wait_ge(*((kept_dve, 2 * v) if k == 0 else (kept_act, v)))
                else:
                    pe.wait_ge(kept_dve, 2 * v + 1)
                for q in range(GT):
                    t = k * GT + q
                    m = pe.transpose(ps_t[(BANKS * u + k) % 2][0:NK, q * P:(q + 1) * P],
                                     prob_n[:, u % 2, t * NK:(t + 1) * NK], g.ident[:])
                m.then_inc(turned, 1)

            def sums(i, u, n):
                v, h = nu * i + u, u % nu // seq
                pe.wait_ge(kept_dve, 2 * v + 2)
                pe.wait_ge(kept_act, v + 1)
                if n == 0:
                    pe.wait_ge(v_kept, 2 * BANKS * i + BANKS * (u // seq + 1))
                done = quads_before(i, u, n)
                if not isinstance(done, int) or done > 0:
                    pe.wait_ge(picked_out, done)
                for k in range(BANKS):
                    for q in range(GT):
                        at = slice(q * qd, (q + 1) * qd)
                        m = pe.matmul(ps_o[at, 0:qr],
                                      vals[:, h, k * GT + q, n * qd:(n + 1) * qd],
                                      prob_t[:, k * GT + q, n * qr:(n + 1) * qr],
                                      start=(k == 0), stop=(k == BANKS - 1), tile_position=(0, q * qd))
                m.then_inc(summed, 1)

            def project(i):
                pe.wait_ge(av_made, 2 * quads * (i + 1))
                n = nq * (i + 2)
                pe.wait_ge(q_kept, min(n, nq * (NP + 1)) if isinstance(i, int) else n)
                for n in range(quads):
                    m = pe.matmul(ps_q[:, 0:PAIR], wo4[:, n, :], av[:, n, :, :], start=(n == 0), stop=(n == quads - 1))
                m.then_inc(projected, 1)

            def step(i, u):
                if live(i, u, 0):
                    scores(i, u)
                if live(i, u, 2):
                    turn(i, u - 2, 0)
                    turn(i, u - 2, 1)
                if (u - 4) % nu == nu - 1 and live(i, u, 4):
                    project(i + (u - 4) // nu)
                if live(i, u, 0) and values_due(u):
                    values(i, *values_due(u))
                if live(i, u, 0) and u == nu - 1:
                    for q in range(nq):
                        queries(i + 1, q)
                if live(i, u, 3) and quad_after(u - 3) is not None:
                    sums(i, u - 3, quad_after(u - 3))
                if live(i, u, 2):
                    turn(i, u - 2, 2)

            for q in range(nq):
                queries(0, q)
            steps(pe, step)

        @block.vector
        def _(dve):
            def queries(i):
                for q in range(nq):
                    n = nq * i + q
                    src = ps_q[0:CR, 0:hq * PAIR].rearrange("p (h b l) -> p b h l", h=hq, b=2)
                    mid = q32[:, 0:hq * PAIR].rearrange("p (b h l) -> p b h l", b=2, h=hq)
                    bias = cb[:, q * hq:(q + 1) * hq].rearrange("p (b h l) -> p b h l", b=1, l=1)
                    dve.wait_ge(q_made, n + 1)
                    dve.tensor_tensor(mid, src, bias.broadcast_to([CR, 2, hq, L]), ALU.add).then_inc(q_added, 1)
                    cols = slice(q * hq * L, (q + 1) * hq * L)
                    flat = q32[:, 0:hq * PAIR].rearrange("p (b c) -> p b c", b=2)
                    dve.wait_ge(q_added, 2 * n + 1)
                    dve.tensor_copy(qhi[:, :, cols], flat).then_inc(q_added, 1)
                    dve.wait_ge(q_added, 2 * (n + 1))
                    dve.tensor_tensor(qlo[:, :, cols], flat, qhi[:, :, cols].bitcast(F32), ALU.subtract
                                      ).then_inc(q_kept, 1)

            def maxima(i, u):
                s = u % 2
                v = nu * i + u
                for k in range(BANKS):
                    dve.wait_ge(scored, BANKS * v + k + 1)
                    dve.tensor_reduce(bank_max[:, s, k:k + 1], ps_s[:, k, 0:BK], AX.X, ALU.max).then_inc(bank_maxed, 1)
                dve.wait_ge(bank_maxed, BANKS * (v + 1))
                dve.tensor_reduce(neg_max[:, s:s + 1], bank_max[:, s, :], AX.X, ALU.max, negate=True
                                  ).then_inc(maxed, 1)

            def keep(i, u, k):
                v = nu * i + u
                dve.wait_ge(turned, BANKS * v + k + 1)
                free_rows(dve, i, u)
                at = u % seq * P
                dve.tensor_copy(prob_t[:, k * GT:(k + 1) * GT, at:at + P],
                                ps_t[(BANKS * u + k) % 2][0:NK, :].rearrange("p (t r) -> p t r", t=GT)
                                ).then_inc(kept_dve, 1)

            def invert(i, u):
                s = u % 2
                v = nu * i + u
                dve.wait_ge(exped, BANKS * (v + 1))
                dve.tensor_reduce(den[:, s:s + 1], bank_den[:, s, :], AX.X, ALU.add).then_inc(summed_up, 1)
                dve.wait_ge(summed_up, v + 1)
                if later(i, u, 1):
                    dve.wait_ge(scaled_pool, v - 1)
                    dve.wait_ge(scaled_act, v - 1)
                dve.reciprocal(rec[:, s:s + 1], den[:, s:s + 1]).then_inc(inverted, 1)

            def pick(i, u, n):
                done = quads_before(i, u, n)
                h = u % nu // seq
                dve.wait_ge(summed, done + 1)
                dve.tensor_tensor(picked[:, n % 2, :].rearrange("p (h q) -> p h q", h=quads),
                                  ps_o[:, 0:qr].rearrange("p (h q) -> p h q", h=quads),
                                  own[:].rearrange("p (h o) -> p h o", o=1).broadcast_to([P, quads, L]), ALU.mult
                                  ).then_inc(picked_out, 1)
                dve.wait_ge(picked_out, done + 1)
                if n == 0 and h == 0 and (not isinstance(i, int) or i > 0):
                    dve.wait_ge(projected, i)
                dve.tensor_reduce(av[:, n, h, :], picked[:, n % 2, :].rearrange("p (h q) -> p q h", h=quads), AX.X,
                                  ALU.add).then_inc(av_made, 1)

            def step(i, u):
                if live(i, u, 0):
                    maxima(i, u)
                if live(i, u, 2):
                    keep(i, u - 2, 0)
                    keep(i, u - 2, 1)
                if live(i, u, 0):
                    invert(i, u)
                if live(i, u, 0) and u == nu - 1:
                    queries(i + 1)
                if live(i, u, 3) and quad_after(u - 3) is not None:
                    pick(i, u - 3, quad_after(u - 3))

            dve.tensor_reduce(own[:], g.hm8[:].rearrange("p (j h) -> p h j", h=quads), AX.X, ALU.add
                              ).then_inc(own_made, 1)
            dve.wait_ge(own_made, 1)
            queries(0)
            steps(dve, step)

        @block.scalar
        def _(act):
            def exps(i, u):
                s = u % 2
                v = nu * i + u
                act.wait_ge(maxed, v + 1)
                if later(i, u, 1):
                    act.wait_ge(scaled_pool, v - 1)
                    act.wait_ge(scaled_act, v - 1)
                for k in range(BANKS):
                    act.activation(prob[:, s, k * BK:(k + 1) * BK], ps_s[:, k, 0:BK], ACT.Exp,
                                   bias=neg_max[:, s:s + 1], accum_out=bank_den[:, s, k:k + 1]).then_inc(exped, 1)

            def scale(i, u):
                s = u % 2
                v = nu * i + u
                act.wait_ge(inverted, v + 1)
                if later(i, u, 1):
                    act.wait_ge(turned, BANKS * (v - 1))
                w = (BANKS - 1) * BK
                act.activation(prob_n[:, s, w:S], prob[:, s, w:S], ACT.Copy, scale=rec[:, s:s + 1]
                               ).then_inc(scaled_act, 1)

            def keep(i, u):
                v = nu * i + u
                act.wait_ge(turned, BANKS * (v + 1))
                free_rows(act, i, u)
                at = u % seq * P
                act.activation(prob_t[:, 2 * GT:KT, at:at + P],
                               ps_t[(BANKS * u + 2) % 2][0:NK, :].rearrange("p (t r) -> p t r", t=GT),
                               ACT.Copy).then_inc(kept_act, 1)

            def keep_values(i, h, k):
                act.wait_ge(v_made, 2 * BANKS * i + BANKS * h + k + 1)
                if not isinstance(i, int) or i > 0:
                    act.wait_ge(summed, 2 * quads * i - quads * (1 - h))
                act.activation(vals[:, h, k * GT:(k + 1) * GT, :],
                               ps_v[0:NK, :].rearrange("p (t r) -> p t r", t=GT), ACT.Copy).then_inc(v_kept, 1)

            def out(i):
                act.wait_ge(projected, i + 1)
                act.activation(g.addt[:, bass.ds(i * PAIR, PAIR)], ps_q[:, 0:PAIR], ACT.Identity,
                               bias=ob[:, 0:1]).then_inc(out_kept, 1)

            def step(i, u):
                if live(i, u, 0):
                    exps(i, u)
                if (u - 4) % nu == nu - 1 and live(i, u, 4):
                    out(i + (u - 4) // nu)
                if live(i, u, 0) and values_due(u):
                    keep_values(i, *values_due(u))
                if live(i, u, 1):
                    scale(i, u - 1)
                if live(i, u, 2):
                    keep(i, u - 2)
            steps(act, step)


def attention(nc, g, name, ctx_d, ctx_t, heads, kc, scale, loads, turns, masked, q_bias, o_bias, mask_row, vo_direct):
    hc = heads // kc
    by_values = heads == HEADS and kc == 1
    with ExitStack() as outer:
        so = Stage(nc, outer, name)
        a_w = so.sb("a", [P, heads, CR])
        if by_values:
            wv = so.sb("wv", [CO, P])
            wo4 = so.sb("wo4", [P, 4, D])
        else:
            vo = so.sb("vo", [CO, heads, D])
        cb = so.sb("cb", [CR, heads])
        ob = so.sb("ob", [P, 1])

        with ExitStack() as ctx:
            st = Stage(nc, ctx, name + "w")
            buf = {n: st.sb(n, shape) for n, shape, _ in loads}
            wkm, wvm = st.sb("wkm", [P, heads, CR]), st.sb("wvm", [P, heads, CO])
            ps = [st.ps(f"ps{n}", [P, 512]) for n in range(8)]
            cleared, loaded, made, kept, mixed = (st.sem(x) for x in ("cleared", "loaded", "made", "kept", "masked"))
            tile = dict(buf, wkm=wkm, wvm=wvm, a=a_w, cb=cb, ob=ob)
            if by_values:
                rep = st.sb("rep", [P, 4, 4, P // 4])
            else:
                tile["vo"] = vo
            clears = [(tile[n][:], v) for n, v in masked["clear"]]
            if mask_row:
                clears += [(cb[C:CR, :], 1.0), (cb[C:CO, :], 0.0)]
            moves = [(tile[n], f, src) for n, _, ls in loads for f, src in ls]
            moves += [(tile[n], f, src) for n, f, src in masked["direct"]]
            jobs = [(lambda s=s: s(tile), None, w, n, lambda d=d: d(tile), 1.0) for s, w, n, d in turns]
            nturn = len(jobs)
            hg = min(hc, 5 if hc < 5 else 4)
            for k in range(kc):
                for h0 in range(0, hc, hg):
                    a, b = k * hc + h0, k * hc + h0 + hg
                    jobs.append((lambda k=k: tile["wq"][:, k, :], lambda a=a, b=b: wkm[:, a:b, :], D, hg * CR,
                                 lambda a=a, b=b: a_w[:, a:b, :], scale))
            if q_bias:
                for h in range(heads):
                    jobs.append((lambda h=h: wkm[:, h, :], lambda: tile["bq"][:, 0:1], CR, 1,
                                 lambda h=h: cb[:, h:h + 1], scale))
            if by_values:
                jobs.append((lambda: tile["wvT"][:, 0, :], None, CO, P, lambda: wv[:], 1.0))
                for n in range(4):
                    jobs.append((lambda n=n: rep[:, n, :, :], lambda: tile["wo"][:, 0, :], P, D,
                                 lambda n=n: wo4[:, n, :], 1.0))
            elif not vo_direct:
                for h in range(heads):
                    jobs.append((lambda h=h: wvm[:, h, :], lambda h=h: tile["wo"][:, h // hc, :], CO, D,
                                 lambda h=h: vo[:, h, :], 1.0))
            block = ctx.enter_context(nc.Block())

            @block.sync
            def _(sp):
                sp.wait_ge(cleared, len(clears))
                for t, f, src in moves:
                    with nc.allow_non_contiguous_dma(reason="biases as columns"):
                        sp.dma_start(f(t), src).then_inc(loaded, 16)
                sp.wait_ge(loaded, 16 * len(moves))

            @block.tensor
            def _(pe):
                pe.wait_ge(loaded, 16 * len(moves))
                for n, (lhs, rhs, rows, cols, _, _) in enumerate(jobs):
                    if n >= 8:
                        pe.wait_ge(kept, n - 7)
                    if n == nturn:
                        pe.wait_ge(mixed, 1 if vo_direct else 2)
                    if rhs is None:
                        src = lhs()
                        k = src.shape[0]
                        m = pe.transpose(ps[n % 8][0:rows, 0:cols], src, g.ident[0:k, 0:k])
                    else:
                        m = pe.matmul(ps[n % 8][0:rows, 0:cols], lhs(), rhs(), start=True, stop=True)
                    m.then_inc(made, 1)

            @block.vector
            def _(dve):
                for n, (t, v) in enumerate(clears):
                    dve.memset(t, v).then_inc(cleared, 1)
                    dve.wait_ge(cleared, n + 1)
                if heads == HEADS:
                    hm = g.hm8 if kc == 1 else g.hm64
                for n, (_, _, rows, cols, dst, sc) in enumerate(jobs):
                    if n == nturn:
                        dve.wait_ge(kept, nturn) if nturn else None
                        dve.wait_ge(loaded, 16 * len(moves))
                        for q, (dst_w, src_w, w) in enumerate(((wkm, "wkT", CR), (wvm, "wvT", CO))):
                            if q == 1 and vo_direct:
                                continue
                            if q == 1 and by_values:
                                dve.tensor_copy(rep[:], g.ident[:].rearrange("p (n o c) -> p n o c", n=4, o=1)
                                                .broadcast_to([P, 4, 4, P // 4])).then_inc(mixed, 1)
                                continue
                            s4 = tile[src_w][:, :, :].rearrange("p k (o c) -> p k o c", o=1)
                            d4 = dst_w[:, :, :].rearrange("p (k h) c -> p k h c", k=kc)
                            if heads == 1:
                                ins = dve.tensor_copy(d4, s4)
                            else:
                                m4 = hm[:, 0:hc].rearrange("p (k h c) -> p k h c", k=1, c=1)
                                ins = dve.tensor_tensor(d4, s4.broadcast_to([P, kc, hc, w]),
                                                        m4.broadcast_to([P, kc, hc, w]), ALU.mult)
                            ins.then_inc(mixed, 1)
                    dve.wait_ge(made, n + 1)
                    out, src = dst(), ps[n % 8][0:rows, 0:cols]
                    if len(out.shape) == 3:
                        src = src.rearrange("p (a b) -> p a b", a=out.shape[1])
                    dve.tensor_scalar(out, src, sc, None, ALU.mult).then_inc(kept, 1)

        if by_values:
            attend_by_values(nc, g, name, ctx_t, a_w, cb, ob, wv, wo4)
            return

        full = heads == HEADS
        gp = 1 if full else 2
        ng = NP // gp
        slots = 2 * gp
        nu = 2 * HEADS * L // P if full else gp
        total = nu * ng
        tg = gp * PAIR
        hq = min(heads, TC // PAIR)
        nq = heads // hq
        width = heads * L if full else P // 2
        with ExitStack() as ctx:
            st = Stage(nc, ctx, name + "m")
            raw = st.sb("raw", [CR, slots, S])
            cxt = st.sb("cxt", [CR, slots, 2, S], F32R)
            cn = st.sb("cn", [NK, slots, KT, CO])
            q32 = st.sb("q32", [CR, TC])
            qhi, qlo = (st.sb(n, [CR, slots, width if full else P], F32R) for n in ("qhi", "qlo"))
            prob = st.sb("prob", [P, 2, S])
            prob_t = st.sb("prob_t", [NK, 2, KT, P])
            bank_max, neg_max = st.sb("bank_max", [P, 2, BANKS]), st.sb("neg_max", [P, 2])
            den, on = st.sb("den", [P, 2]), st.sb("on", [P, 2, CO])
            on_t = st.sb("on_t", [CO, slots, width])
            ps_s = st.ps("ps_s", [P, BANKS, 512])
            ps_t = [st.ps(f"ps_t{n}", [P, 512]) for n in range(2)]
            ps_o, ps_r, ps_q = st.ps("ps_o", [P, 512]), st.ps("ps_r", [P, 512]), st.ps("ps_q", [P, 512])
            ctx_in = [st.sem(f"ctx_in{h}") for h in range(slots)]
            ctxt_in = [st.sem(f"ctxt_in{h}") for h in range(slots)]
            high_made = [st.sem(f"high_made{h}") for h in range(slots)]
            low_made = [st.sem(f"low_made{h}") for h in range(slots)]
            (ones_set, scored, bank_maxed, maxed, exped, turned, kept_dve, kept_act, summed, denned, normed,
             o_turned, o_kept, q_made, q_added, q_kept, projected, out_kept) = (st.sem(x) for x in (
                 "ones_set", "scored", "bank_maxed", "maxed", "exped", "turned", "kept_dve", "kept_act", "summed",
                 "denned", "normed", "o_turned", "o_kept", "q_made", "q_added", "q_kept", "projected", "out_kept"))
            ctx_v = ctx_d.rearrange("b (p t) c -> p b t c", t=KT)
            block = ctx.enter_context(nc.Block())

            def sequences(u):
                u %= nu
                return [u * slots // nu] if full else [2 * u, 2 * u + 1]

            def first_of(u):
                return not full or u % nu % (nu // 2) == 0

            def used(h):
                return (h + 1) * nu // 2 if full else h // 2 + 1

            peel = -(-4 // nu)
            behind = 1 + 3 // nu

            def steps(eng, step):
                for i in range(peel):
                    for u in range(nu):
                        step(i, u)
                with eng.Fori(peel, ng if full else ng - 1) as i:
                    for u in range(nu):
                        step(i, u)
                if not full:
                    for u in range(nu):
                        step(ng - 1, u)
                for u in range(4):
                    step(ng, u)

            def live(i, u, lag):
                return not isinstance(i, int) or 0 <= nu * i + u - lag < total

            def later(i, u, lag):
                return not isinstance(i, int) or nu * i + u - lag > 0

            def low_part(eng, i, h):
                eng.wait_ge(high_made[h], i + 1)
                eng.tensor_tensor(cxt[:, h, 1, :], raw[:, h, :], cxt[:, h, 0, :].bitcast(F32), ALU.subtract
                                  ).then_inc(low_made[h], 1)

            @block.sync
            def _(sp):
                sp.wait_ge(ones_set, 3)

                def load_turned(i, first):
                    for h in range(slots):
                        if not first:
                            sp.wait_ge(low_made[h], i)
                        sp.dma_start(raw[:, h, :], ctx_t[bass.ds(slots * i + h, 1), :, :].rearrange("o r s -> (o r) s")
                                     ).then_inc(ctxt_in[h], 16)

                def load(i, first):
                    for h in range(slots):
                        if not first:
                            sp.wait_ge(summed, nu * i - nu + used(h))
                        sp.dma_start(cn[:, h, :, 0:C],
                                     ctx_v[:, bass.ds(slots * i + h, 1), :, :].rearrange("p o t c -> p (o t) c")
                                     ).then_inc(ctx_in[h], 16)

                load_turned(0, True)
                load_turned(1, False)
                load(0, True)
                with sp.Fori(1, ng - 1) as i:
                    load_turned(i + 1, False)
                    load(i, False)
                load(ng - 1, False)
                for h in range(slots):
                    sp.wait_ge(ctx_in[h], 16 * ng)
                    sp.wait_ge(ctxt_in[h], 16 * ng)

            @block.gpsimd
            def _(pool):
                def split(i, first):
                    for h in range(slots):
                        if full:
                            pool.wait_ge(ctxt_in[h], 16 * (i + 1))
                            if not first:
                                pool.wait_ge(scored, BANKS * (nu * i - nu + used(h)))
                            pool.tensor_tensor(cxt[:, h, 0, :], raw[:, h, :],
                                               g.zeros[0:CR, 0:1].broadcast_to([CR, S]), ALU.add).then_inc(high_made[h], 1)
                        if full or h % 2:
                            low_part(pool, i, h)
                split(0, True)
                with pool.Fori(1, ng) as i:
                    split(i, False)

            @block.tensor
            def _(pe):
                def queries(i, q):
                    n = nq * i + q
                    if not isinstance(n, int) or n > 0:
                        pe.wait_ge(q_kept, n)
                    if q == 0 and (not isinstance(i, int) or i > behind):
                        pe.wait_ge(out_kept, i - behind)
                    for h in range(hq):
                        m = pe.matmul(ps_q[0:CR, h * tg:(h + 1) * tg], a_w[:, q * hq + h, :],
                                      g.xnt[:, bass.ds(i * tg, tg)], start=True, stop=True)
                    m.then_inc(q_made, 1)

                def scores(i, u):
                    v = nu * i + u
                    for h in sequences(u) if first_of(u) else ():
                        pe.wait_ge(low_made[h], i + 1)
                    if u == 0:
                        pe.wait_ge(q_kept, nq * (i + 1))
                    for k in range(BANKS):
                        if later(i, u, 0):
                            pe.wait_ge(exped, BANKS * (v - 1) + k + 1)
                        keys = slice(k * BK, (k + 1) * BK)
                        for h in sequences(u):
                            at = (slice(u * P - h * width, (u + 1) * P - h * width)) if full else slice(0, P)
                            for part, w in ((qhi, 0), (qhi, 1), (qlo, 0)):
                                m = pe.matmul(ps_s[:, k, 0:BK], part[:, h, at], cxt[:, h, w, keys],
                                              start=(part is qhi and w == 0 and h == sequences(u)[0]),
                                              stop=(part is qlo and h == sequences(u)[-1]))
                        m.then_inc(scored, 1)

                def turn(i, u, k):
                    v = nu * i + u
                    pe.wait_ge(exped, BANKS * v + k + 1)
                    if k < 2:
                        if later(i, u, 0):
                            pe.wait_ge(*((kept_dve, 2 * v) if k == 0 else (kept_act, v)))
                    else:
                        pe.wait_ge(kept_dve, 2 * v + 1)
                    for q in range(GT):
                        t = k * GT + q
                        m = pe.transpose(ps_t[(BANKS * u + k) % 2][0:NK, q * P:(q + 1) * P],
                                         prob[:, u % 2, t * NK:(t + 1) * NK], g.ident[:])
                    m.then_inc(turned, 1)

                def sums(i, u):
                    v = nu * i + u
                    pe.wait_ge(kept_dve, 2 * v + 2)
                    pe.wait_ge(kept_act, v + 1)
                    for h in sequences(u) if first_of(u) else ():
                        pe.wait_ge(ctx_in[h], 16 * (i + 1 + (u // nu)))
                    if later(i, u, 0):
                        pe.wait_ge(normed, v)
                    hs = sequences(u)
                    part = P // len(hs)
                    for n, h in enumerate(hs):
                        at = slice(n * part, (n + 1) * part)
                        for t in range(KT):
                            m = pe.matmul(ps_o[at, 0:CO], prob_t[:, u % 2, t, at], cn[:, h, t, :],
                                          start=(t == 0), stop=(t == KT - 1))
                    m.then_inc(summed, 1)

                def o_turn(i, u):
                    v = nu * i + u
                    pe.wait_ge(normed, v + 1)
                    if later(i, u, 0):
                        pe.wait_ge(o_kept, v)
                    pe.transpose(ps_r[0:CO, 0:P], on[:, u % 2, :], g.ident[:]).then_inc(o_turned, 1)

                def project(i):
                    pe.wait_ge(o_kept, nu * (i + 1))
                    n = nq * (i + behind + 1)
                    pe.wait_ge(q_kept, min(n, nq * (ng + 1)) if isinstance(i, int) else n)
                    for h in range(heads):
                        m = pe.matmul(ps_q[:, 0:tg], vo[:, h, :], on_t[:, :, h * L:(h + 1) * L],
                                      start=(h == 0), stop=(h == heads - 1))
                    m.then_inc(projected, 1)

                def step(i, u):
                    if live(i, u, 0):
                        scores(i, u)
                    if live(i, u, 1):
                        turn(i, u - 1, 0)
                        turn(i, u - 1, 1)
                    if (u - 4) % nu == nu - 1 and live(i, u, 4):
                        project(i + (u - 4) // nu)
                    if live(i, u, 3):
                        o_turn(i, u - 3)
                    if live(i, u, 0) and u == nu - 1:
                        for q in range(nq):
                            queries(i + 1, q)
                    if live(i, u, 2):
                        sums(i, u - 2)
                    if live(i, u, 1):
                        turn(i, u - 1, 2)

                for q in range(nq):
                    queries(0, q)
                steps(pe, step)

            @block.vector
            def _(dve):
                def queries(i):
                    for q in range(nq):
                        n = nq * i + q
                        src = ps_q[0:CR, 0:hq * tg].rearrange("p (h b l) -> p b h l", h=hq, b=slots)
                        mid = q32[:, 0:hq * tg].rearrange("p (b h l) -> p b h l", b=slots, h=hq)
                        bias = cb[:, q * hq:(q + 1) * hq].rearrange("p (b h l) -> p b h l", b=1, l=1)
                        dve.wait_ge(q_made, n + 1)
                        dve.tensor_tensor(mid, src, bias.broadcast_to([CR, slots, hq, L]), ALU.add
                                          ).then_inc(q_added, 1)
                        if full:
                            cols = slice(q * hq * L, (q + 1) * hq * L)
                            views = [(qhi[:, :, cols], qlo[:, :, cols], q32[:, 0:hq * tg].rearrange(
                                "p (b c) -> p b c", b=slots))]
                        else:
                            views = [tuple(x[:, h::2, P // 2 * h:P // 2 * h + L] for x in (qhi, qlo)) +
                                     (q32[:, 0:tg].rearrange("p (b c) -> p b c", b=slots)[:, h::2, :],)
                                     for h in range(2)]
                        dve.wait_ge(q_added, (1 + len(views)) * n + 1)
                        for hi, _, x in views:
                            dve.tensor_copy(hi, x).then_inc(q_added, 1)
                        dve.wait_ge(q_added, (1 + len(views)) * (n + 1))
                        for m, (hi, lo, x) in enumerate(views):
                            ins = dve.tensor_tensor(lo, x, hi.bitcast(F32), ALU.subtract)
                        ins.then_inc(q_kept, 1)

                def maxima(i, u):
                    s = u % 2
                    v = nu * i + u
                    for k in range(BANKS):
                        dve.wait_ge(scored, BANKS * v + k + 1)
                        dve.tensor_reduce(bank_max[:, s, k:k + 1], ps_s[:, k, 0:BK], AX.X, ALU.max
                                          ).then_inc(bank_maxed, 1)
                    dve.wait_ge(bank_maxed, BANKS * (v + 1))
                    dve.tensor_reduce(neg_max[:, s:s + 1], bank_max[:, s, :], AX.X, ALU.max, negate=True
                                      ).then_inc(maxed, 1)

                def keep(i, u, k):
                    v = nu * i + u
                    dve.wait_ge(turned, BANKS * v + k + 1)
                    if later(i, u, 1):
                        dve.wait_ge(summed, v - 1)
                    dve.tensor_copy(prob_t[:, u % 2, k * GT:(k + 1) * GT, :],
                                    ps_t[(BANKS * u + k) % 2][0:NK, :].rearrange("p (t r) -> p t r", t=GT)
                                    ).then_inc(kept_dve, 1)

                def normalise(i, u):
                    s = u % 2
                    v = nu * i + u
                    dve.wait_ge(summed, v + 1)
                    dve.reciprocal(den[:, s:s + 1], ps_o[:, C:CO]).then_inc(denned, 1)
                    dve.wait_ge(denned, v + 1)
                    if later(i, u, 1):
                        dve.wait_ge(o_turned, v - 1)
                    dve.tensor_scalar(on[:, s, :], ps_o[:, 0:CO], den[:, s:s + 1], None, ALU.mult
                                      ).then_inc(normed, 1)

                def step(i, u):
                    if live(i, u, 0):
                        maxima(i, u)
                    if live(i, u, 1):
                        keep(i, u - 1, 0)
                        keep(i, u - 1, 1)
                    if live(i, u, 0) and u == nu - 1:
                        queries(i + 1)
                    if not full and live(i, u, -nu):
                        low_part(dve, i + 1, 2 * u)
                    if live(i, u, 2):
                        normalise(i, u - 2)

                dve.memset(qhi[:].bitcast(F32), 0.0).then_inc(ones_set, 1)
                dve.memset(qlo[:].bitcast(F32), 0.0).then_inc(ones_set, 1)
                dve.memset(cn[:, :, :, C:CO], 1.0).then_inc(ones_set, 1)
                dve.wait_ge(ones_set, 2)
                queries(0)
                if not full:
                    for u in range(nu):
                        low_part(dve, 0, 2 * u)
                steps(dve, step)

            @block.scalar
            def _(act):
                def high_part(i, u):
                    for h in sequences(u):
                        act.wait_ge(ctxt_in[h], 16 * (i + 1))
                        act.activation(cxt[:, h, 0, :], raw[:, h, :], ACT.Copy).then_inc(high_made[h], 1)

                def exps(i, u):
                    s = u % 2
                    v = nu * i + u
                    act.wait_ge(maxed, v + 1)
                    if later(i, u, 1):
                        act.wait_ge(turned, BANKS * (v - 1))
                    for k in range(BANKS):
                        act.activation(prob[:, s, k * BK:(k + 1) * BK], ps_s[:, k, 0:BK], ACT.Exp,
                                       bias=neg_max[:, s:s + 1]).then_inc(exped, 1)

                def keep(i, u):
                    v = nu * i + u
                    act.wait_ge(turned, BANKS * (v + 1))
                    if later(i, u, 1):
                        act.wait_ge(summed, v - 1)
                    act.activation(prob_t[:, u % 2, 2 * GT:KT, :],
                                   ps_t[(BANKS * u + 2) % 2][0:NK, :].rearrange("p (t r) -> p t r", t=GT),
                                   ACT.Copy).then_inc(kept_act, 1)

                def o_keep(i, u):
                    v = nu * i + u
                    act.wait_ge(o_turned, v + 1)
                    if u % nu == 0 and (not isinstance(i, int) or v > 0):
                        act.wait_ge(projected, i + u // nu)
                    flat = on_t[:].rearrange("p b c -> p (b c)")
                    act.activation(flat[:, u % nu * P:(u % nu + 1) * P], ps_r[0:CO, 0:P], ACT.Copy
                                   ).then_inc(o_kept, 1)

                def out(i):
                    act.wait_ge(projected, i + 1)
                    act.activation(g.addt[:, bass.ds(i * tg, tg)], ps_q[:, 0:tg], ACT.Identity,
                                   bias=ob[:, 0:1]).then_inc(out_kept, 1)

                def step(i, u):
                    if live(i, u, 0):
                        exps(i, u)
                    if (u - 4) % nu == nu - 1 and live(i, u, 4):
                        out(i + (u - 4) // nu)
                    if live(i, u, 3):
                        o_keep(i, u - 3)
                    if live(i, u, 1):
                        keep(i, u - 1)
                    if not full and live(i, u, -nu):
                        high_part(i + 1, u)

                if not full:
                    for u in range(nu):
                        high_part(0, u)
                steps(act, step)


def head_rows(x, part):
    if len(x.shape) == 2:
        return x.rearrange("(h k d) c -> k h d c", h=HEADS, k=2)[part]
    return x.rearrange("(h k d) -> k h d", h=HEADS, k=2)[part]


def col(x):
    return x.rearrange("(p o) -> p o", o=1)


def spread(x, n):
    return x.rearrange("p (t o) -> p t o", o=1).broadcast_to([P, NT, n])


def logits(nc, g, name, xt, experts, w_dram, b_dram, w_turned, out):
    with ExitStack() as ctx:
        st = Stage(nc, ctx, name)
        raw, w, bias = st.sb("raw", [16, D]), st.sb("w", [D, experts]), st.sb("bias", [1, experts])
        psw, psl = st.ps("psw", [P, 512]), st.ps("psl", [P, NT, experts])
        loaded, turned, kept, made, done = (st.sem(x) for x in ("loaded", "turned", "kept", "made", "done"))
        n_in = 1 + (b_dram is not None)
        block = ctx.enter_context(nc.Block())

        @block.sync
        def _(sp):
            if b_dram is not None:
                sp.dma_start(bias[:], b_dram.rearrange("(o e) -> o e", o=1)).then_inc(loaded, 16)
            sp.dma_start(w[:] if w_turned else raw[0:experts, :], w_dram).then_inc(loaded, 16)
            sp.wait_ge(loaded, 16 * n_in)

        @block.tensor
        def _(pe):
            pe.wait_ge(loaded, 16 * n_in)
            if not w_turned:
                pe.transpose(psw[:, 0:experts], raw[0:experts, :], g.ident[0:experts, 0:experts]).then_inc(turned, 1)
                pe.wait_ge(kept, 1)
            for t in range(NT):
                if b_dram is not None:
                    pe.matmul(psl[:, t, :], g.ones[0:1, :], bias[:], start=True, stop=False)
                m = pe.matmul(psl[:, t, :], xt[:, t * P:(t + 1) * P], w[:], start=b_dram is None, stop=True)
            m.then_inc(made, 1)

        @block.vector
        def _(dve):
            if not w_turned:
                dve.wait_ge(turned, 1)
                dve.tensor_copy(w[:], psw[:, 0:experts]).then_inc(kept, 1)
            dve.wait_ge(made, 1)
            dve.tensor_copy(out, psl[:, :, :]).then_inc(done, 1)


def turn_weights(nc, g, name, experts, src, dst):
    with ExitStack() as ctx:
        st = Stage(nc, ctx, name)
        ps = [st.ps(f"ps{n}", [P, 512]) for n in range(4)]
        made, kept = st.sem("made"), st.sem("kept")
        block = ctx.enter_context(nc.Block())

        @block.tensor
        def _(pe):
            for n in range(4):
                for t in range(4 * n, min(4 * n + 4, NT)):
                    m = pe.transpose(ps[n][0:experts, (t % 4) * P:(t % 4 + 1) * P], src[:, t, :], g.ident[:])
                m.then_inc(made, 1)

        @block.vector
        def _(dve):
            for n in range(4):
                a, b = 512 * n, min(512 * n + 512, T)
                dve.wait_ge(made, n + 1)
                dve.tensor_copy(dst[0:experts, a:b], ps[n][0:experts, 0:b - a]).then_inc(kept, 1)


def route_mixer(nc, g, full, gw):
    with ExitStack() as ctx:
        st = Stage(nc, ctx, "mixer")
        t8 = lambda n: st.sb(n, [P, NT, 8])
        t1 = lambda n: st.sb(n, [P, NT])
        dyn, top, ptop, idx = t8("dyn"), t8("top"), t8("ptop"), st.sb("idx", [P, NT, 8], U32)
        idxf, mag, hot, alive, e1, e2, e3, rw, mask = (t8(n) for n in (
            "idxf", "mag", "hot", "alive", "e1", "e2", "e3", "rw", "mask"))
        s1, s2, csum, valid = t1("s1"), t1("s2"), t1("csum"), t1("valid")
        w9, carry = st.sb("w9", [P, NT, 9]), st.sb("carry", [P, NT, 8])
        ps = st.ps("ps", [P, 512])
        pst = st.ps("pst", [P, 512])
        dved, asked, exped, masked, counted = (st.sem(x) for x in ("dved", "asked", "exped", "masked", "counted"))
        block = ctx.enter_context(nc.Block())
        exps = []

        @block.vector
        def _(dve):
            link = chain(dve, dved)

            def exp(tile):
                exps.append(tile)
                dve.wait_ge(exped, len(exps))

            def tt(out, a, b, op):
                link(dve.tensor_tensor(out, a, b, op))

            def ask(ins):
                ins.then_inc(asked, 1)

            link(dve.tensor_copy(dyn[:], full[:, :, 0:8]))
            for t in range(NT):
                dve.max(top[:, t, :], dyn[:, t, :]).then_inc(dved, 1)
            dve.wait_ge(dved, 1 + NT)
            for t in range(NT):
                dve.max_index(idx[:, t, :], top[:, t, :], dyn[:, t, :]).then_inc(dved, 1)
            dve.wait_ge(dved, 1 + 2 * NT)
            done = [1 + 2 * NT]

            def link(ins):
                done[0] += 1
                ins.then_inc(dved, 1)
                dve.wait_ge(dved, done[0])

            link(dve.tensor_copy(idxf[:], idx[:]))
            link(dve.scalar_tensor_tensor(mag[:], dyn[:], -1.0, dyn[:], ALU.mult, ALU.max))
            ask(dve.tensor_tensor(ptop[:], top[:], top[:, :, 0:1].broadcast_to([P, NT, 8]), ALU.subtract))
            exp(ptop[:])
            link(dve.tensor_reduce(s1[:], ptop[:], AX.X, ALU.add))
            link(dve.reciprocal(s1[:], s1[:]))
            link(dve.tensor_tensor(ptop[:], ptop[:], spread(s1[:], 8), ALU.mult))
            link(dve.memset(csum[:], 0.0))
            link(dve.memset(alive[:], 1.0))
            link(dve.memset(rw[:], 0.0))
            for k in range(4):
                thr = top[:, :, k:k + 1].broadcast_to([P, NT, 8])
                link(dve.tensor_scalar(valid[:], csum[:], 0.75, None, ALU.is_lt))
                link(dve.tensor_tensor(csum[:], csum[:], ptop[:, :, k], ALU.add))
                link(dve.tensor_tensor(hot[:], idxf[:, :, k:k + 1].broadcast_to([P, NT, 8]),
                                       g.iota8[:].rearrange("p (o e) -> p o e", o=1).broadcast_to([P, NT, 8]),
                                       ALU.is_equal))
                link(dve.tensor_tensor(e1[:], thr, dyn[:], ALU.subtract))
                link(dve.tensor_scalar(s2[:], top[:, :, k], -1.0, None, ALU.mult))
                link(dve.tensor_tensor(s2[:], s2[:], top[:, :, k], ALU.max))
                link(dve.tensor_tensor(e2[:], mag[:], spread(s2[:], 8), ALU.max))
                link(dve.tensor_scalar(e2[:], e2[:], 1e-37, None, ALU.max))
                link(dve.reciprocal(e2[:], e2[:]))
                link(dve.tensor_tensor(e2[:], e1[:], e2[:], ALU.mult))
                link(dve.tensor_scalar(e2[:], e2[:], 0.2, None, ALU.is_le))
                link(dve.tensor_tensor(e2[:], e2[:], alive[:], ALU.mult))
                ask(dve.tensor_scalar(e3[:], e1[:], 0.0, -1.0, ALU.max, ALU.mult))
                exp(e3[:])
                link(dve.tensor_tensor(e3[:], e3[:], e2[:], ALU.mult))
                link(dve.tensor_reduce(s1[:], e3[:], AX.X, ALU.add))
                link(dve.reciprocal(s1[:], s1[:]))
                link(dve.tensor_tensor(s1[:], s1[:], valid[:], ALU.mult))
                link(dve.tensor_tensor(e1[:], hot[:], spread(s1[:], 8), ALU.mult))
                link(dve.tensor_tensor(rw[:], rw[:], e1[:], ALU.add))
                link(dve.tensor_tensor(alive[:], alive[:], hot[:], ALU.subtract))
            link(dve.tensor_reduce(s1[:], rw[:], AX.X, ALU.add))
            link(dve.reciprocal(s1[:], s1[:]))
            link(dve.tensor_tensor(rw[:], rw[:], spread(s1[:], 8), ALU.mult))
            dve.tensor_scalar(mask[:], rw[:], 0.0, None, ALU.is_gt).then_inc(masked, 1)
            dve.wait_ge(counted, 1)
            link(dve.memset(carry[:, 0, :], 0.0))
            for t in range(1, NT):
                link(dve.tensor_tensor(carry[:, t, :], carry[:, t - 1, :], pst[:, (t - 1) * 8:t * 8], ALU.add))
            link(dve.tensor_tensor(carry[:], carry[:], ps[:, 0:NT * 8].rearrange("p (t e) -> p t e", e=8), ALU.add))
            link(dve.tensor_scalar(carry[:], carry[:], float(CAP), None, ALU.is_le))
            dve.wait_ge(masked, 1)
            link(dve.tensor_tensor(mask[:], mask[:], carry[:], ALU.mult))
            link(dve.tensor_scalar(e1[:], mask[:], -1.0, BIG, ALU.add, ALU.mult))
            link(dve.tensor_tensor(w9[:, :, 0:8], dyn[:], e1[:], ALU.add))
            link(dve.tensor_copy(w9[:, :, 8:9], full[:, :, 8:9]))
            link(dve.tensor_reduce(s1[:], w9[:], AX.X, ALU.max))
            ask(dve.tensor_tensor(w9[:], w9[:], spread(s1[:], 9), ALU.subtract))
            exp(w9[:])
            link(dve.tensor_reduce(s1[:], w9[:], AX.X, ALU.add))
            link(dve.reciprocal(s1[:], s1[:]))
            link(dve.tensor_tensor(w9[:], w9[:], spread(s1[:], 9), ALU.mult))
            link(dve.tensor_reduce(s1[:], w9[:, :, 0:8], AX.X, ALU.add))
            link(dve.tensor_tensor(rw[:], rw[:], spread(s1[:], 8), ALU.mult))
            link(dve.tensor_tensor(gw[:, :, 0:8], rw[:], mask[:], ALU.mult))
            link(dve.tensor_copy(gw[:, :, 8:9], w9[:, :, 8:9]))

        @block.scalar
        def _(act):
            for n, tile in enumerate(exps):
                act.wait_ge(asked, n + 1)
                act.activation(tile, tile, ACT.Exp).then_inc(exped, 1)

        @block.tensor
        def _(pe):
            pe.wait_ge(masked, 1)
            m = mask[:].rearrange("p t e -> p (t e)")
            pe.matmul(ps[:, 0:NT * 8], g.tri[:], m, start=True, stop=True)
            pe.matmul(pst[:, 0:NT * 8], g.ones[:], m, start=True, stop=True).then_inc(counted, 1)


def route_top2(nc, g, name, lg, experts, of_probs, w, wsum):
    with ExitStack() as ctx:
        st = Stage(nc, ctx, name)
        t8 = lambda n: st.sb(n, [P, NT, 8])
        v, top, idxf, h0, h1 = t8("v"), t8("top"), t8("idxf"), t8("h0"), t8("h1")
        idx = st.sb("idx", [P, NT, 8], U32)
        s1, s2 = st.sb("s1", [P, NT]), st.sb("s2", [P, NT])
        dved, asked, exped = st.sem("dved"), st.sem("asked"), st.sem("exped")
        block = ctx.enter_context(nc.Block())

        @block.vector
        def _(dve):
            link = chain(dve, dved)
            if of_probs:
                link(dve.memset(v[:], -1.0))
                link(dve.tensor_reduce(s1[:], lg, AX.X, ALU.max))
                dve.tensor_tensor(v[:, :, 0:experts], lg, spread(s1[:], experts), ALU.subtract).then_inc(asked, 1)
                dve.wait_ge(exped, 1)
                link(dve.tensor_reduce(s1[:], v[:, :, 0:experts], AX.X, ALU.add))
                link(dve.reciprocal(s1[:], s1[:]))
                link(dve.tensor_tensor(v[:, :, 0:experts], v[:, :, 0:experts], spread(s1[:], experts), ALU.mult))
            else:
                link(dve.tensor_copy(v[:], lg))
            for t in range(NT):
                link(dve.max(top[:, t, :], v[:, t, :]))
            for t in range(NT):
                link(dve.max_index(idx[:, t, :], top[:, t, :], v[:, t, :]))
            link(dve.tensor_copy(idxf[:], idx[:]))
            iota = g.iota8[:].rearrange("p (o e) -> p o e", o=1).broadcast_to([P, NT, 8])
            link(dve.tensor_tensor(h0[:], idxf[:, :, 0:1].broadcast_to([P, NT, 8]), iota, ALU.is_equal))
            link(dve.tensor_tensor(h1[:], idxf[:, :, 1:2].broadcast_to([P, NT, 8]), iota, ALU.is_equal))
            if not of_probs:
                dve.tensor_tensor(v[:, :, 0:2], top[:, :, 0:2], top[:, :, 0:1].broadcast_to([P, NT, 2]),
                                  ALU.subtract).then_inc(asked, 1)
                dve.wait_ge(exped, 1)
                link(dve.tensor_copy(top[:, :, 0:2], v[:, :, 0:2]))
            link(dve.tensor_tensor(s1[:], top[:, :, 0], top[:, :, 1], ALU.add))
            link(dve.reciprocal(s1[:], s1[:]))
            link(dve.tensor_tensor(s2[:], top[:, :, 1], s1[:], ALU.mult))
            link(dve.tensor_tensor(s1[:], top[:, :, 0], s1[:], ALU.mult))
            link(dve.tensor_tensor(h0[:], h0[:], spread(s1[:], 8), ALU.mult))
            link(dve.tensor_tensor(h1[:], h1[:], spread(s2[:], 8), ALU.mult))
            link(dve.tensor_tensor(w, h0[:, :, 0:experts], h1[:, :, 0:experts], ALU.add))
            if wsum is not None:
                link(dve.tensor_reduce(wsum, w, AX.X, ALU.add))

        @block.scalar
        def _(act):
            act.wait_ge(asked, 1)
            t = v[:, :, 0:experts if of_probs else 2]
            act.activation(t, t, ACT.Exp).then_inc(exped, 1)


def gated_mlp(nc, g, name, packs, up_srcs, down_srcs, pick, experts, gwt):
    with ExitStack() as outer:
        so = Stage(nc, outer, name)
        wg, wu, wd = (so.sb(n, [P, packs, D]) for n in ("wg", "wu", "wd"))
        with ExitStack() as ctx:
            st = Stage(nc, ctx, name + "w")
            raw = [st.sb(f"raw{n}", [P, packs, D]) for n in range(2)] + [st.sb("raw2", [P, packs * P])]
            ps = [st.ps(f"ps{n}", [P, 512]) for n in range(8)]
            loaded, made, kept = st.sem("loaded"), st.sem("made"), st.sem("kept")
            jobs = [(raw[w][:, k, :], (wg, wu)[w][:, k, :]) for w in range(2) for k in range(packs)]
            jobs += [(raw[2][:, k * P:(k + 1) * P], wd[:, k, :]) for k in range(packs)]
            n_in = len(up_srcs) + len(down_srcs)
            block = ctx.enter_context(nc.Block())

            @block.sync
            def _(sp):
                for w, k, n, src in up_srcs:
                    sp.dma_start(raw[w][:, k:k + n, :], src.rearrange("(k p) d -> p k d", p=P)).then_inc(loaded, 16)
                for k, n, src in down_srcs:
                    sp.dma_start(raw[2][:, k * P:(k + n) * P].rearrange("d (e i) -> d e i", e=src.shape[0]),
                                 src.rearrange("e d i -> d e i")).then_inc(loaded, 16)
                sp.wait_ge(loaded, 16 * n_in)

            @block.tensor
            def _(pe):
                pe.wait_ge(loaded, 16 * n_in)
                for n, (src, _) in enumerate(jobs):
                    if n >= 8:
                        pe.wait_ge(kept, n - 7)
                    pe.transpose(ps[n % 8][:, 0:P], src, g.ident[:]).then_inc(made, 1)

            @block.vector
            def _(dve):
                for n, (_, dst) in enumerate(jobs):
                    dve.wait_ge(made, n + 1)
                    dve.tensor_copy(dst, ps[n % 8][:, 0:P]).then_inc(kept, 1)

        with ExitStack() as ctx:
            st = Stage(nc, ctx, name + "m")
            sg, up, hid = (st.sb(n, [P, 2, TC]) for n in ("sg", "up", "hid"))
            ps_g, ps_u, ps_w = ([st.ps(f"ps_{n}{k}", [P, 512]) for k in range(2)] for n in "guw")
            ps_y = st.ps("ps_y", [P, 512])
            gated, made, silued, upped, weighted, added, kept = (st.sem(x) for x in (
                "gated", "made", "silued", "upped", "weighted", "added", "kept"))
            block = ctx.enter_context(nc.Block())

            @block.tensor
            def _(pe):
                def down(c, k):
                    n = packs * c + k
                    pe.wait_ge(weighted, n + 1)
                    pe.matmul(ps_y[:, 0:TC], wd[:, k, :], hid[:, k % 2, :], start=(k == 0), stop=(k == packs - 1)
                              ).then_inc(added, 1)

                def chunk(c, first):
                    x = g.xnt[:, bass.ds(c * TC, TC)]
                    for k in range(packs):
                        n = packs * c + k
                        if not first or k >= 2:
                            pe.wait_ge(silued, n - 1)
                        pe.matmul(ps_g[k % 2][:, 0:TC], wg[:, k, :], x, start=True, stop=True).then_inc(gated, 1)
                        if not first or k >= 2:
                            pe.wait_ge(weighted, n - 1)
                        pe.matmul(ps_u[k % 2][:, 0:TC], wu[:, k, :], x, start=True, stop=True)
                        pe.matmul(ps_w[k % 2][:, 0:TC], pick[0:experts, k * P:(k + 1) * P],
                                  gwt[0:experts, bass.ds(c * TC, TC)], start=True, stop=True).then_inc(made, 1)
                        if k == 1 and not first:
                            pe.wait_ge(kept, c)
                        if k > 0:
                            down(c, k - 1)
                    down(c, packs - 1)
                chunk(0, True)
                with pe.Fori(1, NC) as c:
                    chunk(c, False)

            @block.scalar
            def _(act):
                def chunk(c, first):
                    for k in range(packs):
                        n = packs * c + k
                        act.wait_ge(gated, n + 1)
                        if not first or k >= 2:
                            act.wait_ge(upped, n - 1)
                        act.activation(sg[:, k % 2, :], ps_g[k % 2][:, 0:TC], ACT.Silu).then_inc(silued, 1)
                    act.wait_ge(added, packs * (c + 1))
                    act.activation(g.addt[:, bass.ds(c * TC, TC)], ps_y[:, 0:TC], ACT.Copy).then_inc(kept, 1)
                chunk(0, True)
                with act.Fori(1, NC) as c:
                    chunk(c, False)

            @block.vector
            def _(dve):
                def chunk(c, first):
                    for k in range(packs):
                        n = packs * c + k
                        dve.wait_ge(silued, n + 1)
                        dve.wait_ge(made, n + 1)
                        dve.tensor_tensor(up[:, k % 2, :], sg[:, k % 2, :], ps_u[k % 2][:, 0:TC], ALU.mult
                                          ).then_inc(upped, 1)
                        dve.wait_ge(upped, n + 1)
                        if not first or k >= 2:
                            dve.wait_ge(added, n - 1)
                        dve.tensor_tensor(hid[:, k % 2, :], up[:, k % 2, :], ps_w[k % 2][:, 0:TC], ALU.mult
                                          ).then_inc(weighted, 1)
                chunk(0, True)
                with dve.Fori(1, NC) as c:
                    chunk(c, False)


ME, MF = 4, 4


def moe_layer(nc, g, name, w1_d, w2_d, b1_d, b2_d, lg_d, lb_d, gwt):
    with ExitStack() as ctx:
        st = Stage(nc, ctx, name)
        w1, w2 = st.sb("w1", [D, ME, MF, P]), st.sb("w2", [P, ME, MF, D])
        b1, b2, lng, lnb = st.sb("b1", [P, ME, MF]), st.sb("b2", [D, ME]), st.sb("lng", [D, ME]), st.sb("lnb", [D, ME])
        xe, hid, y, wb = st.sb("xe", [D, 2, TC]), st.sb("hid", [P, 2, TC]), st.sb("y", [D, TC]), st.sb("wb", [D, 2, TC])
        ps_h, ps_y, ps_w = ([st.ps(f"ps_{n}{k}", [P, 512]) for k in range(2)] for n in "hyw")
        loaded, scaled, upped, gelued, summed, spread_, wkept, yed, added = (st.sem(x) for x in (
            "loaded", "scaled", "upped", "gelued", "summed", "spread", "wkept", "yed", "added"))
        half = st.sem("half")
        block = ctx.enter_context(nc.Block())

        @block.sync
        def _(sp):
            sp.dma_start(w1[:].rearrange("h e k f -> h e (k f)"), w1_d.rearrange("e h f -> h e f")).then_inc(loaded, 16)
            with nc.allow_non_contiguous_dma(reason="vectors as columns"):
                sp.dma_start(b1[:], b1_d.rearrange("e (k p) -> p e k", p=P)).then_inc(loaded, 16)
                for t, src in ((b2, b2_d), (lng, lg_d), (lnb, lb_d)):
                    sp.dma_start(t[:], src.rearrange("e h -> h e")).then_inc(loaded, 16)
            sp.dma_start(w2[:].rearrange("p e k h -> p (e k) h"), w2_d.rearrange("e (k p) h -> p (e k) h", p=P)
                         ).then_inc(loaded, 16)
            sp.wait_ge(loaded, 96)

        @block.tensor
        def _(pe):
            pe.wait_ge(loaded, 96)

            def chunk(c, first):
                def down(e, k):
                    n = 16 * c + 4 * e + k
                    pe.wait_ge(gelued, n + 1)
                    if k == 0 and not (first and e < 2):
                        pe.wait_ge(yed, 4 * c + e - 1)
                    pe.matmul(ps_y[e % 2][:, 0:TC], w2[:, e, k, :], hid[:, k % 2, :], start=(k == 0), stop=(k == MF - 1)
                              ).then_inc(summed, 1)
                for e in range(ME):
                    m = 4 * c + e
                    if not (first and e < 2):
                        pe.wait_ge(wkept, m - 1)
                    pe.wait_ge(scaled, m + 1)
                    for k in range(MF):
                        n = 16 * c + 4 * e + k
                        if not (first and e == 0 and k < 2):
                            pe.wait_ge(gelued, n - 1)
                        pe.matmul(ps_h[k % 2][:, 0:TC], w1[:, e, k, :], xe[:, e % 2, :], start=True, stop=True
                                  ).then_inc(upped, 1)
                        if k == 0:
                            pe.matmul(ps_w[e % 2][:, 0:TC], g.pick_f1[0:ME, e * P:(e + 1) * P],
                                      gwt[0:ME, bass.ds(c * TC, TC)], start=True, stop=True).then_inc(spread_, 1)
                        if e or k:
                            down(e if k else e - 1, k - 1 if k else MF - 1)
                down(ME - 1, MF - 1)
            chunk(0, True)
            with pe.Fori(1, NC) as c:
                chunk(c, False)

        @block.scalar
        def _(act):
            act.wait_ge(loaded, 96)

            def chunk(c, first):
                for e in range(ME):
                    for k in range(MF):
                        n = 16 * c + 4 * e + k
                        act.wait_ge(upped, n + 1)
                        if not (first and e == 0 and k < 2):
                            act.wait_ge(summed, n - 1)
                        act.activation(hid[:, k % 2, :], ps_h[k % 2][:, 0:TC], ACT.Gelu, bias=b1[:, e, k:k + 1]
                                       ).then_inc(gelued, 1)
            chunk(0, True)
            with act.Fori(1, NC) as c:
                chunk(c, False)

        @block.vector
        def _(dve):
            dve.wait_ge(loaded, 96)

            def scale(c, e, first):
                m = 4 * c + e
                if not (first and e < 2):
                    dve.wait_ge(upped, 4 * (m - 1))
                dve.tensor_scalar(xe[:, e % 2, :], g.xnt[:, bass.ds(c * TC, TC)], lng[:, e:e + 1], lnb[:, e:e + 1],
                                  ALU.mult, ALU.add).then_inc(scaled, 1)

            def chunk(c, first):
                scale(c, 0, first)
                for e in range(ME):
                    m = 4 * c + e
                    if e + 1 < ME:
                        scale(c, e + 1, first)
                    dve.wait_ge(spread_, m + 1)
                    dve.tensor_copy(wb[:, e % 2, :], ps_w[e % 2][:, 0:TC]).then_inc(wkept, 1)
                    dve.wait_ge(wkept, m + 1)
                    dve.wait_ge(summed, 4 * (m + 1))
                    out = g.addt[:, bass.ds(c * TC, TC)]
                    if e == 0:
                        dve.scalar_tensor_tensor(out, ps_y[0][:, 0:TC], b2[:, 0:1], wb[:, 0, :], ALU.add, ALU.mult
                                                 ).then_inc(yed, 1)
                    else:
                        dve.scalar_tensor_tensor(y[:], ps_y[e % 2][:, 0:TC], b2[:, e:e + 1], wb[:, e % 2, :],
                                                 ALU.add, ALU.mult).then_inc(yed, 1)
                        dve.wait_ge(yed, m + 1)
                        dve.tensor_tensor(out, out, y[:], ALU.add).then_inc(added, 1)
            chunk(0, True)
            with dve.Fori(1, NC) as c:
                chunk(c, False)


def mx_linear(nc, g, w_d, b_d):
    with ExitStack() as ctx:
        st = Stage(nc, ctx, "mx")
        w, b = st.sb("w", [P, 1, D]), st.sb("b", [D, 1])
        wt, xt = st.sb("wt", [D, P]), st.sb("xt", [D, T])
        loaded, dved, quantised = st.sem("loaded"), st.sem("dved"), st.sem("quantised")
        turned, kept, made, done = st.sem("turned"), st.sem("kept"), st.sem("made"), st.sem("done")
        ps = [st.ps(f"ps{n}", [P, 512]) for n in range(8)]
        t = [st.sb(f"t{n}", [P, NT, D]) for n in range(4)]
        sc, rs = st.sb("sc", [P, NT * 4]), st.sb("rs", [P, NT * 4])
        block = ctx.enter_context(nc.Block())

        @block.sync
        def _(sp):
            sp.dma_start(w[:, 0, :], w_d).then_inc(loaded, 16)
            with nc.allow_non_contiguous_dma(reason="bias as a column"):
                sp.dma_start(b[:], col(b_d)).then_inc(loaded, 16)
            sp.wait_ge(loaded, 32)

        @block.vector
        def _(dve):
            link = chain(dve, dved)

            def quantise(x, n):
                v = x.rearrange("p t (k c) -> p (t k) c", c=32)
                y, a, r, s = (i[:, 0:n, :].rearrange("p t (k c) -> p (t k) c", c=32) for i in t)
                m = 4 * n
                bc = lambda q: q[:, 0:m].rearrange("p (k o) -> p k o", o=1).broadcast_to([P, m, 32])
                link(dve.tensor_reduce(sc[:, 0:m], v, AX.X, ALU.max, apply_absolute_value=True))
                link(dve.tensor_scalar(sc[:, 0:m], sc[:, 0:m], 1.0 / 7.5, 1e-30, ALU.mult, ALU.max))
                link(dve.reciprocal(rs[:, 0:m], sc[:, 0:m]))
                link(dve.tensor_tensor(y, v, bc(rs), ALU.mult))
                link(dve.scalar_tensor_tensor(a, y, -1.0, y, ALU.mult, ALU.max))
                link(dve.tensor_scalar(r, a, 2.0, -4.0, ALU.is_ge, ALU.mult))
                link(dve.tensor_scalar(a, a, 4.0, -2.0, ALU.is_ge, ALU.mult))
                link(dve.scalar_tensor_tensor(r, r, 8.0, a, ALU.add, ALU.add))
                link(dve.reciprocal(a, r))
                link(dve.tensor_tensor(y, y, r, ALU.mult))
                link(dve.tensor_scalar(s, y, ROUND, None, ALU.add))
                link(dve.tensor_scalar(s, s, -ROUND, None, ALU.add))
                link(dve.tensor_tensor(r, s, y, ALU.subtract))
                link(dve.tensor_scalar(r, r, 0.5, None, ALU.is_ge))
                link(dve.tensor_tensor(s, s, r, ALU.subtract))
                link(dve.tensor_tensor(s, s, a, ALU.mult))
                return s, bc(sc), v

            s, scale, v = quantise(g.xn[:], NT)
            dve.tensor_tensor(v, s, scale, ALU.mult).then_inc(quantised, 1)
            dve.wait_ge(quantised, 1)
            dve.wait_ge(loaded, 32)
            s, scale, v = quantise(w[:], 1)
            dve.tensor_tensor(v, s, scale, ALU.mult).then_inc(quantised, 1)
            for n in range(4):
                a, e = 512 * n, min(512 * n + 512, T)
                dve.wait_ge(turned, n + 1)
                dve.tensor_copy(xt[:, a:e], ps[n][:, 0:e - a]).then_inc(kept, 1)
            dve.wait_ge(turned, 5)
            dve.tensor_copy(wt[:], ps[4][:, 0:P]).then_inc(kept, 1)

        @block.tensor
        def _(pe):
            pe.wait_ge(quantised, 1)
            for n in range(4):
                for q in range(4 * n, min(4 * n + 4, NT)):
                    m = pe.transpose(ps[n][:, (q % 4) * P:(q % 4 + 1) * P], g.xn[:, q, :], g.ident[:])
                m.then_inc(turned, 1)
            pe.wait_ge(quantised, 2)
            pe.transpose(ps[4][:, 0:P], w[:, 0, :], g.ident[:]).then_inc(turned, 1)
            pe.wait_ge(kept, 5)
            for c in range(NC):
                pe.matmul(ps[c][:, 0:TC], wt[:], xt[:, c * TC:(c + 1) * TC], start=True, stop=True).then_inc(made, 1)

        @block.scalar
        def _(act):
            act.wait_ge(loaded, 32)
            for c in range(NC):
                act.wait_ge(made, c + 1)
                act.activation(g.addt[:, c * TC:(c + 1) * TC], ps[c][:, 0:TC], ACT.Identity, bias=b[:, 0:1]
                               ).then_inc(done, 1)


class Globals:
    pass


def build(nc, a, out):
    with ExitStack() as ctx:
        st = Stage(nc, ctx, "g")
        g = Globals()
        g.x, g.xn = st.sb("x", [P, NT, D]), st.sb("xn", [P, NT, D])
        g.xnt, g.addt = st.sb("xnt", [D, T + 2 * PAIR]), st.sb("addt", [D, T])
        g.ident, g.ones, g.tri = st.sb("ident", [P, P]), st.sb("ones", [P, P]), st.sb("tri", [P, P])
        g.hm8, g.hm64, g.iota8 = st.sb("hm8", [P, 16]), st.sb("hm64", [P, 2]), st.sb("iota8", [P, 8])
        g.pick_f0, g.pick_f1, g.pick_f2 = st.sb("pick_f0", [9, 768]), st.sb("pick_f1", [4, 512]), st.sb("pick_f2", [8, 2048])
        g.half = st.sb("half", [P, NT])
        g.zeros = st.sb("zeros", [P, 16])
        ctx_t = nc.dram_tensor("ctx_t", [B, CR, S], F32, kind="Internal").ap()

        constants(nc, g)
        with ExitStack() as c2:
            s2 = Stage(nc, c2, "load")
            loaded = s2.sem("loaded")
            with nc.Block() as block:
                @block.sync
                def _(sp):
                    sp.dma_start(g.x[:], a["x"].rearrange("b l d -> (b l) d").rearrange("(t p) d -> p t d", p=P)
                                 ).then_inc(loaded, 16)
                    sp.wait_ge(loaded, 16)
        context_prep(nc, g, a["ctx_768"], a["mask_BxS2_bf1"], ctx_t)
        renorm(nc, g, "n0", g.x)
        ctx_d = a["ctx_768"]

        def attend(name, **kw):
            attention(nc, g, name, ctx_d, ctx_t, **kw)

        def sub0():
            w = {k: a["L0_xattn_" + k] for k in ("Wq", "bq", "Wkv", "bkv", "Wo", "bo")}
            moves_k, moves_v = [], []
            for h in range(HEADS):
                for part, ls in ((0, moves_k), (1, moves_v)):
                    r0 = 16 * h + 8 * part
                    ls.append((lambda t, h=h: t[8 * h:8 * h + 8, 0, 0:C], w["Wkv"][r0:r0 + 8, :]))
                    ls.append((lambda t, h=h: t[8 * h:8 * h + 8, 0, C:C + 1], col(w["bkv"][r0:r0 + 8])))
            attend("a0", heads=HEADS, kc=1, scale=8.0 ** -0.5,
                   loads=[("wkT", [P, 1, CR], moves_k), ("wvT", [P, 1, CO], moves_v),
                          ("wq", [P, 1, D], [(lambda t: t[:, 0, :], w["Wq"])]),
                          ("wo_raw", [D, P], [(lambda t: t[:], w["Wo"])]), ("wo", [P, 1, D], []),
                          ("bq", [P, 1], [(lambda t: t[:], col(w["bq"]))])],
                   turns=[(lambda t: t["wo_raw"][:], P, D, lambda t: t["wo"][:, 0, :])],
                   masked={"clear": [("wkT", 0.0)], "direct": [("ob", lambda t: t[:], col(w["bo"]))]},
                   q_bias=True, o_bias=True, mask_row=False, vo_direct=False)
            renorm(nc, g, "n1", g.x, g.addt)

        def sub1():
            with ExitStack() as c2:
                s2 = Stage(nc, c2, "f0")
                lg, gw, gwt = s2.sb("lg", [P, NT, 9]), s2.sb("gw", [P, NT, 9]), s2.sb("gwt", [9, T])
                f = {k: a["L0_ffn_" + k] for k in ("gate_w", "dyn_gate_w", "dyn_up_w", "dyn_down_w", "sh_gate_w",
                                                   "sh_up_w", "sh_down_w")}
                logits(nc, g, "f0l", g.xnt, 9, f["gate_w"], None, False, lg[:])
                route_mixer(nc, g, lg, gw)
                turn_weights(nc, g, "f0t", 9, gw, gwt)
                fl = lambda x: x.rearrange("e i d -> (e i) d")
                gated_mlp(nc, g, "f0m", 6,
                          [(0, 0, 4, fl(f["dyn_gate_w"])), (1, 0, 4, fl(f["dyn_up_w"])),
                           (0, 4, 2, fl(f["sh_gate_w"])), (1, 4, 2, fl(f["sh_up_w"]))],
                          [(0, 4, f["dyn_down_w"]), (4, 2, f["sh_down_w"])], g.pick_f0, 9, gwt)
            renorm(nc, g, "n2", g.x, g.addt)

        def sub2():

            w = {k: a["L1_xattn_" + k] for k in ("Wq", "Wk", "Wv", "Wo", "bo")}
            turns = []
            for k in range(8):
                s = slice(k * P, (k + 1) * P)
                turns += [(lambda t, s=s: t["wk_raw"][:, s], P, C, lambda t, k=k: t["wkT"][:, k, 0:C]),
                          (lambda t, s=s: t["wv_raw"][:, s], P, C, lambda t, k=k: t["wvT"][:, k, 0:C]),
                          (lambda t, s=s: t["wq_raw"][:, s], P, D, lambda t, k=k: t["wq"][:, k, :])]
            attend("a1", heads=HEADS, kc=8, scale=64.0 ** -0.5,
                   loads=[("wkT", [P, 8, CR], []), ("wvT", [P, 8, CO], []), ("wq", [P, 8, D], []),
                          ("wk_raw", [C, 1024], [(lambda t: t[:], w["Wk"])]),
                          ("wv_raw", [C, 1024], [(lambda t: t[:], w["Wv"])]),
                          ("wq_raw", [D, 1024], [(lambda t: t[:], w["Wq"])]),
                          ("wo", [P, 8, D], [(lambda t: t[:], w["Wo"].rearrange("(k p) e -> p k e", p=P))])],
                   turns=turns,
                   masked={"clear": [("wkT", 0.0), ("wvT", 0.0), ("cb", 0.0)],
                           "direct": [("ob", lambda t: t[:], col(w["bo"]))]},
                   q_bias=False, o_bias=True, mask_row=False, vo_direct=False)
            renorm(nc, g, "n3", g.x, g.addt)

        def sub3():
            with ExitStack() as c2:
                s2 = Stage(nc, c2, "f1")
                hid, hid_t = s2.sb("hid", [P, NT, D]), s2.sb("hid_t", [D, T])
                lg, gw, gwt, gs = s2.sb("lg", [P, NT, 4]), s2.sb("gw", [P, NT, 4]), s2.sb("gwt", [4, T]), s2.sb("gs", [P, NT])
                copied = s2.sem("copied")
                with nc.Block() as block:
                    @block.vector
                    def _(dve):
                        dve.tensor_copy(hid[:], g.xn[:]).then_inc(copied, 1)
                f = {k: a["L1_ffn_" + k] for k in ("router_w", "router_b", "ln_g", "ln_b", "w1", "b1", "w2", "b2")}
                for m in range(4):
                    if m == 0:
                        renorm(nc, g, f"m{m}n", hid, raw_t=hid_t)
                    else:
                        renorm(nc, g, f"m{m}n", hid, g.addt, scale=gs, raw_t=hid_t)
                    logits(nc, g, f"m{m}l", hid_t, 4, f["router_w"][m], f["router_b"][m], True, lg[:])
                    route_top2(nc, g, f"m{m}r", lg[:], 4, True, gw[:], gs[:])
                    turn_weights(nc, g, f"m{m}t", 4, gw, gwt)
                    moe_layer(nc, g, f"m{m}f", f["w1"][m], f["w2"][m], f["b1"][m], f["b2"][m], f["ln_g"][m], f["ln_b"][m],
                              gwt)
                renorm(nc, g, "m4n", hid, g.addt, scale=gs, raw_t=g.addt, norm=False)
            renorm(nc, g, "n4", g.x, g.addt)

        def sub4():

            w = {k: a["L2_xattn_" + k] for k in ("Wq", "Wk", "Wv", "Wo")}
            attend("a2", heads=HEADS, kc=1, scale=8.0 ** -0.5,
                   loads=[("wkT", [P, 1, CR], []), ("wvT", [P, 1, CO], []), ("wq", [P, 1, D], []),
                          ("wk_raw", [C, P], [(lambda t: t[:], w["Wk"])]),
                          ("wv_raw", [C, P], [(lambda t: t[:], w["Wv"])]),
                          ("wq_raw", [D, P], [(lambda t: t[:], w["Wq"])]),
                          ("wo", [P, 1, D], [(lambda t: t[:, 0, :], w["Wo"])])],
                   turns=[(lambda t: t["wk_raw"][:], P, C, lambda t: t["wkT"][:, 0, 0:C]),
                          (lambda t: t["wv_raw"][:], P, C, lambda t: t["wvT"][:, 0, 0:C]),
                          (lambda t: t["wq_raw"][:], P, D, lambda t: t["wq"][:, 0, :])],
                   masked={"clear": [("wkT", 0.0), ("wvT", 0.0), ("cb", 0.0), ("ob", 0.0)], "direct": []},
                   q_bias=False, o_bias=False, mask_row=True, vo_direct=False)
            renorm(nc, g, "n5", g.x, g.addt)

        def sub5():
            with ExitStack() as c2:
                s2 = Stage(nc, c2, "f2")
                lg, gw, gwt = s2.sb("lg", [P, NT, 8]), s2.sb("gw", [P, NT, 8]), s2.sb("gwt", [8, T])
                f = {k: a["L2_ffn_" + k] for k in ("Wg", "W1", "W2", "W3")}
                logits(nc, g, "f2l", g.xnt, 8, f["Wg"], None, False, lg[:])
                route_top2(nc, g, "f2r", lg[:], 8, False, gw[:], None)
                turn_weights(nc, g, "f2t", 8, gw, gwt)
                fl = lambda x: x.rearrange("e i d -> (e i) d")
                gated_mlp(nc, g, "f2m", 16, [(0, 0, 16, fl(f["W1"])), (1, 0, 16, fl(f["W2"]))], [(0, 16, f["W3"])],
                          g.pick_f2, 8, gwt)
            renorm(nc, g, "n6", g.x, g.addt)

        def sub6():

            w = {k: a["L3_xattn_" + k] for k in ("Wq", "bq", "Wk", "bk", "Wv", "bv")}
            attend("a3", heads=1, kc=1, scale=1.0,
                   loads=[("wkT", [P, 1, CR], [(lambda t: t[:, 0, C:C + 1], col(w["bk"]))]), ("wq", [P, 1, D], []),
                          ("wk_raw", [C, P], [(lambda t: t[:], w["Wk"])]),
                          ("wq_raw", [D, P], [(lambda t: t[:], w["Wq"])]),
                          ("bq", [P, 1], [(lambda t: t[:], col(w["bq"]))])],
                   turns=[(lambda t: t["wk_raw"][:], P, C, lambda t: t["wkT"][:, 0, 0:C]),
                          (lambda t: t["wq_raw"][:], P, D, lambda t: t["wq"][:, 0, :])],
                   masked={"clear": [("wkT", 0.0), ("ob", 0.0)],
                           "direct": [("vo", lambda t: t[0:C, 0, :], w["Wv"]),
                                      ("vo", lambda t: t[C:CO, 0, :], w["bv"].rearrange("(o e) -> o e", o=1))]},
                   q_bias=True, o_bias=False, mask_row=False, vo_direct=True)
            renorm(nc, g, "n7", g.x, g.addt)

        def sub7():
            mx_linear(nc, g, a["L3_ffn_weight"], a["L3_ffn_bias"])
            renorm(nc, g, "n8", g.x, g.addt, norm=False)

        for k, sub in enumerate((sub0, sub1, sub2, sub3, sub4, sub5, sub6, sub7)):
            if ONLY is None or k in ONLY:
                sub()
        with ExitStack() as c2:
            s2 = Stage(nc, c2, "store")
            stored = s2.sem("stored")
            with nc.Block() as block:
                @block.sync
                def _(sp):
                    sp.dma_start(out.rearrange("b l d -> (b l) d").rearrange("(t p) d -> p t d", p=P), g.x[:]
                                 ).then_inc(stored, 16)
                    sp.wait_ge(stored, 16)


_INS = ["x", "ctx_768", "mask_BxS2_bf1", "L0_xattn_Wq", "L0_xattn_bq", "L0_xattn_Wkv", "L0_xattn_bkv", "L0_xattn_Wo",
        "L0_xattn_bo", "L0_ffn_gate_w", "L0_ffn_dyn_gate_w", "L0_ffn_dyn_up_w", "L0_ffn_dyn_down_w",
        "L0_ffn_sh_gate_w", "L0_ffn_sh_up_w", "L0_ffn_sh_down_w", "L1_xattn_Wq", "L1_xattn_Wk", "L1_xattn_Wv",
        "L1_xattn_Wo", "L1_xattn_bo", "L1_ffn_router_w", "L1_ffn_router_b", "L1_ffn_ln_g", "L1_ffn_ln_b", "L1_ffn_w1",
        "L1_ffn_b1", "L1_ffn_w2", "L1_ffn_b2", "L2_xattn_Wq", "L2_xattn_Wk", "L2_xattn_Wv", "L2_xattn_Wo",
        "L2_ffn_Wg", "L2_ffn_W1", "L2_ffn_W2", "L2_ffn_W3", "L3_xattn_Wq", "L3_xattn_bq", "L3_xattn_Wk",
        "L3_xattn_bk", "L3_xattn_Wv", "L3_xattn_bv", "L3_ffn_weight", "L3_ffn_bias"]


def kernel(**inputs):
    import numpy as _np
    import concourse.bacc as _bacc
    from concourse import mybir as _mybir
    from concourse.bass_utils import run_bass_kernel_spmd as _run

    nc = _bacc.Bacc("TRN2", target_bir_lowering=False, num_devices=1)
    arrays, args = {}, {}
    for name in _INS:
        a = _np.ascontiguousarray(inputs[name])
        if a.dtype.kind == "b":
            a = a.view(_np.uint8)
        arrays[f"in_{name}"] = a
        args[name] = nc.dram_tensor(f"in_{name}", a.shape, _mybir.dt.from_np(a.dtype), kind="ExternalInput").ap()
    out = nc.dram_tensor("out_0", (B, L, D), F32, kind="ExternalOutput").ap()
    build(nc, args, out)
    r = _run(nc, [arrays], core_ids=[0])
    return r.results[0]["out_0"]
```

```python
from contextlib import ExitStack

import concourse.bass as bass
from concourse import mybir

F32 = mybir.dt.float32
F32R = mybir.dt.float32r
U8 = mybir.dt.uint8
U32 = mybir.dt.uint32
ALU = mybir.AluOpType
ACT = mybir.ActivationFunctionType
AX = mybir.AxisListType

P = 128
D = 128
B, L = 32, 56
S, C = 1500, 96
T = B * L
NT = T // P
KT, NK = 12, 125
BANKS, BK = 3, 500
GT = KT // BANKS
CR = C + 2
CO = C + 1
PAIR = 2 * L
NP = B // 2
TC = 448
NC = T // TC
BIG = 1.5 * 2.0 ** 127
EPS = 1e-5
HEADS = 16
CAP = 280
LOW = 32
ROUND = 12582912.0


class Stage:

    def __init__(self, nc, ctx, name):
        self.nc, self.ctx, self.name, self.sems = nc, ctx, name, []
        ctx.callback(self.release)

    def release(self):
        if self.sems:
            self.nc.clear_and_free_semaphores(self.sems)
            self.nc.all_engine_barrier()

    def sb(self, name, shape, dt=F32):
        return self.ctx.enter_context(self.nc.sbuf_tensor(f"{self.name}_{name}", shape, dt))

    def ps(self, name, shape):
        return self.ctx.enter_context(self.nc.psum_tensor(f"{self.name}_{name}", shape, F32))

    def sem(self, name):
        self.sems.append(self.nc.alloc_semaphore(f"{self.name}_{name}"))
        return self.sems[-1]


def chain(eng, sem):
    count = [0]

    def link(ins):
        count[0] += 1
        ins.then_inc(sem, 1)
        eng.wait_ge(sem, count[0])

    return link


def constants(nc, g):
    with ExitStack() as ctx:
        st = Stage(nc, ctx, "const")
        cleared, dved = st.sem("cleared"), st.sem("dve")
        block = ctx.enter_context(nc.Block())

        @block.vector
        def _(dve):
            link = chain(dve, dved)
            link(dve.memset(g.ones[:], 1.0))
            link(dve.memset(g.zeros[:], 0.0))
            link(dve.memset(g.xnt[:, T:T + 2 * PAIR], 0.0))
            link(dve.memset(g.half[:], -0.5))

        @block.gpsimd
        def _(pool):
            pool.memset(g.ident[:], 0.0).then_inc(cleared, 1)
            pool.memset(g.tri[:], 1.0).then_inc(cleared, 1)
            pool.memset(g.hm8[:], 1.0).then_inc(cleared, 1)
            pool.memset(g.hm64[:], 1.0).then_inc(cleared, 1)
            picks = ((g.pick_f0, 12, 64), (g.pick_f1, ME, 128), (g.pick_f2, 8, 256))
            for tile, _, _ in picks:
                pool.memset(tile[:], 1.0).then_inc(cleared, 1)
            pool.iota(g.iota8[:], [[1, 8]], base=0, channel_multiplier=0,
                      allow_small_or_imprecise_dtypes=True).then_inc(cleared, 1)
            pool.wait_ge(cleared, 8)
            pool.affine_select(out=g.ident[:], in_=g.ident[:], compare_op=ALU.not_equal, fill=1.0, base=0,
                               pattern=[[-1, P]], channel_multiplier=1).then_inc(cleared, 1)
            pool.affine_select(out=g.tri[:], in_=g.tri[:], compare_op=ALU.is_ge, fill=0.0, base=0,
                               pattern=[[1, P]], channel_multiplier=-1).then_inc(cleared, 1)

            def band(tile, cols, width, n):
                pool.affine_select(out=tile, in_=tile, compare_op=ALU.is_ge, fill=0.0, base=0,
                                   pattern=[[-width, cols]], channel_multiplier=1).then_inc(cleared, 1)
                pool.wait_ge(cleared, n + 1)
                pool.affine_select(out=tile, in_=tile, compare_op=ALU.is_ge, fill=0.0, base=width - 1,
                                   pattern=[[width, cols]], channel_multiplier=-1).then_inc(cleared, 1)

            band(g.hm8[:], 16, 8, 10)
            band(g.hm64[:], 2, 64, 12)
            for tile, cols, width in picks:
                v = tile[:].rearrange("e (c w) -> e c w", w=width)
                pool.affine_select(out=v, in_=v, compare_op=ALU.is_equal, fill=0.0, base=0,
                                   pattern=[[-1, cols], [0, width]], channel_multiplier=1).then_inc(cleared, 1)
            pool.wait_ge(cleared, 17)
            pool.tensor_copy(g.pick_f0[:, 9 * 64:12 * 64].rearrange("e (c w) -> e c w", w=64),
                             g.pick_f0[:, 8 * 64:9 * 64].rearrange("e (c w) -> e c w", c=1).broadcast_to([9, 3, 64])
                             ).then_inc(cleared, 1)
            pool.wait_ge(cleared, 18)


def context_prep(nc, g, ctx_d, mask_d, ctx_t):
    with ExitStack() as ctx:
        st = Stage(nc, ctx, "cprep")
        nat = st.sb("nat", [NK, 2, KT, C])
        tr = st.sb("tr", [CO, 2, S])
        mask8, maskf = st.sb("mask8", [B, S], U8), st.sb("maskf", [B, S])
        ps = [st.ps(f"ps{n}", [P, 512]) for n in range(6)]
        loaded = [st.sem(f"loaded{n}") for n in range(2)]
        stored = [st.sem(f"stored{n}") for n in range(2)]
        mask_in, mask_done, mask_out = st.sem("mask_in"), st.sem("mask_done"), st.sem("mask_out")
        turned, kept, ones = st.sem("turned"), st.sem("kept"), st.sem("ones")
        block = ctx.enter_context(nc.Block())
        ctx_v = ctx_d.rearrange("b (p t) c -> p b (t c)", t=KT)

        @block.sync
        def _(sp):
            sp.dma_start(mask8[:], mask_d).then_inc(mask_in, 16)
            for h in range(2):
                sp.dma_start(nat[:, h, :, :].rearrange("p t c -> p (t c)"), ctx_v[:, h, :]).then_inc(loaded[h], 16)
            sp.wait_ge(mask_done, 2)
            sp.dma_start(ctx_t[:, C + 1, :], maskf[:]).then_inc(mask_out, 16)

            with sp.Fori(1, NP) as i:
                for h in range(2):
                    sp.wait_ge(turned, 6 * i - 3 + 3 * h - 0)
                    sp.dma_start(nat[:, h, :, :].rearrange("p t c -> p (t c)"),
                                 ctx_v[:, bass.ds(2 * i + h, 1), :].rearrange("p o c -> p (o c)")
                                 ).then_inc(loaded[h], 16)
            sp.wait_ge(mask_out, 16)

        @block.tensor
        def _(pe):
            def pair(i, first):
                for h in range(2):
                    pe.wait_ge(loaded[h], 16 * (i + 1))
                    for k in range(BANKS):
                        if not first:
                            pe.wait_ge(kept, 6 * i + 3 * h + k - 5)
                        for q in range(GT):
                            m = pe.transpose(ps[3 * h + k][0:C, q * NK:(q + 1) * NK], nat[:, h, k * GT + q, :],
                                             g.ident[0:NK, 0:NK])
                        m.then_inc(turned, 1)
            pair(0, True)
            with pe.Fori(1, NP) as i:
                pair(i, False)

        @block.vector
        def _(dve):
            dve.memset(tr[C:C + 1, :, :], 1.0).then_inc(ones, 1)
            dve.wait_ge(mask_in, 16)
            dve.tensor_scalar(maskf[:].rearrange("b (t p) -> b t p", t=KT),
                              mask8[:].rearrange("b (p t) -> b t p", t=KT), -1.0, None, ALU.add
                              ).then_inc(mask_done, 1)
            dve.wait_ge(mask_done, 1)
            dve.tensor_scalar(maskf[:], maskf[:], BIG, None, ALU.mult).then_inc(mask_done, 1)

            def pair(i, first):
                for h in range(2):
                    for k in range(BANKS):
                        dve.wait_ge(turned, 6 * i + 3 * h + k + 1)
                        if not first and k == 0:
                            dve.wait_ge(stored[h], 16 * i)
                        dve.tensor_copy(tr[0:C, h, k * BK:(k + 1) * BK], ps[3 * h + k][0:C, 0:BK]).then_inc(kept, 1)
            pair(0, True)
            with dve.Fori(1, NP) as i:
                pair(i, False)

        @block.scalar
        def _(act):
            act.wait_ge(ones, 1)
            with act.Fori(0, NP) as i:
                for h in range(2):
                    act.wait_ge(kept, 6 * i + 3 * h + 3)
                    act.dma_start(ctx_t[bass.ds(2 * i + h, 1), 0:CO, :].rearrange("o r s -> (o r) s"), tr[:, h, :]
                                  ).then_inc(stored[h], 16)
            for h in range(2):
                act.wait_ge(stored[h], 16 * NP)


def renorm(nc, g, name, base, addt=None, scale=None, raw_t=None, norm=True):
    with ExitStack() as ctx:
        st = Stage(nc, ctx, name)
        xc, sq = g.xn, st.sb("sq", [P, NT, D])
        mu, var, rstd = st.sb("mu", [P, NT]), st.sb("var", [P, NT]), st.sb("rstd", [P, NT])
        psa = [st.ps(f"psa{n}", [P, 4, P]) for n in range(4)]
        psb = [st.ps(f"psb{n}", [P, 4, P]) for n in range(4)]
        turned, based, raw_turned, dved = st.sem("turned"), st.sem("based"), st.sem("raw_turned"), st.sem("dved")
        raw_kept, powed, back, varred, normed = (st.sem(x) for x in ("raw_kept", "powed", "back", "varred", "normed"))
        kept, centred, squared = st.sem("kept"), st.sem("centred"), st.sem("squared")
        groups = [(n, 4 * n, min(4 * n + 4, NT)) for n in range(4)]
        block = ctx.enter_context(nc.Block())

        def bc(x, a, b):
            return x[:, a:b].rearrange("p (t o) -> p t o", o=1).broadcast_to([P, b - a, D])

        @block.tensor
        def _(pe):
            for n, a, b in groups if addt is not None else ():
                for t in range(a, b):
                    m = pe.transpose(psa[n][:, t - a, :], addt[:, t * P:(t + 1) * P], g.ident[:])
                m.then_inc(turned, 1)
            for n, a, b in groups if raw_t is not None else ():
                if addt is not None:
                    pe.wait_ge(based, n + 1)
                for t in range(a, b):
                    m = pe.transpose(psb[n][:, t - a, :], base[:, t, :], g.ident[:])
                m.then_inc(raw_turned, 1)
            for n, a, b in groups if norm else ():
                pe.wait_ge(normed, n + 1)
                if raw_t is not None:
                    pe.wait_ge(raw_kept, n + 1)
                for t in range(a, b):
                    m = pe.transpose(psb[n][:, t - a, :], g.xn[:, t, :], g.ident[:])
                m.then_inc(back, 1)

        @block.vector
        def _(dve):
            link = chain(dve, dved)

            def variance(link, n, a, b):
                dve.wait_ge(squared, n + 1)
                link(dve.tensor_reduce(var[:, a:b], sq[:, a:b, :], AX.X, ALU.add))
                dve.tensor_scalar(var[:, a:b], var[:, a:b], 1.0 / D, EPS, ALU.mult, ALU.add).then_inc(varred, 1)

            for n, a, b in groups:
                v = base[:, a:b, :]
                if scale is not None:
                    link(dve.tensor_tensor(v, v, bc(scale, a, b), ALU.mult))
                if addt is not None:
                    dve.wait_ge(turned, n + 1)
                    dve.tensor_tensor(v, v, psa[n][:, 0:b - a, :], ALU.add).then_inc(based, 1)
                    dve.wait_ge(based, n + 1)
                if norm:
                    link(dve.tensor_reduce(mu[:, a:b], v, AX.X, ALU.add))
                    link(dve.tensor_scalar(mu[:, a:b], mu[:, a:b], 1.0 / D, None, ALU.mult))
                    dve.tensor_tensor(xc[:, a:b, :], v, bc(mu, a, b), ALU.subtract).then_inc(centred, 1)
                    if n > 0:
                        variance(link, *groups[n - 1])
            if norm:
                variance(link, *groups[-1])
            for n, a, b in groups if norm else ():
                dve.wait_ge(powed, n + 1)
                dve.tensor_tensor(g.xn[:, a:b, :], xc[:, a:b, :], bc(rstd, a, b), ALU.mult).then_inc(normed, 1)

        @block.gpsimd
        def _(pool):
            for n, a, b in groups if norm else ():
                pool.wait_ge(varred, n + 1)
                pool.tensor_tensor(rstd[:, a:b], var[:, a:b], g.half[:, a:b], ALU.pow).then_inc(powed, 1)

        @block.scalar
        def _(act):
            for n, a, b in groups:
                if norm:
                    act.wait_ge(centred, n + 1)
                    act.activation(sq[:, a:b, :], xc[:, a:b, :], ACT.Square).then_inc(squared, 1)
                if raw_t is not None:
                    act.wait_ge(raw_turned, n + 1)
                    act.activation(raw_t[:, a * P:b * P].rearrange("p (t c) -> p t c", c=P), psb[n][:, 0:b - a, :],
                                   ACT.Copy).then_inc(raw_kept, 1)
            for n, a, b in groups if norm else ():
                act.wait_ge(back, n + 1)
                act.activation(g.xnt[:, a * P:b * P].rearrange("p (t c) -> p t c", c=P), psb[n][:, 0:b - a, :],
                               ACT.Copy).then_inc(kept, 1)


def attend_by_keys_and_values(nc, g, name, ctx_t, masked, ob, wk, wq3, bq3, wv, wo4):
    nu, seq = 2 * HEADS * L // P, HEADS * L // P
    quads, dims = 4, P // HEADS
    qr, qd = HEADS * L // quads, P // quads
    total = nu * NP
    ends = [-(-qr * (x + 1) // P) - 1 for x in range(quads)]
    due = [ends[x] + 3 + x // 3 for x in range(quads)]
    tail = seq + due[-1] + 2 - nu + 1
    pitch = 352
    kr = 3 * qd + (1 if masked else 0)
    parts = 4 if masked else 3
    with ExitStack() as ctx:
        st = Stage(nc, ctx, name + "m")
        raw = st.sb("raw", [CO, 2, S])
        k_hi, k_lo = st.sb("k_hi", [P, S], F32R), st.sb("k_lo", [P, S], F32R)
        ks = st.sb("ks", [3 * qd + 1, quads, S], F32R)
        qf, qp = st.sb("qf", [3 * qd, TC]), st.sb("qp", [3 * qd, TC], F32R)
        qs = st.sb("qs", [3 * qd + 1, 2, quads * pitch], F32R)
        vals = st.sb("vals", [NK, 2, KT, P])
        prob, prob_n = st.sb("prob", [P, 2, S]), st.sb("prob_n", [P, 2, S])
        prob_t = st.sb("prob_t", [NK, KT, HEADS * L])
        bank_max, neg_max = st.sb("bank_max", [P, 2, BANKS]), st.sb("neg_max", [P, 2])
        bank_den, den, rec = st.sb("bank_den", [P, 2, BANKS]), st.sb("den", [P, 2]), st.sb("rec", [P, 2])
        own = st.sb("own", [P, quads])
        picked = st.sb("picked", [P, 2, qr])
        av = st.sb("av", [P, quads, 2, L])
        ps_s = st.ps("ps_s", [P, BANKS, 512])
        ps_t = [st.ps(f"ps_t{n}", [P, 512]) for n in range(2)]
        ps_o, ps_v, ps_q = st.ps("ps_o", [P, 512]), st.ps("ps_v", [P, 512]), st.ps("ps_q", [P, 512])
        ctxt_in = [st.sem(f"ctxt_in{h}") for h in range(2)]
        keys_in = [st.sem(f"keys_in{n}") for n in range(quads)]
        (own_made, cleared, scored, bank_maxed, maxed, exped, summed_up, inverted, scaled, turned, kept_dve, kept_act,
         summed, picked_out, av_made, k_made, high_made, k_kept, v_made, v_kept, q_made, q_biased, q_rounded, q_split,
         q_kept, projected, out_kept) = (
            st.sem(x) for x in (
                "own_made", "cleared", "scored", "bank_maxed", "maxed", "exped", "summed_up", "inverted", "scaled",
                "turned", "kept_dve", "kept_act", "summed", "picked_out", "av_made", "k_made", "high_made", "k_kept",
                "v_made", "v_kept", "q_made", "q_biased", "q_rounded", "q_split", "q_kept", "projected", "out_kept"))
        block = ctx.enter_context(nc.Block())

        def steps(eng, step):
            for u in range(nu):
                step(0, u)
            with eng.Fori(1, NP - 1) as i:
                for u in range(nu):
                    step(i, u)
            for u in range(nu):
                step(NP - 1, u)
            for u in range(tail):
                step(NP, u)

        def live(i, u, lag):
            return not isinstance(i, int) or 0 <= nu * i + u - lag < total

        def later(i, u, lag):
            return not isinstance(i, int) or nu * i + u - lag > 0

        def quads_due(i, u, lag):
            for x in range(quads):
                first = u - lag - due[x]
                if first % seq == 0 and (not isinstance(i, int) or 0 <= nu * i + first < total):
                    yield first // seq % 2, 2 * i + first // seq, x, nu * i + first + ends[x]

        def free_rows(eng, i, u):
            if not isinstance(i, int) or nu * i + u >= seq:
                last = (u % seq * P + P - 1) // qr
                eng.wait_ge(summed, quads * (2 * i + u // seq - 1) + last + 1)

        def made_in(i, u):
            n, k = 2 * i + u // seq + 1, u % seq - 1
            if k < 0 or isinstance(i, int) and n >= 2 * NP:
                return None
            return ("keys" if k < BANKS else "values", n, (u // seq + 1) % 2, k % BANKS)

        def parts_in(eng, n):
            if not isinstance(n, int) or n > 0:
                for x in range(quads):
                    eng.wait_ge(keys_in[x], 16 * parts * n)

        @block.sync
        def _(sp):
            sp.wait_ge(cleared, 2)

            def load(i, h, first):
                if not first:
                    sp.wait_ge(v_made, BANKS * (2 * i + h - 1))
                sp.dma_start(raw[:, h, :], ctx_t[bass.ds(2 * i + h, 1), 0:CO, :].rearrange("o r s -> (o r) s")
                             ).then_inc(ctxt_in[h], 16)

            def spread_keys(n, first):
                sp.wait_ge(k_kept, BANKS * (n + 1))
                for x in range(quads):
                    if not first:
                        sp.wait_ge(scored, BANKS * (seq * (n - 1) + ends[x] + 1))
                    rows = slice(x * qd, (x + 1) * qd)
                    for m, part in enumerate((k_hi, k_lo, k_hi)):
                        sp.dma_start(ks[m * qd:(m + 1) * qd, x, :].bitcast(F32), part[rows, :].bitcast(F32)
                                     ).then_inc(keys_in[x], 16)
                    if masked:
                        sp.dma_start(ks[3 * qd:kr, x, :].bitcast(F32), ctx_t[bass.ds(n, 1), C + 1, :]
                                     ).then_inc(keys_in[x], 16)

            def pair(i, last):
                if not last:
                    load(i + 1, 0, False)
                spread_keys(2 * i + 1, False)
                if not last:
                    load(i + 1, 1, False)
                    spread_keys(2 * i + 2, False)

            load(0, 0, True)
            load(0, 1, True)
            spread_keys(0, True)
            with sp.Fori(0, NP - 1) as i:
                pair(i, False)
            pair(NP - 1, True)
            for h in range(2):
                sp.wait_ge(ctxt_in[h], 16 * NP)
            for x in range(quads):
                sp.wait_ge(keys_in[x], 16 * parts * 2 * NP)

        @block.gpsimd
        def _(pool):
            def pick_queries(i, b):
                n = 2 * i + b
                pool.wait_ge(q_split, i + 1)
                if not isinstance(n, int) or n > 1:
                    pool.wait_ge(scored, BANKS * seq * (n - 1))
                rows = 3 * qd
                out = qs[0:rows, b, :].rearrange("p (x w) -> p x w", x=quads)[:, :, 0:qr]
                src = qp[:].bitcast(F32).rearrange("p (x b l) -> p x b l", x=quads, b=2)[:, :, b, :]
                pool.tensor_tensor(
                    out.rearrange("p x (h l) -> p x h l", h=quads),
                    src.rearrange("p x (h l) -> p x h l", h=1).broadcast_to([rows, quads, quads, L]),
                    own[0:rows, :].rearrange("p (x h l) -> p x h l", x=1, l=1).broadcast_to([rows, quads, quads, L]),
                    ALU.mult).then_inc(q_kept, 1)

            def step(i, u):
                if not live(i, u, 0):
                    return
                v = nu * i + u
                s = u % 2
                pool.wait_ge(inverted, v + 1)
                if later(i, u, 1):
                    pool.wait_ge(turned, BANKS * (v - 1))
                for k in range(BANKS):
                    at = slice(k * BK, (k + 1) * BK)
                    pool.tensor_tensor(prob_n[:, s, at], prob[:, s, at], rec[:, s:s + 1].broadcast_to([P, BK]), ALU.mult
                                       ).then_inc(scaled, 1)
                if u == 1 and (not isinstance(i, int) or i > 0):
                    pick_queries(i, 1)
                if u == 9 and live(i, u, -nu):
                    pick_queries(i + 1, 0)
            pool.wait_ge(cleared, 2)
            pick_queries(0, 0)
            pick_queries(0, 1)
            steps(pool, step)

        @block.tensor
        def _(pe):
            def queries(i):
                if not isinstance(i, int) or i > 1:
                    pe.wait_ge(out_kept, i - 1)
                for x in range(quads):
                    m = pe.matmul(ps_q[0:3 * qd, x * PAIR:(x + 1) * PAIR], wq3[:, x, :],
                                  g.xnt[:, bass.ds(i * PAIR, PAIR)], start=True, stop=True)
                m.then_inc(q_made, 1)

            def scores(i, u):
                v, h, w = nu * i + u, u // seq, u % seq
                xs = sorted({w * P // qr, (w * P + P - 1) // qr})
                for x in xs:
                    if x * qr >= w * P:
                        pe.wait_ge(keys_in[x], 16 * parts * (2 * i + h + 1))
                if w == 0:
                    pe.wait_ge(q_kept, 2 * i + h + 1)
                for k in range(BANKS):
                    if later(i, u, 0):
                        pe.wait_ge(exped, BANKS * (v - 1) + k + 1)
                    for x in xs:
                        at = x * pitch + w * P - x * qr
                        m = pe.matmul(ps_s[:, k, 0:BK], qs[0:kr, h, at:at + P], ks[0:kr, x, k * BK:(k + 1) * BK],
                                      start=(x == xs[0]), stop=(x == xs[-1]))
                    m.then_inc(scored, 1)

            def keys(n, h, k):
                pe.wait_ge(ctxt_in[h], 8 * (n + 2 - h))
                if k > 0:
                    pe.wait_ge(k_kept, BANKS * n + k)
                elif not isinstance(n, int) or n > 0:
                    pe.wait_ge(v_kept, BANKS * n)
                pe.matmul(ps_v[:, 0:BK], wk[:], raw[:, h, k * BK:(k + 1) * BK], start=True, stop=True
                          ).then_inc(k_made, 1)

            def values(n, h, k):
                if k > 0:
                    pe.wait_ge(v_kept, BANKS * n + k)
                else:
                    pe.wait_ge(k_kept, BANKS * (n + 1))
                for q in range(GT):
                    t = k * GT + q
                    m = pe.matmul(ps_v[0:NK, q * P:(q + 1) * P], raw[:, h, t * NK:(t + 1) * NK], wv[:],
                                  start=True, stop=True)
                m.then_inc(v_made, 1)

            def turn(i, u, k):
                v = nu * i + u
                pe.wait_ge(scaled, BANKS * v + k + 1)
                if k == 2:
                    pe.wait_ge(kept_act, 2 * v + 1)
                elif later(i, u, 0):
                    pe.wait_ge(*((kept_dve, v) if k == 0 else (kept_act, 2 * v)))
                for q in range(GT):
                    t = k * GT + q
                    m = pe.transpose(ps_t[(BANKS * u + k) % 2][0:NK, q * P:(q + 1) * P],
                                     prob_n[:, u % 2, t * NK:(t + 1) * NK], g.ident[:])
                m.then_inc(turned, 1)

            def sums(h, seq_n, n, v):
                pe.wait_ge(kept_dve, v + 1)
                pe.wait_ge(kept_act, 2 * v + 2)
                if n == 0:
                    pe.wait_ge(v_kept, BANKS * (seq_n + 1))
                done = quads * seq_n + n
                if not isinstance(done, int) or done > 0:
                    pe.wait_ge(picked_out, done)
                for k in range(BANKS):
                    for q in range(GT):
                        at = slice(q * qd, (q + 1) * qd)
                        m = pe.matmul(ps_o[at, 0:qr],
                                      vals[:, h, k * GT + q, n * qd:(n + 1) * qd],
                                      prob_t[:, k * GT + q, n * qr:(n + 1) * qr],
                                      start=(k == 0), stop=(k == BANKS - 1), tile_position=(0, q * qd))
                m.then_inc(summed, 1)

            def project(i):
                pe.wait_ge(av_made, 2 * quads * (i + 1))
                pe.wait_ge(q_biased, min(i + 2, NP) if isinstance(i, int) else i + 2)
                for n in range(quads):
                    m = pe.matmul(ps_q[:, 0:PAIR], wo4[:, n, :], av[:, n, :, :], start=(n == 0), stop=(n == quads - 1))
                m.then_inc(projected, 1)

            def step(i, u):
                what, n_next, h_next, k_next = (live(i, u, 0) and made_in(i, u)) or [None] * 4
                if live(i, u, 0):
                    scores(i, u)
                if what == "keys":
                    keys(n_next, h_next, k_next)
                if live(i, u, 2):
                    turn(i, u - 2, 0)
                    turn(i, u - 2, 1)
                for n in quads_due(i, u, 0):
                    sums(*n)
                for h, seq_n, x, _ in quads_due(i, u, 2):
                    if x == quads - 1 and h == 1:
                        project(i - 1)
                if what == "values":
                    values(n_next, h_next, k_next)
                if u == 8 and live(i, u, -nu):
                    queries(i + 1)
                if live(i, u, 2):
                    turn(i, u - 2, 2)

            queries(0)
            for k in range(BANKS):
                keys(0, 0, k)
            for k in range(BANKS):
                values(0, 0, k)
            steps(pe, step)

        @block.vector
        def _(dve):
            def queries(i):
                rows = 3 * qd
                dve.wait_ge(q_made, i + 1)
                dve.tensor_tensor(qf[:].rearrange("p (x c) -> p x c", x=quads),
                                  ps_q[0:rows, 0:TC].rearrange("p (x c) -> p x c", x=quads),
                                  bq3[:].rearrange("p (x c) -> p x c", c=1).broadcast_to([rows, quads, PAIR]), ALU.add
                                  ).then_inc(q_biased, 1)
                dve.wait_ge(q_biased, i + 1)
                if not isinstance(i, int) or i > 0:
                    dve.wait_ge(q_kept, 2 * i)
                dve.tensor_copy(qp[:], qf[:]).then_inc(q_rounded, 1)
                dve.wait_ge(q_rounded, i + 1)
                low = slice(2 * qd, rows)
                dve.tensor_tensor(qp[low, :], qf[low, :], qp[low, :].bitcast(F32), ALU.subtract).then_inc(q_split, 1)

            def low_keys(n, k):
                if k == 0:
                    parts_in(dve, n)
                dve.wait_ge(high_made, BANKS * n + k + 1)
                at = slice(k * BK, (k + 1) * BK)
                dve.tensor_tensor(k_lo[:, at], ps_v[:, 0:BK], k_hi[:, at].bitcast(F32), ALU.subtract
                                  ).then_inc(k_kept, 1)

            def maxima(i, u):
                s = u % 2
                v = nu * i + u
                for k in range(BANKS):
                    dve.wait_ge(scored, BANKS * v + k + 1)
                    dve.tensor_reduce(bank_max[:, s, k:k + 1], ps_s[:, k, 0:BK], AX.X, ALU.max).then_inc(bank_maxed, 1)
                dve.wait_ge(bank_maxed, BANKS * (v + 1))
                dve.tensor_reduce(neg_max[:, s:s + 1], bank_max[:, s, :], AX.X, ALU.max, negate=True
                                  ).then_inc(maxed, 1)

            def keep(i, u):
                v = nu * i + u
                dve.wait_ge(turned, BANKS * v + 2)
                free_rows(dve, i, u)
                at = u % seq * P
                dve.tensor_copy(prob_t[:, GT:2 * GT, at:at + P],
                                ps_t[(BANKS * u + 1) % 2][0:NK, :].rearrange("p (t r) -> p t r", t=GT)).then_inc(kept_dve, 1)

            def invert(i, u):
                s = u % 2
                v = nu * i + u
                dve.wait_ge(exped, BANKS * (v + 1))
                dve.tensor_reduce(den[:, s:s + 1], bank_den[:, s, :], AX.X, ALU.add).then_inc(summed_up, 1)
                dve.wait_ge(summed_up, v + 1)
                if later(i, u, 1):
                    dve.wait_ge(scaled, BANKS * (v - 1))
                dve.reciprocal(rec[:, s:s + 1], den[:, s:s + 1]).then_inc(inverted, 1)

            def pick(i, h, seq_n, n, v):
                done = quads * seq_n + n
                dve.wait_ge(summed, done + 1)
                dve.tensor_tensor(picked[:, n % 2, :].rearrange("p (h q) -> p h q", h=quads),
                                  ps_o[:, 0:qr].rearrange("p (h q) -> p h q", h=quads),
                                  own[:].rearrange("p (h o) -> p h o", o=1).broadcast_to([P, quads, L]), ALU.mult
                                  ).then_inc(picked_out, 1)
                dve.wait_ge(picked_out, done + 1)
                if n == 0 and h == 0 and (not isinstance(v, int) or v > nu):
                    dve.wait_ge(projected, i)
                dve.tensor_reduce(av[:, n, h, :], picked[:, n % 2, :].rearrange("p (h q) -> p q h", h=quads), AX.X,
                                  ALU.add).then_inc(av_made, 1)

            def step(i, u):
                for n in quads_due(i, u, 1):
                    if n[2] == quads - 1:
                        pick(i, *n)
                if live(i, u, 0):
                    maxima(i, u)
                if live(i, u, 1):
                    invert(i, u - 1)
                if live(i, u, 2):
                    keep(i, u - 2)
                if live(i, u, 0) and made_in(i, u) and made_in(i, u)[0] == "keys":
                    low_keys(made_in(i, u)[1], made_in(i, u)[3])
                for n in quads_due(i, u, 1):
                    if n[2] < quads - 1:
                        pick(i, *n)
                if u == 8 and live(i, u, -nu):
                    queries(i + 1)

            dve.tensor_reduce(own[:], g.hm8[:].rearrange("p (j h) -> p h j", h=quads), AX.X, ALU.add
                              ).then_inc(own_made, 1)
            dve.memset(qs[:].bitcast(F32), 0.0).then_inc(own_made, 1)
            dve.wait_ge(own_made, 2)
            dve.memset(qs[3 * qd:3 * qd + 1, :, :].rearrange("p b (x w) -> p (b x) w", x=quads)[:, :, 0:qr].bitcast(F32),
                       1.0).then_inc(cleared, 2)
            queries(0)
            for k in range(BANKS):
                low_keys(0, k)
            steps(dve, step)

        @block.scalar
        def _(act):
            def exps(i, u):
                s = u % 2
                v = nu * i + u
                act.wait_ge(maxed, v + 1)
                if later(i, u, 1):
                    act.wait_ge(scaled, BANKS * (v - 1))
                for k in range(BANKS):
                    act.activation(prob[:, s, k * BK:(k + 1) * BK], ps_s[:, k, 0:BK], ACT.Exp,
                                   bias=neg_max[:, s:s + 1], accum_out=bank_den[:, s, k:k + 1]).then_inc(exped, 1)

            def keep(i, u, k):
                v = nu * i + u
                act.wait_ge(turned, BANKS * v + k + 1)
                free_rows(act, i, u)
                at = u % seq * P
                act.activation(prob_t[:, k * GT:(k + 1) * GT, at:at + P],
                               ps_t[(BANKS * u + k) % 2][0:NK, :].rearrange("p (t r) -> p t r", t=GT),
                               ACT.Copy).then_inc(kept_act, 1)

            def high_keys(n, k):
                if k == 0:
                    parts_in(act, n)
                act.wait_ge(k_made, BANKS * n + k + 1)
                act.activation(k_hi[:, k * BK:(k + 1) * BK], ps_v[:, 0:BK], ACT.Copy).then_inc(high_made, 1)

            def keep_values(n, h, k):
                act.wait_ge(v_made, BANKS * n + k + 1)
                if not isinstance(n, int) or n > 1:
                    act.wait_ge(summed, quads * (n - 1))
                act.activation(vals[:, h, k * GT:(k + 1) * GT, :],
                               ps_v[0:NK, :].rearrange("p (t r) -> p t r", t=GT), ACT.Copy).then_inc(v_kept, 1)

            def out(i):
                act.wait_ge(projected, i + 1)
                act.activation(g.addt[:, bass.ds(i * PAIR, PAIR)], ps_q[:, 0:PAIR], ACT.Identity,
                               bias=ob[:, 0:1]).then_inc(out_kept, 1)

            def step(i, u):
                what, n, h, k = (live(i, u, 0) and made_in(i, u)) or [None] * 4
                if what == "keys":
                    high_keys(n, k)
                if live(i, u, 2):
                    keep(i, u - 2, 0)
                if live(i, u, 0):
                    exps(i, u)
                for h_done, _, x, _ in quads_due(i, u, 2):
                    if x == quads - 1 and h_done == 1:
                        out(i - 1)
                if what == "values":
                    keep_values(n, h, k)
                if live(i, u, 2):
                    keep(i, u - 2, 2)

            for k in range(BANKS):
                high_keys(0, k)
            for k in range(BANKS):
                keep_values(0, 0, k)
            steps(act, step)


def attention(nc, g, name, ctx_d, ctx_t, heads, kc, scale, loads, turns, masked, q_bias, mask_row, vo_direct):
    hc = heads // kc
    by_values = heads == HEADS and kc == 1
    with ExitStack() as outer:
        so = Stage(nc, outer, name)
        if by_values:
            wk, wv = so.sb("wk", [CO, P]), so.sb("wv", [CO, P])
            wq3, cb = so.sb("wq3", [P, 4, 96]), so.sb("bq3", [96, 4])
            wo4 = so.sb("wo4", [P, 4, D])
        else:
            a_w = so.sb("a", [P, heads, CR])
            vo = so.sb("vo", [CO, heads, D])
            cb = so.sb("cb", [CR, heads])
        ob = so.sb("ob", [P, 1])

        with ExitStack() as ctx:
            st = Stage(nc, ctx, name + "w")
            buf = {n: st.sb(n, shape) for n, shape, _ in loads}
            if not by_values:
                wkm, wvm = st.sb("wkm", [P, heads, CR]), st.sb("wvm", [P, heads, CO])
            ps = [st.ps(f"ps{n}", [P, 512]) for n in range(8)]
            cleared, loaded, made, kept, mixed = (st.sem(x) for x in ("cleared", "loaded", "made", "kept", "masked"))
            if by_values:
                rep = st.sb("rep", [P, 4, 4, P // 4])
                tile = dict(buf, cb=cb, ob=ob)
            else:
                tile = dict(buf, wkm=wkm, wvm=wvm, a=a_w, vo=vo, cb=cb, ob=ob)
            clears = [(tile[n][:], v) for n, v in masked["clear"]]
            if mask_row and not by_values:
                clears += [(cb[C:CR, :], 1.0), (cb[C:CO, :], 0.0)]
            moves = [(tile[n], f, src) for n, _, ls in loads for f, src in ls]
            moves += [(tile[n], f, src) for n, f, src in masked["direct"]]
            jobs = [(lambda s=s: s(tile), None, w, n, lambda d=d: d(tile), 1.0) for s, w, n, d in turns]
            nturn = len(jobs)
            hg = min(hc, 5 if hc < 5 else 4)
            for k in range(0 if by_values else kc):
                for h0 in range(0, hc, hg):
                    a, b = k * hc + h0, k * hc + h0 + hg
                    jobs.append((lambda k=k: tile["wq"][:, k, :], lambda a=a, b=b: wkm[:, a:b, :], D, hg * CR,
                                 lambda a=a, b=b: a_w[:, a:b, :], scale))
            if q_bias and not by_values:
                for h in range(heads):
                    jobs.append((lambda h=h: wkm[:, h, :], lambda: tile["bq"][:, 0:1], CR, 1,
                                 lambda h=h: cb[:, h:h + 1], scale))
            if by_values:
                jobs.append((lambda: tile["wkT"][:, 0, 0:CO], None, CO, P, lambda: wk[:], 1.0))
                jobs.append((lambda: tile["wvT"][:, 0, :], None, CO, P, lambda: wv[:], 1.0))
                for n in range(4):
                    jobs.append((lambda n=n: rep[:, n, :, :], lambda: tile["wo"][:, 0, :], P, D,
                                 lambda n=n: wo4[:, n, :], 1.0))
                    jobs.append((lambda: tile["wq"][:, 0, :], lambda n=n: rep[:, n, 0:3, :], D, 96,
                                 lambda n=n: wq3[:, n, :], scale))
                    if q_bias:
                        jobs.append((lambda n=n: rep[:, n, 0:3, :], lambda: tile["bq"][:, 0:1], 96, 1,
                                     lambda n=n: cb[:, n:n + 1], scale))
            elif not vo_direct:
                for h in range(heads):
                    jobs.append((lambda h=h: wvm[:, h, :], lambda h=h: tile["wo"][:, h // hc, :], CO, D,
                                 lambda h=h: vo[:, h, :], 1.0))
            block = ctx.enter_context(nc.Block())

            @block.sync
            def _(sp):
                sp.wait_ge(cleared, len(clears))
                for t, f, src in moves:
                    with nc.allow_non_contiguous_dma(reason="biases as columns"):
                        sp.dma_start(f(t), src).then_inc(loaded, 16)
                sp.wait_ge(loaded, 16 * len(moves))

            @block.tensor
            def _(pe):
                pe.wait_ge(loaded, 16 * len(moves))
                for n, (lhs, rhs, rows, cols, _, _) in enumerate(jobs):
                    if n >= 8:
                        pe.wait_ge(kept, n - 7)
                    if n == nturn:
                        pe.wait_ge(mixed, 1 if vo_direct or by_values else 2)
                    if rhs is None:
                        src = lhs()
                        k = src.shape[0]
                        m = pe.transpose(ps[n % 8][0:rows, 0:cols], src, g.ident[0:k, 0:k])
                    else:
                        m = pe.matmul(ps[n % 8][0:rows, 0:cols], lhs(), rhs(), start=True, stop=True)
                    m.then_inc(made, 1)

            @block.vector
            def _(dve):
                for n, (t, v) in enumerate(clears):
                    dve.memset(t, v).then_inc(cleared, 1)
                    dve.wait_ge(cleared, n + 1)
                if heads == HEADS:
                    hm = g.hm8 if kc == 1 else g.hm64
                for n, (_, _, rows, cols, dst, sc) in enumerate(jobs):
                    if n == nturn:
                        dve.wait_ge(kept, nturn) if nturn else None
                        dve.wait_ge(loaded, 16 * len(moves))
                        if by_values:
                            dve.tensor_copy(rep[:], g.ident[:].rearrange("p (n o c) -> p n o c", n=4, o=1)
                                            .broadcast_to([P, 4, 4, P // 4])).then_inc(mixed, 1)
                        for q, (dst_w, src_w, w) in enumerate(() if by_values else ((wkm, "wkT", CR), (wvm, "wvT", CO))):
                            if q == 1 and vo_direct:
                                continue
                            s4 = tile[src_w][:, :, :].rearrange("p k (o c) -> p k o c", o=1)
                            d4 = dst_w[:, :, :].rearrange("p (k h) c -> p k h c", k=kc)
                            if heads == 1:
                                ins = dve.tensor_copy(d4, s4)
                            else:
                                m4 = hm[:, 0:hc].rearrange("p (k h c) -> p k h c", k=1, c=1)
                                ins = dve.tensor_tensor(d4, s4.broadcast_to([P, kc, hc, w]),
                                                        m4.broadcast_to([P, kc, hc, w]), ALU.mult)
                            ins.then_inc(mixed, 1)
                    dve.wait_ge(made, n + 1)
                    out, src = dst(), ps[n % 8][0:rows, 0:cols]
                    if len(out.shape) == 3:
                        src = src.rearrange("p (a b) -> p a b", a=out.shape[1])
                    dve.tensor_scalar(out, src, sc, None, ALU.mult).then_inc(kept, 1)

        if by_values:
            attend_by_keys_and_values(nc, g, name, ctx_t, mask_row, ob, wk, wq3, cb, wv, wo4)
            return

        full = heads == HEADS
        gp = 1 if full else 2
        ng = NP // gp
        slots = 2 * gp
        nu = 2 * HEADS * L // P if full else gp
        total = nu * ng
        tg = gp * PAIR
        hq = min(heads, TC // PAIR)
        nq = heads // hq
        width = heads * L if full else P // 2
        with ExitStack() as ctx:
            st = Stage(nc, ctx, name + "m")
            raw = st.sb("raw", [CR, slots, S])
            cxt = st.sb("cxt", [CR, slots, 2, S], F32R)
            cn = st.sb("cn", [NK, slots, KT, CO])
            q32 = st.sb("q32", [CR, TC])
            qhi, qlo = (st.sb(n, [CR, slots, width if full else P], F32R) for n in ("qhi", "qlo"))
            prob = st.sb("prob", [P, 2, S])
            prob_t = st.sb("prob_t", [NK, 2, KT, P])
            bank_max, neg_max = st.sb("bank_max", [P, 2, BANKS]), st.sb("neg_max", [P, 2])
            den, on = st.sb("den", [P, 2]), st.sb("on", [P, 2, CO])
            on_t = st.sb("on_t", [CO, slots, width])
            ps_s = st.ps("ps_s", [P, BANKS, 512])
            ps_t = [st.ps(f"ps_t{n}", [P, 512]) for n in range(2)]
            ps_o, ps_r, ps_q = st.ps("ps_o", [P, 512]), st.ps("ps_r", [P, 512]), st.ps("ps_q", [P, 512])
            ctx_in = [st.sem(f"ctx_in{h}") for h in range(slots)]
            ctxt_in = [st.sem(f"ctxt_in{h}") for h in range(slots)]
            high_made = [st.sem(f"high_made{h}") for h in range(slots)]
            low_made = [st.sem(f"low_made{h}") for h in range(slots)]
            (ones_set, scored, bank_maxed, maxed, exped, turned, kept_dve, kept_act, summed, denned, normed,
             o_turned, o_kept, q_made, q_added, q_kept, projected, out_kept) = (st.sem(x) for x in (
                 "ones_set", "scored", "bank_maxed", "maxed", "exped", "turned", "kept_dve", "kept_act", "summed",
                 "denned", "normed", "o_turned", "o_kept", "q_made", "q_added", "q_kept", "projected", "out_kept"))
            ctx_v = ctx_d.rearrange("b (p t) c -> p b t c", t=KT)
            block = ctx.enter_context(nc.Block())

            def sequences(u):
                u %= nu
                return [u * slots // nu] if full else [2 * u, 2 * u + 1]

            def first_of(u):
                return not full or u % nu % (nu // 2) == 0

            def used(h):
                return (h + 1) * nu // 2 if full else h // 2 + 1

            peel = -(-4 // nu)
            behind = 1 + 3 // nu

            def steps(eng, step):
                for i in range(peel):
                    for u in range(nu):
                        step(i, u)
                with eng.Fori(peel, ng if full else ng - 1) as i:
                    for u in range(nu):
                        step(i, u)
                if not full:
                    for u in range(nu):
                        step(ng - 1, u)
                for u in range(4):
                    step(ng, u)

            def live(i, u, lag):
                return not isinstance(i, int) or 0 <= nu * i + u - lag < total

            def later(i, u, lag):
                return not isinstance(i, int) or nu * i + u - lag > 0

            def low_part(eng, i, h):
                eng.wait_ge(high_made[h], i + 1)
                eng.tensor_tensor(cxt[:, h, 1, :], raw[:, h, :], cxt[:, h, 0, :].bitcast(F32), ALU.subtract
                                  ).then_inc(low_made[h], 1)

            @block.sync
            def _(sp):
                sp.wait_ge(ones_set, 3)

                def load_turned(i, first):
                    for h in range(slots):
                        if not first:
                            sp.wait_ge(low_made[h], i)
                        sp.dma_start(raw[:, h, :], ctx_t[bass.ds(slots * i + h, 1), :, :].rearrange("o r s -> (o r) s")
                                     ).then_inc(ctxt_in[h], 16)

                def load(i, first):
                    for h in range(slots):
                        if not first:
                            sp.wait_ge(summed, nu * i - nu + used(h))
                        sp.dma_start(cn[:, h, :, 0:C],
                                     ctx_v[:, bass.ds(slots * i + h, 1), :, :].rearrange("p o t c -> p (o t) c")
                                     ).then_inc(ctx_in[h], 16)

                load_turned(0, True)
                load_turned(1, False)
                load(0, True)
                with sp.Fori(1, ng - 1) as i:
                    load_turned(i + 1, False)
                    load(i, False)
                load(ng - 1, False)
                for h in range(slots):
                    sp.wait_ge(ctx_in[h], 16 * ng)
                    sp.wait_ge(ctxt_in[h], 16 * ng)

            @block.gpsimd
            def _(pool):
                def split(i, first):
                    for h in range(slots):
                        if full:
                            pool.wait_ge(ctxt_in[h], 16 * (i + 1))
                            if not first:
                                pool.wait_ge(scored, BANKS * (nu * i - nu + used(h)))
                            pool.tensor_tensor(cxt[:, h, 0, :], raw[:, h, :],
                                               g.zeros[0:CR, 0:1].broadcast_to([CR, S]), ALU.add).then_inc(high_made[h], 1)
                        if full or h % 2:
                            low_part(pool, i, h)
                split(0, True)
                with pool.Fori(1, ng) as i:
                    split(i, False)

            @block.tensor
            def _(pe):
                def queries(i, q):
                    n = nq * i + q
                    if not isinstance(n, int) or n > 0:
                        pe.wait_ge(q_kept, n)
                    if q == 0 and (not isinstance(i, int) or i > behind):
                        pe.wait_ge(out_kept, i - behind)
                    for h in range(hq):
                        m = pe.matmul(ps_q[0:CR, h * tg:(h + 1) * tg], a_w[:, q * hq + h, :],
                                      g.xnt[:, bass.ds(i * tg, tg)], start=True, stop=True)
                    m.then_inc(q_made, 1)

                def scores(i, u):
                    v = nu * i + u
                    for h in sequences(u) if first_of(u) else ():
                        pe.wait_ge(low_made[h], i + 1)
                    if u == 0:
                        pe.wait_ge(q_kept, nq * (i + 1))
                    for k in range(BANKS):
                        if later(i, u, 0):
                            pe.wait_ge(exped, BANKS * (v - 1) + k + 1)
                        keys = slice(k * BK, (k + 1) * BK)
                        for h in sequences(u):
                            at = (slice(u * P - h * width, (u + 1) * P - h * width)) if full else slice(0, P)
                            for part, w in ((qhi, 0), (qhi, 1), (qlo, 0)):
                                m = pe.matmul(ps_s[:, k, 0:BK], part[:, h, at], cxt[:, h, w, keys],
                                              start=(part is qhi and w == 0 and h == sequences(u)[0]),
                                              stop=(part is qlo and h == sequences(u)[-1]))
                        m.then_inc(scored, 1)

                def turn(i, u, k):
                    v = nu * i + u
                    pe.wait_ge(exped, BANKS * v + k + 1)
                    if k < 2:
                        if later(i, u, 0):
                            pe.wait_ge(*((kept_dve, 2 * v) if k == 0 else (kept_act, v)))
                    else:
                        pe.wait_ge(kept_dve, 2 * v + 1)
                    for q in range(GT):
                        t = k * GT + q
                        m = pe.transpose(ps_t[(BANKS * u + k) % 2][0:NK, q * P:(q + 1) * P],
                                         prob[:, u % 2, t * NK:(t + 1) * NK], g.ident[:])
                    m.then_inc(turned, 1)

                def sums(i, u):
                    v = nu * i + u
                    pe.wait_ge(kept_dve, 2 * v + 2)
                    pe.wait_ge(kept_act, v + 1)
                    for h in sequences(u) if first_of(u) else ():
                        pe.wait_ge(ctx_in[h], 16 * (i + 1 + (u // nu)))
                    if later(i, u, 0):
                        pe.wait_ge(normed, v)
                    hs = sequences(u)
                    part = P // len(hs)
                    for n, h in enumerate(hs):
                        at = slice(n * part, (n + 1) * part)
                        for t in range(KT):
                            m = pe.matmul(ps_o[at, 0:CO], prob_t[:, u % 2, t, at], cn[:, h, t, :],
                                          start=(t == 0), stop=(t == KT - 1))
                    m.then_inc(summed, 1)

                def o_turn(i, u):
                    v = nu * i + u
                    pe.wait_ge(normed, v + 1)
                    if later(i, u, 0):
                        pe.wait_ge(o_kept, v)
                    pe.transpose(ps_r[0:CO, 0:P], on[:, u % 2, :], g.ident[:]).then_inc(o_turned, 1)

                def project(i):
                    pe.wait_ge(o_kept, nu * (i + 1))
                    n = nq * (i + behind + 1)
                    pe.wait_ge(q_kept, min(n, nq * (ng + 1)) if isinstance(i, int) else n)
                    for h in range(heads):
                        m = pe.matmul(ps_q[:, 0:tg], vo[:, h, :], on_t[:, :, h * L:(h + 1) * L],
                                      start=(h == 0), stop=(h == heads - 1))
                    m.then_inc(projected, 1)

                def step(i, u):
                    if live(i, u, 0):
                        scores(i, u)
                    if live(i, u, 1):
                        turn(i, u - 1, 0)
                        turn(i, u - 1, 1)
                    if (u - 4) % nu == nu - 1 and live(i, u, 4):
                        project(i + (u - 4) // nu)
                    if live(i, u, 3):
                        o_turn(i, u - 3)
                    if live(i, u, 0) and u == nu - 1:
                        for q in range(nq):
                            queries(i + 1, q)
                    if live(i, u, 2):
                        sums(i, u - 2)
                    if live(i, u, 1):
                        turn(i, u - 1, 2)

                for q in range(nq):
                    queries(0, q)
                steps(pe, step)

            @block.vector
            def _(dve):
                def queries(i):
                    for q in range(nq):
                        n = nq * i + q
                        src = ps_q[0:CR, 0:hq * tg].rearrange("p (h b l) -> p b h l", h=hq, b=slots)
                        mid = q32[:, 0:hq * tg].rearrange("p (b h l) -> p b h l", b=slots, h=hq)
                        bias = cb[:, q * hq:(q + 1) * hq].rearrange("p (b h l) -> p b h l", b=1, l=1)
                        dve.wait_ge(q_made, n + 1)
                        dve.tensor_tensor(mid, src, bias.broadcast_to([CR, slots, hq, L]), ALU.add
                                          ).then_inc(q_added, 1)
                        if full:
                            cols = slice(q * hq * L, (q + 1) * hq * L)
                            views = [(qhi[:, :, cols], qlo[:, :, cols], q32[:, 0:hq * tg].rearrange(
                                "p (b c) -> p b c", b=slots))]
                        else:
                            views = [tuple(x[:, h::2, P // 2 * h:P // 2 * h + L] for x in (qhi, qlo)) +
                                     (q32[:, 0:tg].rearrange("p (b c) -> p b c", b=slots)[:, h::2, :],)
                                     for h in range(2)]
                        dve.wait_ge(q_added, (1 + len(views)) * n + 1)
                        for hi, _, x in views:
                            dve.tensor_copy(hi, x).then_inc(q_added, 1)
                        dve.wait_ge(q_added, (1 + len(views)) * (n + 1))
                        for m, (hi, lo, x) in enumerate(views):
                            ins = dve.tensor_tensor(lo, x, hi.bitcast(F32), ALU.subtract)
                        ins.then_inc(q_kept, 1)

                def maxima(i, u):
                    s = u % 2
                    v = nu * i + u
                    for k in range(BANKS):
                        dve.wait_ge(scored, BANKS * v + k + 1)
                        dve.tensor_reduce(bank_max[:, s, k:k + 1], ps_s[:, k, 0:BK], AX.X, ALU.max
                                          ).then_inc(bank_maxed, 1)
                    dve.wait_ge(bank_maxed, BANKS * (v + 1))
                    dve.tensor_reduce(neg_max[:, s:s + 1], bank_max[:, s, :], AX.X, ALU.max, negate=True
                                      ).then_inc(maxed, 1)

                def keep(i, u, k):
                    v = nu * i + u
                    dve.wait_ge(turned, BANKS * v + k + 1)
                    if later(i, u, 1):
                        dve.wait_ge(summed, v - 1)
                    dve.tensor_copy(prob_t[:, u % 2, k * GT:(k + 1) * GT, :],
                                    ps_t[(BANKS * u + k) % 2][0:NK, :].rearrange("p (t r) -> p t r", t=GT)
                                    ).then_inc(kept_dve, 1)

                def normalise(i, u):
                    s = u % 2
                    v = nu * i + u
                    dve.wait_ge(summed, v + 1)
                    dve.reciprocal(den[:, s:s + 1], ps_o[:, C:CO]).then_inc(denned, 1)
                    dve.wait_ge(denned, v + 1)
                    if later(i, u, 1):
                        dve.wait_ge(o_turned, v - 1)
                    dve.tensor_scalar(on[:, s, :], ps_o[:, 0:CO], den[:, s:s + 1], None, ALU.mult
                                      ).then_inc(normed, 1)

                def step(i, u):
                    if live(i, u, 0):
                        maxima(i, u)
                    if live(i, u, 1):
                        keep(i, u - 1, 0)
                        keep(i, u - 1, 1)
                    if live(i, u, 0) and u == nu - 1:
                        queries(i + 1)
                    if not full and live(i, u, -nu):
                        low_part(dve, i + 1, 2 * u)
                    if live(i, u, 2):
                        normalise(i, u - 2)

                dve.memset(qhi[:].bitcast(F32), 0.0).then_inc(ones_set, 1)
                dve.memset(qlo[:].bitcast(F32), 0.0).then_inc(ones_set, 1)
                dve.memset(cn[:, :, :, C:CO], 1.0).then_inc(ones_set, 1)
                dve.wait_ge(ones_set, 2)
                queries(0)
                if not full:
                    for u in range(nu):
                        low_part(dve, 0, 2 * u)
                steps(dve, step)

            @block.scalar
            def _(act):
                def high_part(i, u):
                    for h in sequences(u):
                        act.wait_ge(ctxt_in[h], 16 * (i + 1))
                        act.activation(cxt[:, h, 0, :], raw[:, h, :], ACT.Copy).then_inc(high_made[h], 1)

                def exps(i, u):
                    s = u % 2
                    v = nu * i + u
                    act.wait_ge(maxed, v + 1)
                    if later(i, u, 1):
                        act.wait_ge(turned, BANKS * (v - 1))
                    for k in range(BANKS):
                        act.activation(prob[:, s, k * BK:(k + 1) * BK], ps_s[:, k, 0:BK], ACT.Exp,
                                       bias=neg_max[:, s:s + 1]).then_inc(exped, 1)

                def keep(i, u):
                    v = nu * i + u
                    act.wait_ge(turned, BANKS * (v + 1))
                    if later(i, u, 1):
                        act.wait_ge(summed, v - 1)
                    act.activation(prob_t[:, u % 2, 2 * GT:KT, :],
                                   ps_t[(BANKS * u + 2) % 2][0:NK, :].rearrange("p (t r) -> p t r", t=GT),
                                   ACT.Copy).then_inc(kept_act, 1)

                def o_keep(i, u):
                    v = nu * i + u
                    act.wait_ge(o_turned, v + 1)
                    if u % nu == 0 and (not isinstance(i, int) or v > 0):
                        act.wait_ge(projected, i + u // nu)
                    flat = on_t[:].rearrange("p b c -> p (b c)")
                    act.activation(flat[:, u % nu * P:(u % nu + 1) * P], ps_r[0:CO, 0:P], ACT.Copy
                                   ).then_inc(o_kept, 1)

                def out(i):
                    act.wait_ge(projected, i + 1)
                    act.activation(g.addt[:, bass.ds(i * tg, tg)], ps_q[:, 0:tg], ACT.Identity,
                                   bias=ob[:, 0:1]).then_inc(out_kept, 1)

                def step(i, u):
                    if live(i, u, 0):
                        exps(i, u)
                    if (u - 4) % nu == nu - 1 and live(i, u, 4):
                        out(i + (u - 4) // nu)
                    if live(i, u, 3):
                        o_keep(i, u - 3)
                    if live(i, u, 1):
                        keep(i, u - 1)
                    if not full and live(i, u, -nu):
                        high_part(i + 1, u)

                if not full:
                    for u in range(nu):
                        high_part(0, u)
                steps(act, step)


def head_rows(x, part):
    if len(x.shape) == 2:
        return x.rearrange("(h k d) c -> k h d c", h=HEADS, k=2)[part]
    return x.rearrange("(h k d) -> k h d", h=HEADS, k=2)[part]


def col(x):
    return x.rearrange("(p o) -> p o", o=1)


def spread(x, n):
    return x.rearrange("p (t o) -> p t o", o=1).broadcast_to([P, NT, n])


def logits_of(nc, g, name, xt, experts, w, bias, loaded, out):
    with ExitStack() as ctx:
        st = Stage(nc, ctx, name)
        psl = st.ps("psl", [P, NT, experts])
        made, done = st.sem("made"), st.sem("done")
        block = ctx.enter_context(nc.Block())

        @block.tensor
        def _(pe):
            pe.wait_ge(loaded, 32)
            for t in range(NT):
                pe.matmul(psl[:, t, :], g.ones[0:1, :], bias, start=True, stop=False)
                m = pe.matmul(psl[:, t, :], xt[:, t * P:(t + 1) * P], w, start=False, stop=True)
            m.then_inc(made, 1)

        @block.vector
        def _(dve):
            dve.wait_ge(made, 1)
            dve.tensor_copy(out, psl[:, :, :]).then_inc(done, 1)


def logits(nc, g, name, xt, experts, w_dram, b_dram, w_turned, out):
    with ExitStack() as ctx:
        st = Stage(nc, ctx, name)
        raw, w, bias = st.sb("raw", [16, D]), st.sb("w", [D, experts]), st.sb("bias", [1, experts])
        psw, psl = st.ps("psw", [P, 512]), st.ps("psl", [P, NT, experts])
        loaded, turned, kept, made, done = (st.sem(x) for x in ("loaded", "turned", "kept", "made", "done"))
        n_in = 1 + (b_dram is not None)
        block = ctx.enter_context(nc.Block())

        @block.sync
        def _(sp):
            if b_dram is not None:
                sp.dma_start(bias[:], b_dram.rearrange("(o e) -> o e", o=1)).then_inc(loaded, 16)
            sp.dma_start(w[:] if w_turned else raw[0:experts, :], w_dram).then_inc(loaded, 16)
            sp.wait_ge(loaded, 16 * n_in)

        @block.tensor
        def _(pe):
            pe.wait_ge(loaded, 16 * n_in)
            if not w_turned:
                pe.transpose(psw[:, 0:experts], raw[0:experts, :], g.ident[0:experts, 0:experts]).then_inc(turned, 1)
                pe.wait_ge(kept, 1)
            for t in range(NT):
                if b_dram is not None:
                    pe.matmul(psl[:, t, :], g.ones[0:1, :], bias[:], start=True, stop=False)
                m = pe.matmul(psl[:, t, :], xt[:, t * P:(t + 1) * P], w[:], start=b_dram is None, stop=True)
            m.then_inc(made, 1)

        @block.vector
        def _(dve):
            if not w_turned:
                dve.wait_ge(turned, 1)
                dve.tensor_copy(w[:], psw[:, 0:experts]).then_inc(kept, 1)
            dve.wait_ge(made, 1)
            dve.tensor_copy(out, psl[:, :, :]).then_inc(done, 1)


def turn_weights(nc, g, name, experts, src, dst, pick=None, pick_r=None):
    with ExitStack() as ctx:
        st = Stage(nc, ctx, name)
        ps = [st.ps(f"ps{n}", [P, 512]) for n in range(4)]
        cleared, made, high, kept, picked = (st.sem(x) for x in ("cleared", "made", "high", "kept", "picked"))
        block = ctx.enter_context(nc.Block())

        @block.tensor
        def _(pe):
            for n in range(4):
                for t in range(4 * n, min(4 * n + 4, NT)):
                    m = pe.transpose(ps[n][0:experts, (t % 4) * P:(t % 4 + 1) * P], src[:, t, :], g.ident[:])
                m.then_inc(made, 1)

        @block.scalar
        def _(act):
            if pick_r is not None:
                act.wait_ge(cleared, 2)
                act.activation(pick_r[0:experts, :], pick, ACT.Copy).then_inc(picked, 1)
                act.activation(pick_r[LOW:LOW + experts, :], pick, ACT.Copy).then_inc(picked, 1)

        @block.vector
        def _(dve):
            dve.memset(dst[:].bitcast(F32), 0.0).then_inc(cleared, 1)
            if pick_r is not None:
                dve.memset(pick_r[:].bitcast(F32), 0.0).then_inc(cleared, 1)
            dve.wait_ge(cleared, 1)
            for n in range(4):
                a, b = 512 * n, min(512 * n + 512, T)
                dve.wait_ge(made, n + 1)
                dve.tensor_copy(dst[0:experts, a:b], ps[n][0:experts, 0:b - a]).then_inc(high, 1)
            for n in range(4):
                a, b = 512 * n, min(512 * n + 512, T)
                dve.wait_ge(high, n + 1)
                dve.tensor_tensor(dst[LOW:LOW + experts, a:b], ps[n][0:experts, 0:b - a],
                                  dst[0:experts, a:b].bitcast(F32), ALU.subtract).then_inc(kept, 1)


def route_mixer(nc, g, full, gw):
    with ExitStack() as ctx:
        st = Stage(nc, ctx, "mixer")
        t8 = lambda n: st.sb(n, [P, NT, 8])
        t1 = lambda n: st.sb(n, [P, NT])
        dyn, top, ptop, idx = t8("dyn"), t8("top"), t8("ptop"), st.sb("idx", [P, NT, 8], U32)
        idxf, mag, hot, alive, e1, e2, e3, rw, mask = (t8(n) for n in (
            "idxf", "mag", "hot", "alive", "e1", "e2", "e3", "rw", "mask"))
        s1, s2, csum, valid = t1("s1"), t1("s2"), t1("csum"), t1("valid")
        w9, carry = st.sb("w9", [P, NT, 9]), st.sb("carry", [P, NT, 8])
        ps = st.ps("ps", [P, 512])
        pst = st.ps("pst", [P, 512])
        dved, asked, exped, masked, counted = (st.sem(x) for x in ("dved", "asked", "exped", "masked", "counted"))
        block = ctx.enter_context(nc.Block())
        exps = []

        @block.vector
        def _(dve):
            link = chain(dve, dved)

            def exp(tile):
                exps.append(tile)
                dve.wait_ge(exped, len(exps))

            def tt(out, a, b, op):
                link(dve.tensor_tensor(out, a, b, op))

            def ask(ins):
                ins.then_inc(asked, 1)

            link(dve.tensor_copy(dyn[:], full[:, :, 0:8]))
            for t in range(NT):
                dve.max(top[:, t, :], dyn[:, t, :]).then_inc(dved, 1)
            dve.wait_ge(dved, 1 + NT)
            for t in range(NT):
                dve.max_index(idx[:, t, :], top[:, t, :], dyn[:, t, :]).then_inc(dved, 1)
            dve.wait_ge(dved, 1 + 2 * NT)
            done = [1 + 2 * NT]

            def link(ins):
                done[0] += 1
                ins.then_inc(dved, 1)
                dve.wait_ge(dved, done[0])

            link(dve.tensor_copy(idxf[:], idx[:]))
            link(dve.scalar_tensor_tensor(mag[:], dyn[:], -1.0, dyn[:], ALU.mult, ALU.max))
            ask(dve.tensor_tensor(ptop[:], top[:], top[:, :, 0:1].broadcast_to([P, NT, 8]), ALU.subtract))
            exp(ptop[:])
            link(dve.tensor_reduce(s1[:], ptop[:], AX.X, ALU.add))
            link(dve.reciprocal(s1[:], s1[:]))
            link(dve.tensor_tensor(ptop[:], ptop[:], spread(s1[:], 8), ALU.mult))
            link(dve.memset(csum[:], 0.0))
            link(dve.memset(alive[:], 1.0))
            link(dve.memset(rw[:], 0.0))
            for k in range(4):
                thr = top[:, :, k:k + 1].broadcast_to([P, NT, 8])
                link(dve.tensor_scalar(valid[:], csum[:], 0.75, None, ALU.is_lt))
                link(dve.tensor_tensor(csum[:], csum[:], ptop[:, :, k], ALU.add))
                link(dve.tensor_tensor(hot[:], idxf[:, :, k:k + 1].broadcast_to([P, NT, 8]),
                                       g.iota8[:].rearrange("p (o e) -> p o e", o=1).broadcast_to([P, NT, 8]),
                                       ALU.is_equal))
                link(dve.tensor_tensor(e1[:], thr, dyn[:], ALU.subtract))
                link(dve.tensor_scalar(s2[:], top[:, :, k], -1.0, None, ALU.mult))
                link(dve.tensor_tensor(s2[:], s2[:], top[:, :, k], ALU.max))
                link(dve.tensor_tensor(e2[:], mag[:], spread(s2[:], 8), ALU.max))
                link(dve.tensor_scalar(e2[:], e2[:], 1e-37, None, ALU.max))
                link(dve.reciprocal(e2[:], e2[:]))
                link(dve.tensor_tensor(e2[:], e1[:], e2[:], ALU.mult))
                link(dve.tensor_scalar(e2[:], e2[:], 0.2, None, ALU.is_le))
                link(dve.tensor_tensor(e2[:], e2[:], alive[:], ALU.mult))
                ask(dve.tensor_scalar(e3[:], e1[:], 0.0, -1.0, ALU.max, ALU.mult))
                exp(e3[:])
                link(dve.tensor_tensor(e3[:], e3[:], e2[:], ALU.mult))
                link(dve.tensor_reduce(s1[:], e3[:], AX.X, ALU.add))
                link(dve.reciprocal(s1[:], s1[:]))
                link(dve.tensor_tensor(s1[:], s1[:], valid[:], ALU.mult))
                link(dve.tensor_tensor(e1[:], hot[:], spread(s1[:], 8), ALU.mult))
                link(dve.tensor_tensor(rw[:], rw[:], e1[:], ALU.add))
                link(dve.tensor_tensor(alive[:], alive[:], hot[:], ALU.subtract))
            link(dve.tensor_reduce(s1[:], rw[:], AX.X, ALU.add))
            link(dve.reciprocal(s1[:], s1[:]))
            link(dve.tensor_tensor(rw[:], rw[:], spread(s1[:], 8), ALU.mult))
            dve.tensor_scalar(mask[:], rw[:], 0.0, None, ALU.is_gt).then_inc(masked, 1)
            dve.wait_ge(counted, 1)
            link(dve.memset(carry[:, 0, :], 0.0))
            for t in range(1, NT):
                link(dve.tensor_tensor(carry[:, t, :], carry[:, t - 1, :], pst[:, (t - 1) * 8:t * 8], ALU.add))
            link(dve.tensor_tensor(carry[:], carry[:], ps[:, 0:NT * 8].rearrange("p (t e) -> p t e", e=8), ALU.add))
            link(dve.tensor_scalar(carry[:], carry[:], float(CAP), None, ALU.is_le))
            dve.wait_ge(masked, 1)
            link(dve.tensor_tensor(mask[:], mask[:], carry[:], ALU.mult))
            link(dve.tensor_scalar(e1[:], mask[:], -1.0, BIG, ALU.add, ALU.mult))
            link(dve.tensor_tensor(w9[:, :, 0:8], dyn[:], e1[:], ALU.add))
            link(dve.tensor_copy(w9[:, :, 8:9], full[:, :, 8:9]))
            link(dve.tensor_reduce(s1[:], w9[:], AX.X, ALU.max))
            ask(dve.tensor_tensor(w9[:], w9[:], spread(s1[:], 9), ALU.subtract))
            exp(w9[:])
            link(dve.tensor_reduce(s1[:], w9[:], AX.X, ALU.add))
            link(dve.reciprocal(s1[:], s1[:]))
            link(dve.tensor_tensor(w9[:], w9[:], spread(s1[:], 9), ALU.mult))
            link(dve.tensor_reduce(s1[:], w9[:, :, 0:8], AX.X, ALU.add))
            link(dve.tensor_tensor(rw[:], rw[:], spread(s1[:], 8), ALU.mult))
            link(dve.tensor_tensor(gw[:, :, 0:8], rw[:], mask[:], ALU.mult))
            link(dve.tensor_copy(gw[:, :, 8:9], w9[:, :, 8:9]))

        @block.scalar
        def _(act):
            for n, tile in enumerate(exps):
                act.wait_ge(asked, n + 1)
                act.activation(tile, tile, ACT.Exp).then_inc(exped, 1)

        @block.tensor
        def _(pe):
            pe.wait_ge(masked, 1)
            m = mask[:].rearrange("p t e -> p (t e)")
            pe.matmul(ps[:, 0:NT * 8], g.tri[:], m, start=True, stop=True)
            pe.matmul(pst[:, 0:NT * 8], g.ones[:], m, start=True, stop=True).then_inc(counted, 1)


def route_top2(nc, g, name, lg, experts, of_probs, w, wsum):
    with ExitStack() as ctx:
        st = Stage(nc, ctx, name)
        t8 = lambda n: st.sb(n, [P, NT, 8])
        v, top, idxf, h0, h1 = t8("v"), t8("top"), t8("idxf"), t8("h0"), t8("h1")
        idx = st.sb("idx", [P, NT, 8], U32)
        s1, s2 = st.sb("s1", [P, NT]), st.sb("s2", [P, NT])
        dved, asked, exped = st.sem("dved"), st.sem("asked"), st.sem("exped")
        block = ctx.enter_context(nc.Block())

        @block.vector
        def _(dve):
            link = chain(dve, dved)
            if of_probs:
                link(dve.memset(v[:], -1.0))
                link(dve.tensor_reduce(s1[:], lg, AX.X, ALU.max))
                dve.tensor_tensor(v[:, :, 0:experts], lg, spread(s1[:], experts), ALU.subtract).then_inc(asked, 1)
                dve.wait_ge(exped, 1)
                link(dve.tensor_reduce(s1[:], v[:, :, 0:experts], AX.X, ALU.add))
                link(dve.reciprocal(s1[:], s1[:]))
                link(dve.tensor_tensor(v[:, :, 0:experts], v[:, :, 0:experts], spread(s1[:], experts), ALU.mult))
            else:
                link(dve.tensor_copy(v[:], lg))
            for t in range(NT):
                link(dve.max(top[:, t, :], v[:, t, :]))
            for t in range(NT):
                link(dve.max_index(idx[:, t, :], top[:, t, :], v[:, t, :]))
            link(dve.tensor_copy(idxf[:], idx[:]))
            iota = g.iota8[:].rearrange("p (o e) -> p o e", o=1).broadcast_to([P, NT, 8])
            link(dve.tensor_tensor(h0[:], idxf[:, :, 0:1].broadcast_to([P, NT, 8]), iota, ALU.is_equal))
            link(dve.tensor_tensor(h1[:], idxf[:, :, 1:2].broadcast_to([P, NT, 8]), iota, ALU.is_equal))
            if not of_probs:
                dve.tensor_tensor(v[:, :, 0:2], top[:, :, 0:2], top[:, :, 0:1].broadcast_to([P, NT, 2]),
                                  ALU.subtract).then_inc(asked, 1)
                dve.wait_ge(exped, 1)
                link(dve.tensor_copy(top[:, :, 0:2], v[:, :, 0:2]))
            link(dve.tensor_tensor(s1[:], top[:, :, 0], top[:, :, 1], ALU.add))
            link(dve.reciprocal(s1[:], s1[:]))
            link(dve.tensor_tensor(s2[:], top[:, :, 1], s1[:], ALU.mult))
            link(dve.tensor_tensor(s1[:], top[:, :, 0], s1[:], ALU.mult))
            link(dve.tensor_tensor(h0[:], h0[:], spread(s1[:], 8), ALU.mult))
            link(dve.tensor_tensor(h1[:], h1[:], spread(s2[:], 8), ALU.mult))
            link(dve.tensor_tensor(w, h0[:, :, 0:experts], h1[:, :, 0:experts], ALU.add))
            if wsum is not None:
                link(dve.tensor_reduce(wsum, w, AX.X, ALU.add))

        @block.scalar
        def _(act):
            act.wait_ge(asked, 1)
            t = v[:, :, 0:experts if of_probs else 2]
            act.activation(t, t, ACT.Exp).then_inc(exped, 1)


def gated_mlp(nc, g, name, packs, up_srcs, down_srcs, pick, experts, gwt):
    with ExitStack() as outer:
        so = Stage(nc, outer, name)
        wg, wu, wd = ([so.sb(f"{n}{part}", [P, packs, D], F32R) for part in ("hi", "lo")] for n in ("wg", "wu", "wd"))
        with ExitStack() as ctx:
            st = Stage(nc, ctx, name + "w")
            raw = [st.sb(f"raw{n}", [P, packs, D]) for n in range(2)] + [st.sb("raw2", [P, packs * P])]
            ps = [st.ps(f"ps{n}", [P, 512]) for n in range(8)]
            loaded, made, high, kept = st.sem("loaded"), st.sem("made"), st.sem("high"), st.sem("kept")
            jobs = [(raw[w][:, k, :], [t[:, k, :] for t in (wg, wu)[w]]) for w in range(2) for k in range(packs)]
            jobs += [(raw[2][:, k * P:(k + 1) * P], [t[:, k, :] for t in wd]) for k in range(packs)]
            n_in = len(up_srcs) + len(down_srcs)
            block = ctx.enter_context(nc.Block())

            @block.sync
            def _(sp):
                for w, k, n, src in up_srcs:
                    sp.dma_start(raw[w][:, k:k + n, :], src.rearrange("(k p) d -> p k d", p=P)).then_inc(loaded, 16)
                for k, n, src in down_srcs:
                    sp.dma_start(raw[2][:, k * P:(k + n) * P].rearrange("d (e i) -> d e i", e=src.shape[0]),
                                 src.rearrange("e d i -> d e i")).then_inc(loaded, 16)
                sp.wait_ge(loaded, 16 * n_in)

            @block.tensor
            def _(pe):
                pe.wait_ge(loaded, 16 * n_in)
                for n, (src, _) in enumerate(jobs):
                    if n >= 8:
                        pe.wait_ge(kept, n - 7)
                    pe.transpose(ps[n % 8][:, 0:P], src, g.ident[:]).then_inc(made, 1)

            @block.scalar
            def _(act):
                for n, (_, dst) in enumerate(jobs):
                    act.wait_ge(made, n + 1)
                    act.activation(dst[0], ps[n % 8][:, 0:P], ACT.Copy).then_inc(high, 1)

            @block.vector
            def _(dve):
                for n, (_, dst) in enumerate(jobs):
                    dve.wait_ge(high, n + 1)
                    dve.tensor_tensor(dst[1], ps[n % 8][:, 0:P], dst[0].bitcast(F32), ALU.subtract).then_inc(kept, 1)

        with ExitStack() as ctx:
            st = Stage(nc, ctx, name + "m")
            ring = 4 if packs % 4 == 0 else 3
            xh, xl = (st.sb(n, [D, T], F32R) for n in ("xh", "xl"))
            sg, up = (st.sb(n, [P, 2, TC]) for n in ("sg", "up"))
            hid = st.sb("hid", [P, ring, TC])
            hh, hl = (st.sb(n, [P, ring, TC], F32R) for n in ("hh", "hl"))
            ps_g, ps_u, ps_w = ([st.ps(f"ps_{n}{k}", [P, 512]) for k in range(2)] for n in "guw")
            ps_y = st.ps("ps_y", [P, 512])
            (x_high, x_low, gated, made, silued, upped, weighted, h_high, h_low, added, kept) = (st.sem(x) for x in (
                "x_high", "x_low", "gated", "made", "silued", "upped", "weighted", "h_high", "h_low", "added", "kept"))
            block = ctx.enter_context(nc.Block())

            def three(pe, out, w, k, x, start, stop):
                for q, (a, z) in enumerate(((0, 0), (0, 1), (1, 0))):
                    m = pe.matmul(out, w[a][:, k, :], x[z], start=(start and q == 0), stop=(stop and q == 2))
                return m

            @block.tensor
            def _(pe):
                def down(c, k, n):
                    pe.wait_ge(h_low, n + 1)
                    if k == 0 and not (isinstance(c, int) and c == 0):
                        pe.wait_ge(kept, c)
                    s = k % packs
                    three(pe, ps_y[:, 0:TC], wd, s, (hh[:, s % ring, :], hl[:, s % ring, :]), s == 0, s == packs - 1
                          ).then_inc(added, 1)

                def chunk(c, first):
                    x = (xh[:, bass.ds(c * TC, TC)], xl[:, bass.ds(c * TC, TC)])
                    pe.wait_ge(x_low, c + 1)
                    for k in range(packs):
                        n = packs * c + k
                        if not first or k >= 2:
                            pe.wait_ge(silued, n - 1)
                        three(pe, ps_g[k % 2][:, 0:TC], wg, k, x, True, True).then_inc(gated, 1)
                        if not first or k >= 2:
                            pe.wait_ge(weighted, n - 1)
                        three(pe, ps_u[k % 2][:, 0:TC], wu, k, x, True, True)
                        pe.matmul(ps_w[k % 2][:, 0:TC], pick[:, k * P:(k + 1) * P], gwt[:, bass.ds(c * TC, TC)],
                                  start=True, stop=True).then_inc(made, 1)
                        if not first or k >= 2:
                            down(c, k - 2, n - 2)
                chunk(0, True)
                with pe.Fori(1, NC) as c:
                    chunk(c, False)
                for k in range(packs - 2, packs):
                    down(NC - 1, k, packs * (NC - 1) + k)

            @block.scalar
            def _(act):
                for c in range(NC):
                    at = slice(c * TC, (c + 1) * TC)
                    act.activation(xh[:, at], g.xnt[:, at], ACT.Copy).then_inc(x_high, 1)

                def high(n, k):
                    act.wait_ge(weighted, n + 1)
                    act.activation(hh[:, k % packs % ring, :], hid[:, k % packs % ring, :], ACT.Copy).then_inc(h_high, 1)

                def out(c):
                    act.wait_ge(added, packs * (c + 1))
                    act.activation(g.addt[:, bass.ds(c * TC, TC)], ps_y[:, 0:TC], ACT.Copy).then_inc(kept, 1)

                def chunk(c, first):
                    for k in range(packs):
                        n = packs * c + k
                        if k == 2 and not first:
                            out(c - 1)
                        act.wait_ge(gated, n + 1)
                        if not first or k >= 2:
                            act.wait_ge(upped, n - 1)
                        act.activation(sg[:, k % 2, :], ps_g[k % 2][:, 0:TC], ACT.Silu).then_inc(silued, 1)
                        if not first or k >= 1:
                            high(n - 1, k - 1)
                chunk(0, True)
                with act.Fori(1, NC) as c:
                    chunk(c, False)
                high(packs * NC - 1, packs - 1)
                out(NC - 1)

            @block.gpsimd
            def _(pool):
                with pool.Fori(0, NC) as c:
                    for k in range(packs):
                        pool.wait_ge(h_high, packs * c + k + 1)
                        pool.tensor_tensor(hl[:, k % ring, :], hid[:, k % ring, :], hh[:, k % ring, :].bitcast(F32),
                                           ALU.subtract).then_inc(h_low, 1)

            @block.vector
            def _(dve):
                for c in range(NC):
                    at = slice(c * TC, (c + 1) * TC)
                    dve.wait_ge(x_high, c + 1)
                    dve.tensor_tensor(xl[:, at], g.xnt[:, at], xh[:, at].bitcast(F32), ALU.subtract).then_inc(x_low, 1)

                def chunk(c, first):
                    for k in range(packs):
                        n = packs * c + k
                        dve.wait_ge(silued, n + 1)
                        dve.wait_ge(made, n + 1)
                        dve.tensor_tensor(up[:, k % 2, :], sg[:, k % 2, :], ps_u[k % 2][:, 0:TC], ALU.mult
                                          ).then_inc(upped, 1)
                        dve.wait_ge(upped, n + 1)
                        if not first or k >= ring:
                            dve.wait_ge(added, n - ring + 1)
                        dve.tensor_tensor(hid[:, k % ring, :], up[:, k % 2, :], ps_w[k % 2][:, 0:TC], ALU.mult
                                          ).then_inc(weighted, 1)
                chunk(0, True)
                with dve.Fori(1, NC) as c:
                    chunk(c, False)


ME, MF = 4, 4


def moe_layer(nc, g, name, w1, w2, b1, b2, lng, lnb, loaded, gwt, pick_r):
    with ExitStack() as ctx:
        st = Stage(nc, ctx, name)
        w1h, w1l = (st.sb(n, [D, ME * MF * P], F32R) for n in ("w1h", "w1l"))
        w2h, w2l = (st.sb(n, [P, ME * MF * D], F32R) for n in ("w2h", "w2l"))
        xe, hid = st.sb("xe", [D, 2, TC]), st.sb("hid", [P, MF, TC])
        xh, xl = (st.sb(n, [D, 2, TC], F32R) for n in ("xh", "xl"))
        hh, hl = (st.sb(n, [P, MF, TC], F32R) for n in ("hh", "hl"))
        y, wb = st.sb("y", [D, TC]), st.sb("wb", [D, 2, TC])
        ps_h, ps_y, ps_w = ([st.ps(f"ps_{n}{k}", [P, 512]) for k in range(2)] for n in "hyw")
        (w_high, w1_low, w2_low, scaled, x_high, x_low, upped, gelued, h_high, h_low, summed, spread_, wkept, yed,
         added) = (st.sem(x) for x in (
             "w_high", "w1_low", "w2_low", "scaled", "x_high", "x_low", "upped", "gelued", "h_high", "h_low",
             "summed", "spread", "wkept", "yed", "added"))
        w1f = w1.rearrange("h e k f -> h (e k f)")
        w2f = w2.rearrange("p e k h -> p (e k h)")
        block = ctx.enter_context(nc.Block())

        @block.tensor
        def _(pe):
            def down(c, e, k):
                n = 16 * c + 4 * e + k
                pe.wait_ge(h_low, n + 1)
                if k == 0 and not (isinstance(c, int) and 4 * c + e < 2):
                    pe.wait_ge(yed, 4 * c + e - 1)
                at = slice((MF * (e % ME) + k) * D, (MF * (e % ME) + k + 1) * D)
                for q, (w, h) in enumerate(((w2h, hh), (w2h, hl), (w2l, hh))):
                    m = pe.matmul(ps_y[e % 2][:, 0:TC], w[:, at], h[:, k, :], start=(k == 0 and q == 0),
                                  stop=(k == MF - 1 and q == 2))
                m.then_inc(summed, 1)

            def chunk(c, first):
                for e in range(ME):
                    m = 4 * c + e
                    if not (first and e < 2):
                        pe.wait_ge(wkept, m - 1)
                    pe.wait_ge(x_low, m + 1)
                    for k in range(MF):
                        n = 16 * c + 4 * e + k
                        if not (first and e == 0 and k < 2):
                            pe.wait_ge(gelued, n - 1)
                        at = slice((MF * e + k) * P, (MF * e + k + 1) * P)
                        for q, (w, x) in enumerate(((w1h, xh), (w1h, xl), (w1l, xh))):
                            t = pe.matmul(ps_h[k % 2][:, 0:TC], w[:, at], x[:, e % 2, :], start=(q == 0), stop=(q == 2))
                        t.then_inc(upped, 1)
                        if k == 0:
                            pe.matmul(ps_w[e % 2][:, 0:TC], pick_r[:, e * P:(e + 1) * P],
                                      gwt[:, bass.ds(c * TC, TC)], start=True, stop=True).then_inc(spread_, 1)
                        if first and e == 0 and k == 0:
                            pe.wait_ge(w2_low, 1)
                        if not (first and 4 * e + k < 3):
                            down(c, (4 * e + k - 3) // 4, (k + 1) % 4)
            pe.wait_ge(w1_low, 1)
            chunk(0, True)
            with pe.Fori(1, NC) as c:
                chunk(c, False)
            for k in range(1, MF):
                down(NC - 1, ME - 1, k)

        @block.gpsimd
        def _(pool):
            with pool.Fori(0, NC) as c:
                for n in range(ME * MF):
                    k = n % MF
                    pool.wait_ge(h_high, 16 * c + n + 1)
                    pool.tensor_tensor(hl[:, k, :], hid[:, k, :], hh[:, k, :].bitcast(F32), ALU.subtract
                                       ).then_inc(h_low, 1)

        @block.scalar
        def _(act):
            act.wait_ge(loaded, 96)
            act.activation(w1h[:], w1f, ACT.Copy).then_inc(w_high, 1)
            act.activation(w2h[:], w2f, ACT.Copy).then_inc(w_high, 1)

            def high(n, k):
                act.wait_ge(gelued, n + 1)
                act.activation(hh[:, k, :], hid[:, k, :], ACT.Copy).then_inc(h_high, 1)

            def chunk(c, first):
                for e in range(ME):
                    for k in range(MF):
                        n = 16 * c + 4 * e + k
                        act.wait_ge(upped, n + 1)
                        if not (first and e == 0):
                            act.wait_ge(summed, n - 3)
                        act.activation(hid[:, k, :], ps_h[k % 2][:, 0:TC], ACT.Gelu, bias=b1[:, e, k:k + 1]
                                       ).then_inc(gelued, 1)
                        if not (first and e == 0 and k == 0):
                            high(n - 1, (k - 1) % MF)
            chunk(0, True)
            with act.Fori(1, NC) as c:
                chunk(c, False)
            high(16 * NC - 1, MF - 1)

        @block.vector
        def _(dve):
            dve.wait_ge(loaded, 96)
            dve.wait_ge(w_high, 1)
            dve.tensor_tensor(w1l[:], w1f, w1h[:].bitcast(F32), ALU.subtract).then_inc(w1_low, 1)

            def scale(c, e, first):
                m = 4 * c + e
                if not (first and e < 2):
                    dve.wait_ge(upped, 4 * (m - 1))
                dve.tensor_scalar(xe[:, e % 2, :], g.xnt[:, bass.ds(c * TC, TC)], lng[:, e:e + 1], lnb[:, e:e + 1],
                                  ALU.mult, ALU.add).then_inc(scaled, 1)
                dve.wait_ge(scaled, m + 1)
                dve.tensor_copy(xh[:, e % 2, :], xe[:, e % 2, :]).then_inc(x_high, 1)
                dve.wait_ge(x_high, m + 1)
                dve.tensor_tensor(xl[:, e % 2, :], xe[:, e % 2, :], xh[:, e % 2, :].bitcast(F32), ALU.subtract
                                  ).then_inc(x_low, 1)

            def add(c, e):
                m = 4 * c + e
                dve.wait_ge(summed, 4 * (m + 1))
                out = g.addt[:, bass.ds(c * TC if e >= 0 else c * TC - TC, TC)]
                x = e % ME
                if x == 0:
                    dve.scalar_tensor_tensor(out, ps_y[0][:, 0:TC], b2[:, 0:1], wb[:, 0, :], ALU.add, ALU.mult
                                             ).then_inc(yed, 1)
                else:
                    done = 3 * (c if e >= 0 else c - 1) + x - 1
                    if not isinstance(done, int) or done > 0:
                        dve.wait_ge(added, done)
                    dve.scalar_tensor_tensor(y[:], ps_y[x % 2][:, 0:TC], b2[:, x:x + 1], wb[:, x % 2, :],
                                             ALU.add, ALU.mult).then_inc(yed, 1)
                    dve.wait_ge(yed, m + 1)
                    dve.tensor_tensor(out, out, y[:], ALU.add).then_inc(added, 1)

            def chunk(c, first, last=False):
                for e in range(ME):
                    m = 4 * c + e
                    if e + 1 < ME:
                        scale(c, e + 1, first)
                    elif not last:
                        scale(c + 1, 0, False)
                    dve.wait_ge(spread_, m + 1)
                    dve.tensor_copy(wb[:, e % 2, :], ps_w[e % 2][:, 0:TC]).then_inc(wkept, 1)
                    dve.wait_ge(wkept, m + 1)
                    if not (first and e == 0):
                        add(c, e - 1)

            scale(0, 0, True)
            dve.wait_ge(w_high, 2)
            dve.tensor_tensor(w2l[:], w2f, w2h[:].bitcast(F32), ALU.subtract).then_inc(w2_low, 1)
            chunk(0, True)
            with dve.Fori(1, NC - 1) as c:
                chunk(c, False)
            chunk(NC - 1, False, True)
            add(NC - 1, ME - 1)


def mx_linear(nc, g, w_d, b_d):
    with ExitStack() as ctx:
        st = Stage(nc, ctx, "mx")
        w, b = st.sb("w", [P, 1, D]), st.sb("b", [D, 1])
        wt, xt = st.sb("wt", [D, P]), st.sb("xt", [D, T])
        loaded, dved, quantised = st.sem("loaded"), st.sem("dved"), st.sem("quantised")
        turned, kept, made, done = st.sem("turned"), st.sem("kept"), st.sem("made"), st.sem("done")
        ps = [st.ps(f"ps{n}", [P, 512]) for n in range(8)]
        t = [st.sb(f"t{n}", [P, NT, D]) for n in range(4)]
        sc, rs = st.sb("sc", [P, NT * 4]), st.sb("rs", [P, NT * 4])
        block = ctx.enter_context(nc.Block())

        @block.sync
        def _(sp):
            sp.dma_start(w[:, 0, :], w_d).then_inc(loaded, 16)
            with nc.allow_non_contiguous_dma(reason="bias as a column"):
                sp.dma_start(b[:], col(b_d)).then_inc(loaded, 16)
            sp.wait_ge(loaded, 32)

        @block.vector
        def _(dve):
            link = chain(dve, dved)

            def quantise(x, n):
                v = x.rearrange("p t (k c) -> p (t k) c", c=32)
                y, a, r, s = (i[:, 0:n, :].rearrange("p t (k c) -> p (t k) c", c=32) for i in t)
                m = 4 * n
                bc = lambda q: q[:, 0:m].rearrange("p (k o) -> p k o", o=1).broadcast_to([P, m, 32])
                link(dve.tensor_reduce(sc[:, 0:m], v, AX.X, ALU.max, apply_absolute_value=True))
                link(dve.tensor_scalar(sc[:, 0:m], sc[:, 0:m], 1.0 / 7.5, 1e-30, ALU.mult, ALU.max))
                link(dve.reciprocal(rs[:, 0:m], sc[:, 0:m]))
                link(dve.tensor_tensor(y, v, bc(rs), ALU.mult))
                link(dve.scalar_tensor_tensor(a, y, -1.0, y, ALU.mult, ALU.max))
                link(dve.tensor_scalar(r, a, 2.0, -4.0, ALU.is_ge, ALU.mult))
                link(dve.tensor_scalar(a, a, 4.0, -2.0, ALU.is_ge, ALU.mult))
                link(dve.scalar_tensor_tensor(r, r, 8.0, a, ALU.add, ALU.add))
                link(dve.reciprocal(a, r))
                link(dve.tensor_tensor(y, y, r, ALU.mult))
                link(dve.tensor_scalar(s, y, ROUND, None, ALU.add))
                link(dve.tensor_scalar(s, s, -ROUND, None, ALU.add))
                link(dve.tensor_tensor(r, s, y, ALU.subtract))
                link(dve.tensor_scalar(r, r, 0.5, None, ALU.is_ge))
                link(dve.tensor_tensor(s, s, r, ALU.subtract))
                link(dve.tensor_tensor(s, s, a, ALU.mult))
                return s, bc(sc), v

            s, scale, v = quantise(g.xn[:], NT)
            dve.tensor_tensor(v, s, scale, ALU.mult).then_inc(quantised, 1)
            dve.wait_ge(quantised, 1)
            dve.wait_ge(loaded, 32)
            s, scale, v = quantise(w[:], 1)
            dve.tensor_tensor(v, s, scale, ALU.mult).then_inc(quantised, 1)
            for n in range(4):
                a, e = 512 * n, min(512 * n + 512, T)
                dve.wait_ge(turned, n + 1)
                dve.tensor_copy(xt[:, a:e], ps[n][:, 0:e - a]).then_inc(kept, 1)
            dve.wait_ge(turned, 5)
            dve.tensor_copy(wt[:], ps[4][:, 0:P]).then_inc(kept, 1)

        @block.tensor
        def _(pe):
            pe.wait_ge(quantised, 1)
            for n in range(4):
                for q in range(4 * n, min(4 * n + 4, NT)):
                    m = pe.transpose(ps[n][:, (q % 4) * P:(q % 4 + 1) * P], g.xn[:, q, :], g.ident[:])
                m.then_inc(turned, 1)
            pe.wait_ge(quantised, 2)
            pe.transpose(ps[4][:, 0:P], w[:, 0, :], g.ident[:]).then_inc(turned, 1)
            pe.wait_ge(kept, 5)
            for c in range(NC):
                pe.matmul(ps[c][:, 0:TC], wt[:], xt[:, c * TC:(c + 1) * TC], start=True, stop=True).then_inc(made, 1)

        @block.scalar
        def _(act):
            act.wait_ge(loaded, 32)
            for c in range(NC):
                act.wait_ge(made, c + 1)
                act.activation(g.addt[:, c * TC:(c + 1) * TC], ps[c][:, 0:TC], ACT.Identity, bias=b[:, 0:1]
                               ).then_inc(done, 1)


class Globals:
    pass


def build(nc, a, out):
    with ExitStack() as ctx:
        st = Stage(nc, ctx, "g")
        g = Globals()
        g.x, g.xn = st.sb("x", [P, NT, D]), st.sb("xn", [P, NT, D])
        g.xnt, g.addt = st.sb("xnt", [D, T + 2 * PAIR]), st.sb("addt", [D, T])
        g.ident, g.ones, g.tri = st.sb("ident", [P, P]), st.sb("ones", [P, P]), st.sb("tri", [P, P])
        g.hm8, g.hm64, g.iota8 = st.sb("hm8", [P, 16]), st.sb("hm64", [P, 2]), st.sb("iota8", [P, 8])
        g.pick_f0, g.pick_f1, g.pick_f2 = st.sb("pick_f0", [9, 768]), st.sb("pick_f1", [4, 512]), st.sb("pick_f2", [8, 2048])
        g.half = st.sb("half", [P, NT])
        g.zeros = st.sb("zeros", [P, 16])
        ctx_t = nc.dram_tensor("ctx_t", [B, CR, S], F32, kind="Internal").ap()

        constants(nc, g)
        with ExitStack() as c2:
            s2 = Stage(nc, c2, "load")
            loaded = s2.sem("loaded")
            with nc.Block() as block:
                @block.sync
                def _(sp):
                    sp.dma_start(g.x[:], a["x"].rearrange("b l d -> (b l) d").rearrange("(t p) d -> p t d", p=P)
                                 ).then_inc(loaded, 16)
                    sp.wait_ge(loaded, 16)
        context_prep(nc, g, a["ctx_768"], a["mask_BxS2_bf1"], ctx_t)
        renorm(nc, g, "n0", g.x)
        ctx_d = a["ctx_768"]

        def attend(name, **kw):
            attention(nc, g, name, ctx_d, ctx_t, **kw)

        def attention_0():
            w = {k: a["L0_xattn_" + k] for k in ("Wq", "bq", "Wkv", "bkv", "Wo", "bo")}
            moves_k, moves_v = [], []
            for h in range(HEADS):
                for part, ls in ((0, moves_k), (1, moves_v)):
                    r0 = 16 * h + 8 * part
                    ls.append((lambda t, h=h: t[8 * h:8 * h + 8, 0, 0:C], w["Wkv"][r0:r0 + 8, :]))
                    ls.append((lambda t, h=h: t[8 * h:8 * h + 8, 0, C:C + 1], col(w["bkv"][r0:r0 + 8])))
            attend("a0", heads=HEADS, kc=1, scale=8.0 ** -0.5,
                   loads=[("wkT", [P, 1, CR], moves_k), ("wvT", [P, 1, CO], moves_v),
                          ("wq", [P, 1, D], [(lambda t: t[:, 0, :], w["Wq"])]),
                          ("wo_raw", [D, P], [(lambda t: t[:], w["Wo"])]), ("wo", [P, 1, D], []),
                          ("bq", [P, 1], [(lambda t: t[:], col(w["bq"]))])],
                   turns=[(lambda t: t["wo_raw"][:], P, D, lambda t: t["wo"][:, 0, :])],
                   masked={"clear": [("wkT", 0.0)], "direct": [("ob", lambda t: t[:], col(w["bo"]))]},
                   q_bias=True, mask_row=False, vo_direct=False)
            renorm(nc, g, "n1", g.x, g.addt)

        def ffn_0():
            with ExitStack() as c2:
                s2 = Stage(nc, c2, "f0")
                lg, gw, gwt = s2.sb("lg", [P, NT, 9]), s2.sb("gw", [P, NT, 9]), s2.sb("gwt", [LOW + 9, T], F32R)
                pick_r = s2.sb("pick_r", [LOW + 9, 768], F32R)
                f = {k: a["L0_ffn_" + k] for k in ("gate_w", "dyn_gate_w", "dyn_up_w", "dyn_down_w", "sh_gate_w",
                                                   "sh_up_w", "sh_down_w")}
                logits(nc, g, "f0l", g.xnt, 9, f["gate_w"], None, False, lg[:])
                route_mixer(nc, g, lg, gw)
                turn_weights(nc, g, "f0t", 9, gw, gwt, g.pick_f0[:], pick_r)
                fl = lambda x: x.rearrange("e i d -> (e i) d")
                gated_mlp(nc, g, "f0m", 6,
                          [(0, 0, 4, fl(f["dyn_gate_w"])), (1, 0, 4, fl(f["dyn_up_w"])),
                           (0, 4, 2, fl(f["sh_gate_w"])), (1, 4, 2, fl(f["sh_up_w"]))],
                          [(0, 4, f["dyn_down_w"]), (4, 2, f["sh_down_w"])], pick_r, 9, gwt)
            renorm(nc, g, "n2", g.x, g.addt)

        def attention_1():

            w = {k: a["L1_xattn_" + k] for k in ("Wq", "Wk", "Wv", "Wo", "bo")}
            turns = []
            for k in range(8):
                s = slice(k * P, (k + 1) * P)
                turns += [(lambda t, s=s: t["wk_raw"][:, s], P, C, lambda t, k=k: t["wkT"][:, k, 0:C]),
                          (lambda t, s=s: t["wv_raw"][:, s], P, C, lambda t, k=k: t["wvT"][:, k, 0:C]),
                          (lambda t, s=s: t["wq_raw"][:, s], P, D, lambda t, k=k: t["wq"][:, k, :])]
            attend("a1", heads=HEADS, kc=8, scale=64.0 ** -0.5,
                   loads=[("wkT", [P, 8, CR], []), ("wvT", [P, 8, CO], []), ("wq", [P, 8, D], []),
                          ("wk_raw", [C, 1024], [(lambda t: t[:], w["Wk"])]),
                          ("wv_raw", [C, 1024], [(lambda t: t[:], w["Wv"])]),
                          ("wq_raw", [D, 1024], [(lambda t: t[:], w["Wq"])]),
                          ("wo", [P, 8, D], [(lambda t: t[:], w["Wo"].rearrange("(k p) e -> p k e", p=P))])],
                   turns=turns,
                   masked={"clear": [("wkT", 0.0), ("wvT", 0.0), ("cb", 0.0)],
                           "direct": [("ob", lambda t: t[:], col(w["bo"]))]},
                   q_bias=False, mask_row=False, vo_direct=False)
            renorm(nc, g, "n3", g.x, g.addt)

        def ffn_1():
            with ExitStack() as c2:
                s2 = Stage(nc, c2, "f1")
                hid, hid_t = s2.sb("hid", [P, NT, D]), s2.sb("hid_t", [D, T])
                lg, gw, gwt, gs = s2.sb("lg", [P, NT, 4]), s2.sb("gw", [P, NT, 4]), s2.sb("gwt", [LOW + 4, T], F32R), s2.sb("gs", [P, NT])
                w1, w2 = s2.sb("w1", [D, 4, ME, MF, P]), s2.sb("w2", [P, 4, ME, MF, D])
                b1, vecs = s2.sb("b1", [P, 4, ME, MF]), s2.sb("vecs", [D, 4, 3, ME])
                rw, rb = s2.sb("rw", [D, 4, ME]), s2.sb("rb", [1, 4, ME])
                pick_r = s2.sb("pick_r", [LOW + 4, 512], F32R)
                copied = s2.sem("copied")
                router_in, layer_in = s2.sem("router_in"), [s2.sem(f"layer{m}_in") for m in range(4)]
                f = {k: a["L1_ffn_" + k] for k in ("router_w", "router_b", "ln_g", "ln_b", "w1", "b1", "w2", "b2")}
                with nc.Block() as block:
                    @block.sync
                    def _(sp):
                        sp.dma_start(rb[:], f["router_b"].rearrange("(o m) e -> o m e", o=1)).then_inc(router_in, 16)
                        with nc.allow_non_contiguous_dma(reason="the router's few columns"):
                            sp.dma_start(rw[:], f["router_w"].rearrange("m d e -> d m e")).then_inc(router_in, 16)
                        for m in range(4):
                            sp.dma_start(w1[:, m, :, :, :].rearrange("h e k f -> h e (k f)"),
                                         f["w1"][m].rearrange("e h f -> h e f")).then_inc(layer_in[m], 16)
                            with nc.allow_non_contiguous_dma(reason="vectors as columns"):
                                sp.dma_start(b1[:, m, :, :], f["b1"][m].rearrange("e (k p) -> p e k", p=P)
                                             ).then_inc(layer_in[m], 16)
                                for n, src in enumerate((f["b2"], f["ln_g"], f["ln_b"])):
                                    sp.dma_start(vecs[:, m, n, :], src[m].rearrange("e h -> h e")
                                                 ).then_inc(layer_in[m], 16)
                            sp.dma_start(w2[:, m, :, :, :].rearrange("p e k h -> p (e k) h"),
                                         f["w2"][m].rearrange("e (k p) h -> p (e k) h", p=P)).then_inc(layer_in[m], 16)

                    @block.vector
                    def _(dve):
                        dve.tensor_copy(hid[:], g.xn[:]).then_inc(copied, 1)
                for m in range(4):
                    if m == 0:
                        renorm(nc, g, f"m{m}n", hid, raw_t=hid_t)
                    else:
                        renorm(nc, g, f"m{m}n", hid, g.addt, scale=gs, raw_t=hid_t)
                    logits_of(nc, g, f"m{m}l", hid_t, ME, rw[:, m, :], rb[:, m, :], router_in, lg[:])
                    route_top2(nc, g, f"m{m}r", lg[:], 4, True, gw[:], gs[:])
                    turn_weights(nc, g, f"m{m}t", 4, gw, gwt, g.pick_f1[:] if m == 0 else None, pick_r if m == 0 else None)
                    moe_layer(nc, g, f"m{m}f", w1[:, m], w2[:, m], b1[:, m], vecs[:, m, 0], vecs[:, m, 1],
                              vecs[:, m, 2], layer_in[m], gwt, pick_r)
                renorm(nc, g, "m4n", hid, g.addt, scale=gs, raw_t=g.addt, norm=False)
            renorm(nc, g, "n4", g.x, g.addt)

        def attention_2():

            w = {k: a["L2_xattn_" + k] for k in ("Wq", "Wk", "Wv", "Wo")}
            attend("a2", heads=HEADS, kc=1, scale=8.0 ** -0.5,
                   loads=[("wkT", [P, 1, CR], []), ("wvT", [P, 1, CO], []), ("wq", [P, 1, D], []),
                          ("wk_raw", [C, P], [(lambda t: t[:], w["Wk"])]),
                          ("wv_raw", [C, P], [(lambda t: t[:], w["Wv"])]),
                          ("wq_raw", [D, P], [(lambda t: t[:], w["Wq"])]),
                          ("wo", [P, 1, D], [(lambda t: t[:, 0, :], w["Wo"])])],
                   turns=[(lambda t: t["wk_raw"][:], P, C, lambda t: t["wkT"][:, 0, 0:C]),
                          (lambda t: t["wv_raw"][:], P, C, lambda t: t["wvT"][:, 0, 0:C]),
                          (lambda t: t["wq_raw"][:], P, D, lambda t: t["wq"][:, 0, :])],
                   masked={"clear": [("wkT", 0.0), ("wvT", 0.0), ("cb", 0.0), ("ob", 0.0)], "direct": []},
                   q_bias=False, mask_row=True, vo_direct=False)
            renorm(nc, g, "n5", g.x, g.addt)

        def ffn_2():
            with ExitStack() as c2:
                s2 = Stage(nc, c2, "f2")
                lg, gw, gwt = s2.sb("lg", [P, NT, 8]), s2.sb("gw", [P, NT, 8]), s2.sb("gwt", [LOW + 8, T], F32R)
                pick_r = s2.sb("pick_r", [LOW + 8, 2048], F32R)
                f = {k: a["L2_ffn_" + k] for k in ("Wg", "W1", "W2", "W3")}
                logits(nc, g, "f2l", g.xnt, 8, f["Wg"], None, False, lg[:])
                route_top2(nc, g, "f2r", lg[:], 8, False, gw[:], None)
                turn_weights(nc, g, "f2t", 8, gw, gwt, g.pick_f2[:], pick_r)
                fl = lambda x: x.rearrange("e i d -> (e i) d")
                gated_mlp(nc, g, "f2m", 16, [(0, 0, 16, fl(f["W1"])), (1, 0, 16, fl(f["W2"]))], [(0, 16, f["W3"])],
                          pick_r, 8, gwt)
            renorm(nc, g, "n6", g.x, g.addt)

        def attention_3():

            w = {k: a["L3_xattn_" + k] for k in ("Wq", "bq", "Wk", "bk", "Wv", "bv")}
            attend("a3", heads=1, kc=1, scale=1.0,
                   loads=[("wkT", [P, 1, CR], [(lambda t: t[:, 0, C:C + 1], col(w["bk"]))]), ("wq", [P, 1, D], []),
                          ("wk_raw", [C, P], [(lambda t: t[:], w["Wk"])]),
                          ("wq_raw", [D, P], [(lambda t: t[:], w["Wq"])]),
                          ("bq", [P, 1], [(lambda t: t[:], col(w["bq"]))])],
                   turns=[(lambda t: t["wk_raw"][:], P, C, lambda t: t["wkT"][:, 0, 0:C]),
                          (lambda t: t["wq_raw"][:], P, D, lambda t: t["wq"][:, 0, :])],
                   masked={"clear": [("wkT", 0.0), ("ob", 0.0)],
                           "direct": [("vo", lambda t: t[0:C, 0, :], w["Wv"]),
                                      ("vo", lambda t: t[C:CO, 0, :], w["bv"].rearrange("(o e) -> o e", o=1))]},
                   q_bias=True, mask_row=False, vo_direct=True)
            renorm(nc, g, "n7", g.x, g.addt)

        def ffn_3():
            mx_linear(nc, g, a["L3_ffn_weight"], a["L3_ffn_bias"])
            renorm(nc, g, "n8", g.x, g.addt, norm=False)

        for sub in (attention_0, ffn_0, attention_1, ffn_1, attention_2, ffn_2, attention_3, ffn_3):
            sub()
        with ExitStack() as c2:
            s2 = Stage(nc, c2, "store")
            stored = s2.sem("stored")
            with nc.Block() as block:
                @block.sync
                def _(sp):
                    sp.dma_start(out.rearrange("b l d -> (b l) d").rearrange("(t p) d -> p t d", p=P), g.x[:]
                                 ).then_inc(stored, 16)
                    sp.wait_ge(stored, 16)


_INS = ["x", "ctx_768", "mask_BxS2_bf1", "L0_xattn_Wq", "L0_xattn_bq", "L0_xattn_Wkv", "L0_xattn_bkv", "L0_xattn_Wo",
        "L0_xattn_bo", "L0_ffn_gate_w", "L0_ffn_dyn_gate_w", "L0_ffn_dyn_up_w", "L0_ffn_dyn_down_w",
        "L0_ffn_sh_gate_w", "L0_ffn_sh_up_w", "L0_ffn_sh_down_w", "L1_xattn_Wq", "L1_xattn_Wk", "L1_xattn_Wv",
        "L1_xattn_Wo", "L1_xattn_bo", "L1_ffn_router_w", "L1_ffn_router_b", "L1_ffn_ln_g", "L1_ffn_ln_b", "L1_ffn_w1",
        "L1_ffn_b1", "L1_ffn_w2", "L1_ffn_b2", "L2_xattn_Wq", "L2_xattn_Wk", "L2_xattn_Wv", "L2_xattn_Wo",
        "L2_ffn_Wg", "L2_ffn_W1", "L2_ffn_W2", "L2_ffn_W3", "L3_xattn_Wq", "L3_xattn_bq", "L3_xattn_Wk",
        "L3_xattn_bk", "L3_xattn_Wv", "L3_xattn_bv", "L3_ffn_weight", "L3_ffn_bias"]


def kernel(**inputs):
    import numpy as _np
    import concourse.bacc as _bacc
    from concourse import mybir as _mybir
    from concourse.bass_utils import run_bass_kernel_spmd as _run

    nc = _bacc.Bacc("TRN2", target_bir_lowering=False, num_devices=1)
    arrays, args = {}, {}
    for name in _INS:
        a = _np.ascontiguousarray(inputs[name])
        if a.dtype.kind == "b":
            a = a.view(_np.uint8)
        arrays[f"in_{name}"] = a
        args[name] = nc.dram_tensor(f"in_{name}", a.shape, _mybir.dt.from_np(a.dtype), kind="ExternalInput").ap()
    out = nc.dram_tensor("out_0", (B, L, D), F32, kind="ExternalOutput").ap()
    build(nc, args, out)
    r = _run(nc, [arrays], core_ids=[0])
    return r.results[0]["out_0"]
```
